# Optimizing a Trainium2 kernel written in Bass

```python
import numpy as np
import jax
import jax.numpy as jnp

def _softmax(x, axis=-1):
    return jax.nn.softmax(x, axis=axis)

def _gelu(x):
    return jax.nn.gelu(x, approximate=True)

def _silu(x):
    return jax.nn.silu(x)

def _sigmoid(x):
    return jax.nn.sigmoid(x)

def _layernorm(x, axis=-1, eps=1e-05):
    m = jnp.mean(x, axis=axis, keepdims=True)
    v = jnp.var(x, axis=axis, keepdims=True)
    return (x - m) / jnp.sqrt(v + eps)

def _scatter_add(tgt, idx, src, axis=0):
    return tgt.at[idx].add(src)

def _segment_sum(src, seg, n):
    return jax.ops.segment_sum(src, seg, n)
kernel_name = 'mk_decoder_preln_d4_seqx_r8_ba68d5'

def setup_inputs(seed: int=0):
    np.random.seed(seed)
    _w = jnp.asarray

    def _rec_inputs():
        import jax
        import jax.numpy as jnp
        _rk = jax.random.key(seed)
        x = -0.0002928 + 1 * jax.random.normal(jax.random.fold_in(_rk, 1), (16, 256, 128), jnp.float32)
        _lenS = 256 - jax.random.randint(jax.random.fold_in(_rk, 7), (16,), 0, max(1, 256 // 4) + 1, jnp.int32)
        _lenS2 = 64 - jax.random.randint(jax.random.fold_in(_rk, 8), (16,), 0, max(1, 64 // 4) + 1, jnp.int32)
        _ctx_1024P = jax.random.normal(jax.random.fold_in(_rk, 11), (16, 16, 128), jnp.float32)
        _ctx_1024c = jax.random.dirichlet(jax.random.fold_in(_rk, 511), 0.3 * jnp.ones((16,), jnp.float32), (16, 64))
        _ctx_1024t = jnp.einsum('bsk,bkd->bsd', _ctx_1024c, _ctx_1024P)
        _ctx_1024t = _ctx_1024t * jax.lax.rsqrt(jnp.mean(jnp.square(_ctx_1024t)) + 1e-12) * 0.953939
        ctx_1024 = -1.39393e-06 + 0.999914 * (_ctx_1024t + 0.3 * jax.random.normal(jax.random.fold_in(_rk, 611), (16, 64, 128), jnp.float32))
        _validS = jnp.arange(256)[None, :] < _lenS[:, None]
        _validS2 = jnp.arange(64)[None, :] < _lenS2[:, None]
        _causal = jnp.tril(jnp.ones((256, 256), dtype=bool))
        mask_BxS2_bf0 = jnp.logical_not(jnp.ones((16, 64), dtype=bool))
        return (x, ctx_1024, mask_BxS2_bf0)
    x, ctx_1024, mask_BxS2_bf0 = _rec_inputs()

    def _L0_attn_setup():
        import jax, jax.numpy as jnp
        import numpy as np
        W_SEG = 256
        R = 4
        OFFSET = 0
        H = 16
        C = 128
        M = W_SEG // R

        def _mha(xi, w_in, b_in, w_out, b_out):
            b, s, m, c = xi.shape
            dh = c // H
            qkv = jnp.einsum('bsmc,ec->bsme', xi, w_in) + b_in
            q, k, v = jnp.split(qkv, 3, axis=-1)
            q = q.reshape(b, s, m, H, dh)
            k = k.reshape(b, s, m, H, dh)
            v = v.reshape(b, s, m, H, dh)
            scores = jnp.einsum('bsqhd,bskhd->bshqk', q, k) / jnp.sqrt(jnp.asarray(dh, xi.dtype))
            causal = jnp.tril(jnp.ones((m, m), dtype=bool))
            scores = jnp.where(causal, scores, jnp.asarray(-1000000000.0, xi.dtype))
            p = jax.nn.softmax(scores, axis=-1)
            o = jnp.einsum('bshqk,bskhd->bsqhd', p, v).reshape(b, s, m, c)
            return jnp.einsum('bsmc,oc->bsmo', o, w_out) + b_out
        key = jax.random.key(seed)
        k1, k2, k3, k4, k5 = jax.random.split(key, 5)
        x = jax.random.normal(k1, (4, 1024, C), dtype=jnp.float32)
        w_in = jax.random.normal(k2, (3 * C, C), dtype=jnp.float32) * C ** (-0.5)
        b_in = jnp.zeros((3 * C,), dtype=jnp.float32)
        w_out = jax.random.normal(k3, (C, C), dtype=jnp.float32) * C ** (-0.5)
        b_out = jnp.zeros((C,), dtype=jnp.float32)
        return {'x': x, 'w_in': w_in, 'b_in': b_in, 'w_out': w_out, 'b_out': b_out}
    _L0_attn_all = _L0_attn_setup()
    _L0_attn_in = {k: v for k, v in _L0_attn_all.items() if k in ('w_in', 'b_in', 'w_out', 'b_out')}
    del _L0_attn_all

    def _L0_xattn_setup():
        import jax, jax.numpy as jnp
        import numpy as np
        B, TQ, TK = (2, 256, 256)
        X_TO_DIM = 128
        X_FROM_DIM = 128
        HIDDEN = 128
        H = 16
        DH = HIDDEN // H
        key = jax.random.key(seed)
        ks = jax.random.split(key, 10)
        s = 0.02
        return {'x_to': jax.random.normal(ks[0], (B, TQ, X_TO_DIM), dtype=jnp.float32), 'x_from': jax.random.normal(ks[1], (B, TK, X_FROM_DIM), dtype=jnp.float32), 'Wq': jax.random.normal(ks[2], (H, X_TO_DIM, DH), dtype=jnp.float32) * s, 'bq': jax.random.normal(ks[3], (H, DH), dtype=jnp.float32) * s, 'Wk': jax.random.normal(ks[4], (H, X_FROM_DIM, DH), dtype=jnp.float32) * s, 'bk': jax.random.normal(ks[5], (H, DH), dtype=jnp.float32) * s, 'Wv': jax.random.normal(ks[6], (H, X_FROM_DIM, DH), dtype=jnp.float32) * s, 'bv': jax.random.normal(ks[7], (H, DH), dtype=jnp.float32) * s, 'Wo': jax.random.normal(ks[8], (HIDDEN, HIDDEN), dtype=jnp.float32) * s, 'bo': jax.random.normal(ks[9], (HIDDEN,), dtype=jnp.float32) * s}
    _L0_xattn_all = _L0_xattn_setup()
    _L0_xattn_in = {k: v for k, v in _L0_xattn_all.items() if k in ('Wq', 'bq', 'Wk', 'bk', 'Wv', 'bv', 'Wo', 'bo')}
    del _L0_xattn_all

    def _L0_ffn_setup():
        import jax, jax.numpy as jnp
        import numpy as np
        B, S, D = (4, 512, 128)
        E, F_EXP = (16, 256)
        F_C = 2.0
        F_SH = 256
        key = jax.random.key(seed)
        ks = jax.random.split(key, 8)
        s = 0.02
        return {'hidden_states': jax.random.normal(ks[0], (B, S, D), jnp.float32), 'gate_w': jax.random.normal(ks[1], (E, D), jnp.float32) * s, 'Wg': jax.random.normal(ks[2], (E, F_EXP, D), jnp.float32) * s, 'Wu': jax.random.normal(ks[3], (E, F_EXP, D), jnp.float32) * s, 'Wd': jax.random.normal(ks[4], (E, D, F_EXP), jnp.float32) * s, 'Ws_g': jax.random.normal(ks[5], (F_SH, D), jnp.float32) * s, 'Ws_u': jax.random.normal(ks[6], (F_SH, D), jnp.float32) * s, 'Ws_d': jax.random.normal(ks[7], (D, F_SH), jnp.float32) * s}
    _L0_ffn_all = _L0_ffn_setup()
    _L0_ffn_in = {k: v for k, v in _L0_ffn_all.items() if k in ('gate_w', 'Wg', 'Wu', 'Wd', 'Ws_g', 'Ws_u', 'Ws_d')}
    del _L0_ffn_all

    def _L1_attn_setup():
        import jax, jax.numpy as jnp
        import numpy as np
        NEG_FILL = jnp.finfo(jnp.float32).min
        key = jax.random.key(seed)
        k0, k1, k2, k3, k4 = jax.random.split(key, 5)
        B, N, E, D = (4, 512, 128, 32)
        STD = 0.05
        inputs = jax.random.normal(k0, (B, N, E), dtype=jnp.float32)
        Wq = STD * jax.random.normal(k1, (E, D), dtype=jnp.float32)
        Wk = STD * jax.random.normal(k2, (E, D), dtype=jnp.float32)
        Wvdown = STD * jax.random.normal(k3, (E, D), dtype=jnp.float32)
        Wvup = STD * jax.random.normal(k4, (D, E), dtype=jnp.float32)
        return {'inputs': inputs, 'Wq': Wq, 'Wk': Wk, 'Wvdown': Wvdown, 'Wvup': Wvup}
    _L1_attn_all = _L1_attn_setup()
    _L1_attn_in = {k: v for k, v in _L1_attn_all.items() if k in ('Wq', 'Wk', 'Wvdown', 'Wvup')}
    del _L1_attn_all

    def _L1_xattn_setup():
        import jax, jax.numpy as jnp
        import numpy as np
        B, SQ, SKV, D, H = (2, 256, 256, 128, 16)
        HD = D // H

        def cross_attention(query, context, mask, Wq, bq, Wkv, bkv, Wout, bout, num_heads):
            b, sq, d = query.shape
            skv = context.shape[1]
            hd = d // num_heads
            scale = hd ** (-0.5)
            q = query @ Wq + bq
            kv = context @ Wkv + bkv
            kv = kv.reshape(b, skv, 2, num_heads, hd).transpose(2, 0, 3, 1, 4)
            k, v = (kv[0], kv[1])
            q = q.reshape(b, sq, num_heads, hd).transpose(0, 2, 1, 3)
            scores = jnp.einsum('bhid,bhjd->bhij', q, k) * scale
            scores = jnp.where(mask[:, None, None, :], -jnp.inf, scores)
            attn = jax.nn.softmax(scores, axis=-1)
            out = jnp.einsum('bhij,bhjd->bhid', attn, v)
            out = out.transpose(0, 2, 1, 3).reshape(b, sq, d)
            return out @ Wout + bout
        key = jax.random.key(seed)
        ks = jax.random.split(key, 6)
        scale = 1.0 / np.sqrt(D)
        return {'query': jax.random.normal(ks[0], (B, SQ, D), dtype=jnp.float32), 'context': jax.random.normal(ks[1], (B, SKV, D), dtype=jnp.float32), 'mask': jnp.zeros((B, SKV), dtype=bool), 'Wq': jax.random.normal(ks[2], (D, D), dtype=jnp.float32) * scale, 'bq': jnp.zeros((D,), dtype=jnp.float32), 'Wkv': jax.random.normal(ks[3], (D, 2 * D), dtype=jnp.float32) * scale, 'bkv': jnp.zeros((2 * D,), dtype=jnp.float32), 'Wout': jax.random.normal(ks[4], (D, D), dtype=jnp.float32) * scale, 'bout': jnp.zeros((D,), dtype=jnp.float32), 'num_heads': H}
    _L1_xattn_all = _L1_xattn_setup()
    _L1_xattn_in = {k: v for k, v in _L1_xattn_all.items() if k in ('Wq', 'bq', 'Wkv', 'bkv', 'Wout', 'bout')}
    del _L1_xattn_all

    def _L1_ffn_setup():
        import jax, jax.numpy as jnp
        import numpy as np

        def fixed_quant(x, width, frac_width):
            scale = jnp.float32(2.0 ** frac_width)
            imax = jnp.float32(2 ** (width - 1) - 1)
            imin = jnp.float32(-2 ** (width - 1))
            return jnp.clip(jnp.round(x * scale), imin, imax) / scale
        IN_F, HID_F, OUT_F = (128, 512, 128)
        B, S = (4, 256)
        ACT_Q = (8, 4)
        W_Q = (8, 6)
        BIAS_Q = (8, 6)

        def quantized_linear(x, w, b):
            xq = fixed_quant(x, *ACT_Q)
            wq = fixed_quant(w, *W_Q)
            bq = fixed_quant(b, *BIAS_Q)
            return jnp.einsum('bsi,oi->bso', xq, wq) + bq

        def quantized_relu(x):
            return jax.nn.relu(fixed_quant(x, *ACT_Q))
        key = jax.random.key(seed)
        k_x, k_w1, k_b1, k_w2, k_b2 = jax.random.split(key, 5)
        x = jax.random.normal(k_x, (B, S, IN_F), dtype=jnp.float32)
        w1 = jax.random.normal(k_w1, (HID_F, IN_F), dtype=jnp.float32) / np.sqrt(IN_F)
        b1 = jax.random.normal(k_b1, (HID_F,), dtype=jnp.float32) / np.sqrt(IN_F)
        w2 = jax.random.normal(k_w2, (OUT_F, HID_F), dtype=jnp.float32) / np.sqrt(HID_F)
        b2 = jax.random.normal(k_b2, (OUT_F,), dtype=jnp.float32) / np.sqrt(HID_F)
        return {'x': x, 'w1': w1, 'b1': b1, 'w2': w2, 'b2': b2}
    _L1_ffn_all = _L1_ffn_setup()
    _L1_ffn_in = {k: v for k, v in _L1_ffn_all.items() if k in ('w1', 'b1', 'w2', 'b2')}
    del _L1_ffn_all

    def _L2_attn_setup():
        import math
        import jax, jax.numpy as jnp
        import numpy as np
        N_HEADS = 16
        D_EMBED = 128
        key = jax.random.key(seed)
        ks = jax.random.split(key, 5)
        b, l, d = (2, 256, D_EMBED)
        return {'x': jax.random.normal(ks[0], (b, l, d), dtype=jnp.float32), 'w_in': jax.random.normal(ks[1], (3 * d, d), dtype=jnp.float32) * 0.02, 'b_in': jax.random.normal(ks[2], (3 * d,), dtype=jnp.float32) * 0.02, 'w_out': jax.random.normal(ks[3], (d, d), dtype=jnp.float32) * 0.02, 'b_out': jax.random.normal(ks[4], (d,), dtype=jnp.float32) * 0.02}
    _L2_attn_all = _L2_attn_setup()
    _L2_attn_in = {k: v for k, v in _L2_attn_all.items() if k in ('w_in', 'b_in', 'w_out', 'b_out')}
    del _L2_attn_all

    def _L2_xattn_setup():
        import jax, jax.numpy as jnp
        import numpy as np
        DIM = 128
        CTX_DIM = 128
        HEADS = 16
        DIM_HEAD = 64
        INNER = HEADS * DIM_HEAD
        FF_INNER = 4 * DIM
        EPS = 1e-05

        def layer_norm(x, g, b):
            mu = jnp.mean(x, axis=-1, keepdims=True)
            var = jnp.var(x, axis=-1, keepdims=True)
            return (x - mu) * jax.lax.rsqrt(var + EPS) * g + b
        key = jax.random.key(seed)
        ks = jax.random.split(key, 9)
        b, n, j = (4, 256, 128)
        inp = {'x': jax.random.normal(ks[0], (b, n, DIM), dtype=jnp.float32), 'context': jax.random.normal(ks[1], (b, j, CTX_DIM), dtype=jnp.float32), 'ln_g': jnp.ones((DIM,), jnp.float32), 'ln_b': jnp.zeros((DIM,), jnp.float32), 'cln_g': jnp.ones((CTX_DIM,), jnp.float32), 'cln_b': jnp.zeros((CTX_DIM,), jnp.float32), 'Wq': jax.random.normal(ks[2], (DIM, INNER), dtype=jnp.float32) * DIM ** (-0.5), 'Wkv': jax.random.normal(ks[3], (CTX_DIM, 2 * DIM_HEAD), dtype=jnp.float32) * CTX_DIM ** (-0.5), 'Wo': jax.random.normal(ks[4], (INNER, DIM), dtype=jnp.float32) * INNER ** (-0.5), 'Wff1': jax.random.normal(ks[5], (DIM, 2 * FF_INNER), dtype=jnp.float32) * DIM ** (-0.5), 'Wff2': jax.random.normal(ks[6], (FF_INNER, DIM), dtype=jnp.float32) * FF_INNER ** (-0.5)}
        return inp
    _L2_xattn_all = _L2_xattn_setup()
    _L2_xattn_in = {k: v for k, v in _L2_xattn_all.items() if k in ('ln_g', 'ln_b', 'cln_g', 'cln_b', 'Wq', 'Wkv', 'Wo', 'Wff1', 'Wff2')}
    del _L2_xattn_all

    def _L2_ffn_setup():
        import jax, jax.numpy as jnp
        import numpy as np
        from jax import lax
        D = 128
        H = 512
        E = 8
        TOPK = 2
        key = jax.random.key(seed)
        ks = jax.random.split(key, 7)
        s = 0.02
        return {'x': jax.random.normal(ks[0], (2, 256, D), dtype=jnp.float32), 'W1': jax.random.normal(ks[1], (E, D, H), dtype=jnp.float32) * s, 'b1': jnp.zeros((E, H), dtype=jnp.float32), 'W2': jax.random.normal(ks[2], (E, H, D), dtype=jnp.float32) * s, 'b2': jnp.zeros((E, D), dtype=jnp.float32), 'Wr': jax.random.normal(ks[3], (D, E), dtype=jnp.float32) * s, 'br': jnp.zeros((E,), dtype=jnp.float32)}
    _L2_ffn_all = _L2_ffn_setup()
    _L2_ffn_in = {k: v for k, v in _L2_ffn_all.items() if k in ('W1', 'b1', 'W2', 'b2', 'Wr', 'br')}
    del _L2_ffn_all

    def _L3_attn_setup():
        import jax, jax.numpy as jnp
        import numpy as np
        D_MODEL = 128
        NUM_HEADS = 16
        HEAD_DIM = D_MODEL // NUM_HEADS
        EPS = 1e-08
        key = jax.random.key(seed)
        ks = jax.random.split(key, 6)
        B, T = (4, 256)
        s = 0.02
        return {'x': jax.random.normal(ks[0], (B, T, D_MODEL), dtype=jnp.float32), 'Wq': jax.random.normal(ks[1], (D_MODEL, D_MODEL), dtype=jnp.float32) * s, 'Wk': jax.random.normal(ks[2], (D_MODEL, D_MODEL), dtype=jnp.float32) * s, 'Wv': jax.random.normal(ks[3], (D_MODEL, D_MODEL), dtype=jnp.float32) * s, 'Wo': jax.random.normal(ks[4], (D_MODEL, D_MODEL), dtype=jnp.float32) * s, 'bo': jnp.zeros((D_MODEL,), dtype=jnp.float32)}
    _L3_attn_all = _L3_attn_setup()
    _L3_attn_in = {k: v for k, v in _L3_attn_all.items() if k in ('Wq', 'Wk', 'Wv', 'Wo', 'bo')}
    del _L3_attn_all

    def _L3_xattn_setup():
        import jax, jax.numpy as jnp
        import numpy as np
        DIM = 128
        HEADS = 16
        HEAD_DIM = DIM // HEADS
        B, N, M = (2, 256, 256)

        def _split_heads(x):
            b, s, c = x.shape
            return x.reshape(b, s, HEADS, HEAD_DIM).transpose(0, 2, 1, 3)
        key0 = jax.random.key(seed)
        ks = jax.random.split(key0, 12)
        s = 0.02
        return {'query': jax.random.normal(ks[0], (B, N, DIM), jnp.float32), 'key': jax.random.normal(ks[1], (B, M, DIM), jnp.float32), 'value': jax.random.normal(ks[2], (B, M, DIM), jnp.float32), 'Wq': jax.random.normal(ks[3], (DIM, DIM), jnp.float32) * s, 'bq': jnp.zeros((DIM,), jnp.float32), 'Wk': jax.random.normal(ks[4], (DIM, DIM), jnp.float32) * s, 'bk': jnp.zeros((DIM,), jnp.float32), 'Wv': jax.random.normal(ks[5], (DIM, DIM), jnp.float32) * s, 'bv': jnp.zeros((DIM,), jnp.float32), 'Wp': jax.random.normal(ks[6], (DIM, DIM), jnp.float32) * s, 'bp': jnp.zeros((DIM,), jnp.float32), 'scale': jnp.full((1,), HEAD_DIM ** (-0.5), jnp.float32)}
    _L3_xattn_all = _L3_xattn_setup()
    _L3_xattn_in = {k: v for k, v in _L3_xattn_all.items() if k in ('Wq', 'bq', 'Wk', 'bk', 'Wv', 'bv', 'Wp', 'bp', 'scale')}
    del _L3_xattn_all

    def _L3_ffn_setup():
        import jax, jax.numpy as jnp
        import numpy as np
        B, C, D, O = (4, 512, 128, 128)
        PROJ = 32
        RANKS = [1, 2, 4, 8]
        E = len(RANKS)
        CLAMP_MAX = float(np.log(1.0 / 0.01))

        def _l2norm(v, axis):
            return v / jnp.maximum(jnp.linalg.norm(v, axis=axis, keepdims=True), 1e-12)
        key = jax.random.key(seed)
        ks = jax.random.split(key, 16)
        inp = {'x': jax.random.normal(ks[0], (B, C, D), dtype=jnp.float32), 'W': jax.random.normal(ks[1], (O, D), dtype=jnp.float32) / np.sqrt(D), 'Wp': jax.random.normal(ks[2], (PROJ, D), dtype=jnp.float32) / np.sqrt(D), 'bp': jnp.zeros((PROJ,), dtype=jnp.float32), 'sim': jax.random.normal(ks[3], (PROJ, E), dtype=jnp.float32) * 0.01, 'temp': jnp.full((1,), np.log(1.0 / 0.5), dtype=jnp.float32)}
        for i, r in enumerate(RANKS):
            inp[f'Wd{i}'] = jax.random.normal(ks[4 + 2 * i], (r, D), dtype=jnp.float32) / r
            inp[f'Wu{i}'] = jax.random.normal(ks[5 + 2 * i], (O, r), dtype=jnp.float32) * 0.01
        return inp
    _L3_ffn_all = _L3_ffn_setup()
    _L3_ffn_in = {k: v for k, v in _L3_ffn_all.items() if k in ('W', 'Wp', 'bp', 'sim', 'temp', 'Wd0', 'Wu0', 'Wd1', 'Wu1', 'Wd2', 'Wu2', 'Wd3', 'Wu3')}
    del _L3_ffn_all
    return {'x': x, 'ctx_1024': ctx_1024, 'mask_BxS2_bf0': mask_BxS2_bf0, 'L0_attn_w_in': _L0_attn_in['w_in'], 'L0_attn_b_in': _L0_attn_in['b_in'], 'L0_attn_w_out': _L0_attn_in['w_out'], 'L0_attn_b_out': _L0_attn_in['b_out'], 'L0_xattn_Wq': _L0_xattn_in['Wq'], 'L0_xattn_bq': _L0_xattn_in['bq'], 'L0_xattn_Wk': _L0_xattn_in['Wk'], 'L0_xattn_bk': _L0_xattn_in['bk'], 'L0_xattn_Wv': _L0_xattn_in['Wv'], 'L0_xattn_bv': _L0_xattn_in['bv'], 'L0_xattn_Wo': _L0_xattn_in['Wo'], 'L0_xattn_bo': _L0_xattn_in['bo'], 'L0_ffn_gate_w': _L0_ffn_in['gate_w'], 'L0_ffn_Wg': _L0_ffn_in['Wg'], 'L0_ffn_Wu': _L0_ffn_in['Wu'], 'L0_ffn_Wd': _L0_ffn_in['Wd'], 'L0_ffn_Ws_g': _L0_ffn_in['Ws_g'], 'L0_ffn_Ws_u': _L0_ffn_in['Ws_u'], 'L0_ffn_Ws_d': _L0_ffn_in['Ws_d'], 'L1_attn_Wq': _L1_attn_in['Wq'], 'L1_attn_Wk': _L1_attn_in['Wk'], 'L1_attn_Wvdown': _L1_attn_in['Wvdown'], 'L1_attn_Wvup': _L1_attn_in['Wvup'], 'L1_xattn_Wq': _L1_xattn_in['Wq'], 'L1_xattn_bq': _L1_xattn_in['bq'], 'L1_xattn_Wkv': _L1_xattn_in['Wkv'], 'L1_xattn_bkv': _L1_xattn_in['bkv'], 'L1_xattn_Wout': _L1_xattn_in['Wout'], 'L1_xattn_bout': _L1_xattn_in['bout'], 'L1_ffn_w1': _L1_ffn_in['w1'], 'L1_ffn_b1': _L1_ffn_in['b1'], 'L1_ffn_w2': _L1_ffn_in['w2'], 'L1_ffn_b2': _L1_ffn_in['b2'], 'L2_attn_w_in': _L2_attn_in['w_in'], 'L2_attn_b_in': _L2_attn_in['b_in'], 'L2_attn_w_out': _L2_attn_in['w_out'], 'L2_attn_b_out': _L2_attn_in['b_out'], 'L2_xattn_ln_g': _L2_xattn_in['ln_g'], 'L2_xattn_ln_b': _L2_xattn_in['ln_b'], 'L2_xattn_cln_g': _L2_xattn_in['cln_g'], 'L2_xattn_cln_b': _L2_xattn_in['cln_b'], 'L2_xattn_Wq': _L2_xattn_in['Wq'], 'L2_xattn_Wkv': _L2_xattn_in['Wkv'], 'L2_xattn_Wo': _L2_xattn_in['Wo'], 'L2_xattn_Wff1': _L2_xattn_in['Wff1'], 'L2_xattn_Wff2': _L2_xattn_in['Wff2'], 'L2_ffn_W1': _L2_ffn_in['W1'], 'L2_ffn_b1': _L2_ffn_in['b1'], 'L2_ffn_W2': _L2_ffn_in['W2'], 'L2_ffn_b2': _L2_ffn_in['b2'], 'L2_ffn_Wr': _L2_ffn_in['Wr'], 'L2_ffn_br': _L2_ffn_in['br'], 'L3_attn_Wq': _L3_attn_in['Wq'], 'L3_attn_Wk': _L3_attn_in['Wk'], 'L3_attn_Wv': _L3_attn_in['Wv'], 'L3_attn_Wo': _L3_attn_in['Wo'], 'L3_attn_bo': _L3_attn_in['bo'], 'L3_xattn_Wq': _L3_xattn_in['Wq'], 'L3_xattn_bq': _L3_xattn_in['bq'], 'L3_xattn_Wk': _L3_xattn_in['Wk'], 'L3_xattn_bk': _L3_xattn_in['bk'], 'L3_xattn_Wv': _L3_xattn_in['Wv'], 'L3_xattn_bv': _L3_xattn_in['bv'], 'L3_xattn_Wp': _L3_xattn_in['Wp'], 'L3_xattn_bp': _L3_xattn_in['bp'], 'L3_xattn_scale': _L3_xattn_in['scale'], 'L3_ffn_W': _L3_ffn_in['W'], 'L3_ffn_Wp': _L3_ffn_in['Wp'], 'L3_ffn_bp': _L3_ffn_in['bp'], 'L3_ffn_sim': _L3_ffn_in['sim'], 'L3_ffn_temp': _L3_ffn_in['temp'], 'L3_ffn_Wd0': _L3_ffn_in['Wd0'], 'L3_ffn_Wu0': _L3_ffn_in['Wu0'], 'L3_ffn_Wd1': _L3_ffn_in['Wd1'], 'L3_ffn_Wu1': _L3_ffn_in['Wu1'], 'L3_ffn_Wd2': _L3_ffn_in['Wd2'], 'L3_ffn_Wu2': _L3_ffn_in['Wu2'], 'L3_ffn_Wd3': _L3_ffn_in['Wd3'], 'L3_ffn_Wu3': _L3_ffn_in['Wu3']}

def reference(x, ctx_1024, mask_BxS2_bf0, L0_attn_w_in, L0_attn_b_in, L0_attn_w_out, L0_attn_b_out, L0_xattn_Wq, L0_xattn_bq, L0_xattn_Wk, L0_xattn_bk, L0_xattn_Wv, L0_xattn_bv, L0_xattn_Wo, L0_xattn_bo, L0_ffn_gate_w, L0_ffn_Wg, L0_ffn_Wu, L0_ffn_Wd, L0_ffn_Ws_g, L0_ffn_Ws_u, L0_ffn_Ws_d, L1_attn_Wq, L1_attn_Wk, L1_attn_Wvdown, L1_attn_Wvup, L1_xattn_Wq, L1_xattn_bq, L1_xattn_Wkv, L1_xattn_bkv, L1_xattn_Wout, L1_xattn_bout, L1_ffn_w1, L1_ffn_b1, L1_ffn_w2, L1_ffn_b2, L2_attn_w_in, L2_attn_b_in, L2_attn_w_out, L2_attn_b_out, L2_xattn_ln_g, L2_xattn_ln_b, L2_xattn_cln_g, L2_xattn_cln_b, L2_xattn_Wq, L2_xattn_Wkv, L2_xattn_Wo, L2_xattn_Wff1, L2_xattn_Wff2, L2_ffn_W1, L2_ffn_b1, L2_ffn_W2, L2_ffn_b2, L2_ffn_Wr, L2_ffn_br, L3_attn_Wq, L3_attn_Wk, L3_attn_Wv, L3_attn_Wo, L3_attn_bo, L3_xattn_Wq, L3_xattn_bq, L3_xattn_Wk, L3_xattn_bk, L3_xattn_Wv, L3_xattn_bv, L3_xattn_Wp, L3_xattn_bp, L3_xattn_scale, L3_ffn_W, L3_ffn_Wp, L3_ffn_bp, L3_ffn_sim, L3_ffn_temp, L3_ffn_Wd0, L3_ffn_Wu0, L3_ffn_Wd1, L3_ffn_Wu1, L3_ffn_Wd2, L3_ffn_Wu2, L3_ffn_Wd3, L3_ffn_Wu3):
    import jax
    import jax.numpy as jnp

    def _L0_attn_ref(x, w_in, b_in, w_out, b_out):
        import jax, jax.numpy as jnp
        import numpy as np
        W_SEG = 256
        R = 4
        OFFSET = 0
        H = 16
        C = 128
        M = W_SEG // R

        def _mha(xi, w_in, b_in, w_out, b_out):
            b, s, m, c = xi.shape
            dh = c // H
            qkv = jnp.einsum('bsmc,ec->bsme', xi, w_in) + b_in
            q, k, v = jnp.split(qkv, 3, axis=-1)
            q = q.reshape(b, s, m, H, dh)
            k = k.reshape(b, s, m, H, dh)
            v = v.reshape(b, s, m, H, dh)
            scores = jnp.einsum('bsqhd,bskhd->bshqk', q, k) / jnp.sqrt(jnp.asarray(dh, xi.dtype))
            causal = jnp.tril(jnp.ones((m, m), dtype=bool))
            scores = jnp.where(causal, scores, jnp.asarray(-1000000000.0, xi.dtype))
            p = jax.nn.softmax(scores, axis=-1)
            o = jnp.einsum('bshqk,bskhd->bsqhd', p, v).reshape(b, s, m, c)
            return jnp.einsum('bsmc,oc->bsmo', o, w_out) + b_out
        b, n, c = x.shape
        s = n // W_SEG
        xr = x.reshape(b, s, W_SEG, c)
        xi = xr[:, :, OFFSET::R, :]
        oi = _mha(xi, w_in, b_in, w_out, b_out)
        out = jnp.zeros_like(xr).at[:, :, OFFSET::R, :].set(oi)
        return out.reshape(b, n, c)

    def _L0_xattn_ref(x_to, x_from, Wq, bq, Wk, bk, Wv, bv, Wo, bo):
        import jax, jax.numpy as jnp
        import numpy as np
        B, TQ, TK = (2, 256, 256)
        X_TO_DIM = 128
        X_FROM_DIM = 128
        HIDDEN = 128
        H = 16
        DH = HIDDEN // H
        q = jnp.einsum('btf,hfd->bhtd', x_to, Wq) + bq[None, :, None, :]
        k = jnp.einsum('bsf,hfd->bhsd', x_from, Wk) + bk[None, :, None, :]
        v = jnp.einsum('bsf,hfd->bhsd', x_from, Wv) + bv[None, :, None, :]
        scores = jnp.einsum('bhtd,bhsd->bhts', q, k) / jnp.sqrt(jnp.float32(DH))
        attn = jax.nn.softmax(scores, axis=-1)
        out = jnp.einsum('bhts,bhsd->bhtd', attn, v)
        concat = jnp.transpose(out, (0, 2, 1, 3)).reshape(out.shape[0], out.shape[2], H * DH)
        return concat @ Wo.T + bo

    def _L0_ffn_ref(hidden_states, gate_w, Wg, Wu, Wd, Ws_g, Ws_u, Ws_d):
        import jax, jax.numpy as jnp
        import numpy as np
        B, S, D = (4, 512, 128)
        E, F_EXP = (16, 256)
        F_C = 2.0
        F_SH = 256
        b, s, d = hidden_states.shape
        e = gate_w.shape[0]
        cap = int(s * F_C / e)
        logits = jnp.einsum('bsd,ed->bse', hidden_states, gate_w)
        scores = jax.nn.softmax(logits, axis=-1).transpose(0, 2, 1)
        topk_w, topk_idx = jax.lax.top_k(scores, cap)
        x_tok = jnp.take_along_axis(hidden_states[:, None, :, :], topk_idx[..., None], axis=2)
        g = jnp.einsum('becd,efd->becf', x_tok, Wg)
        u = jnp.einsum('becd,efd->becf', x_tok, Wu)
        h = jax.nn.gelu(g, approximate=False) * u
        eo = jnp.einsum('becf,edf->becd', h, Wd) * topk_w[..., None]
        offs = (jnp.arange(b) * s)[:, None, None]
        flat_idx = (topk_idx + offs).reshape(-1)
        flat = jnp.zeros((b * s, d), hidden_states.dtype)
        flat = flat.at[flat_idx].add(eo.reshape(-1, d))
        out = flat.reshape(b, s, d)
        gs = jnp.einsum('bsd,fd->bsf', hidden_states, Ws_g)
        us = jnp.einsum('bsd,fd->bsf', hidden_states, Ws_u)
        shared = jnp.einsum('bsf,df->bsd', jax.nn.gelu(gs, approximate=False) * us, Ws_d)
        return out + shared

    def _L1_attn_ref(inputs, Wq, Wk, Wvdown, Wvup):
        import jax, jax.numpy as jnp
        import numpy as np
        NEG_FILL = jnp.finfo(jnp.float32).min
        B, N, E = inputs.shape
        D = Wq.shape[1]
        Q = inputs @ Wq
        K = inputs @ Wk
        score = jnp.einsum('bqd,bkd->bqk', Q, K)
        score = score / jnp.sqrt(jnp.float32(D))
        causal = jnp.tril(jnp.ones((N, N), dtype=bool))
        score = jnp.where(causal, score, 0.0)
        score = jnp.where(score != 0, score, NEG_FILL)
        attn = jax.nn.softmax(score, axis=-1)
        V = inputs @ (Wvdown @ Wvup)
        return attn @ V

    def _L1_xattn_ref(query, context, mask, Wq, bq, Wkv, bkv, Wout, bout, num_heads):
        import jax, jax.numpy as jnp
        import numpy as np
        B, SQ, SKV, D, H = (2, 256, 256, 128, 16)
        HD = D // H

        def cross_attention(query, context, mask, Wq, bq, Wkv, bkv, Wout, bout, num_heads):
            b, sq, d = query.shape
            skv = context.shape[1]
            hd = d // num_heads
            scale = hd ** (-0.5)
            q = query @ Wq + bq
            kv = context @ Wkv + bkv
            kv = kv.reshape(b, skv, 2, num_heads, hd).transpose(2, 0, 3, 1, 4)
            k, v = (kv[0], kv[1])
            q = q.reshape(b, sq, num_heads, hd).transpose(0, 2, 1, 3)
            scores = jnp.einsum('bhid,bhjd->bhij', q, k) * scale
            scores = jnp.where(mask[:, None, None, :], -jnp.inf, scores)
            attn = jax.nn.softmax(scores, axis=-1)
            out = jnp.einsum('bhij,bhjd->bhid', attn, v)
            out = out.transpose(0, 2, 1, 3).reshape(b, sq, d)
            return out @ Wout + bout
        return cross_attention(query, context, mask, Wq, bq, Wkv, bkv, Wout, bout, num_heads)

    def _L1_ffn_ref(x, w1, b1, w2, b2):
        import jax, jax.numpy as jnp
        import numpy as np

        def fixed_quant(x, width, frac_width):
            scale = jnp.float32(2.0 ** frac_width)
            imax = jnp.float32(2 ** (width - 1) - 1)
            imin = jnp.float32(-2 ** (width - 1))
            return jnp.clip(jnp.round(x * scale), imin, imax) / scale
        IN_F, HID_F, OUT_F = (128, 512, 128)
        B, S = (4, 256)
        ACT_Q = (8, 4)
        W_Q = (8, 6)
        BIAS_Q = (8, 6)

        def quantized_linear(x, w, b):
            xq = fixed_quant(x, *ACT_Q)
            wq = fixed_quant(w, *W_Q)
            bq = fixed_quant(b, *BIAS_Q)
            return jnp.einsum('bsi,oi->bso', xq, wq) + bq

        def quantized_relu(x):
            return jax.nn.relu(fixed_quant(x, *ACT_Q))
        h = quantized_linear(x, w1, b1)
        h = quantized_relu(h)
        out = quantized_linear(h, w2, b2)
        return out

    def _L2_attn_ref(x, w_in, b_in, w_out, b_out):
        import math
        import jax, jax.numpy as jnp
        import numpy as np
        N_HEADS = 16
        D_EMBED = 128
        b, l, d = x.shape
        h = N_HEADS
        scale = 1.0 / math.sqrt(d // h)
        x_proj = (x @ w_in.T + b_in).reshape(b, l, h, -1)
        q, k, v = jnp.split(x_proj, 3, axis=-1)
        att = jnp.einsum('blhd,bmhd->blmh', q, k) * scale
        att = jax.nn.softmax(att, axis=2)
        opt = jnp.einsum('blmh,blhd->blhd', att, v).reshape(b, l, d)
        return opt @ w_out.T + b_out

    def _L2_xattn_ref(x, context, ln_g, ln_b, cln_g, cln_b, Wq, Wkv, Wo, Wff1, Wff2):
        import jax, jax.numpy as jnp
        import numpy as np
        DIM = 128
        CTX_DIM = 128
        HEADS = 16
        DIM_HEAD = 64
        INNER = HEADS * DIM_HEAD
        FF_INNER = 4 * DIM
        EPS = 1e-05

        def layer_norm(x, g, b):
            mu = jnp.mean(x, axis=-1, keepdims=True)
            var = jnp.var(x, axis=-1, keepdims=True)
            return (x - mu) * jax.lax.rsqrt(var + EPS) * g + b
        scale = DIM_HEAD ** (-0.5)
        xn = layer_norm(x, ln_g, ln_b)
        cn = layer_norm(context, cln_g, cln_b)
        b, n, _ = xn.shape
        q = (xn @ Wq).reshape(b, n, HEADS, DIM_HEAD).transpose(0, 2, 1, 3) * scale
        kv = cn @ Wkv
        k, v = (kv[..., :DIM_HEAD], kv[..., DIM_HEAD:])
        sim = jnp.einsum('bhid,bjd->bhij', q, k)
        attn = jax.nn.softmax(sim, axis=-1)
        out = jnp.einsum('bhij,bjd->bhid', attn, v)
        out = out.transpose(0, 2, 1, 3).reshape(b, n, INNER) @ Wo
        ff = xn @ Wff1
        h, gate = (ff[..., :FF_INNER], ff[..., FF_INNER:])
        out = out + jax.nn.silu(gate) * h @ Wff2
        return out

    def _L2_ffn_ref(x, W1, b1, W2, b2, Wr, br):
        import jax, jax.numpy as jnp
        import numpy as np
        from jax import lax
        D = 128
        H = 512
        E = 8
        TOPK = 2
        B, S, _ = x.shape
        xf = x.reshape(-1, D)
        logits = xf @ Wr + br
        topv, _ = lax.top_k(logits, TOPK)
        thresh = topv[:, TOPK - 1:TOPK]
        masked = jnp.where(logits >= thresh, logits, -jnp.inf)
        weights = jax.nn.softmax(masked, axis=-1)
        h = jax.nn.gelu(jnp.einsum('td,edh->eth', xf, W1) + b1[:, None, :], approximate=False)
        expert_out = jnp.einsum('eth,ehd->etd', h, W2) + b2[:, None, :]
        out = jnp.einsum('etd,te->td', expert_out, weights)
        return out.reshape(B, S, D)

    def _L3_attn_ref(x, Wq, Wk, Wv, Wo, bo):
        import jax, jax.numpy as jnp
        import numpy as np
        D_MODEL = 128
        NUM_HEADS = 16
        HEAD_DIM = D_MODEL // NUM_HEADS
        EPS = 1e-08
        B, T, _ = x.shape
        H, D = (NUM_HEADS, HEAD_DIM)
        scale = jnp.sqrt(jnp.asarray(D, dtype=x.dtype))
        q = (x @ Wq.T).reshape(B, T, H, D).transpose(0, 2, 1, 3)
        k = (x @ Wk.T).reshape(B, T, H, D).transpose(0, 2, 1, 3)
        v = (x @ Wv.T).reshape(B, T, H, D).transpose(0, 2, 1, 3)
        s = jnp.einsum('bhtd,bhsd->bhts', q, k) / scale
        m = jnp.max(s, axis=-1, keepdims=True)
        e = jnp.exp(s - m)
        num = jnp.einsum('bhts,bhsd->bhtd', e, v)
        den = jnp.sum(e, axis=-1, keepdims=True) + EPS
        out = (num / den).transpose(0, 2, 1, 3).reshape(B, T, H * D)
        return out @ Wo.T + bo

    def _L3_xattn_ref(query, key, value, Wq, bq, Wk, bk, Wv, bv, Wp, bp, scale):
        import jax, jax.numpy as jnp
        import numpy as np
        DIM = 128
        HEADS = 16
        HEAD_DIM = DIM // HEADS
        B, N, M = (2, 256, 256)

        def _split_heads(x):
            b, s, c = x.shape
            return x.reshape(b, s, HEADS, HEAD_DIM).transpose(0, 2, 1, 3)
        q = _split_heads(query @ Wq.T + bq)
        k = _split_heads(key @ Wk.T + bk)
        v = _split_heads(value @ Wv.T + bv)
        attn = jnp.einsum('bhnd,bhmd->bhnm', q, k) * scale[0]
        attn = jax.nn.softmax(attn, axis=-1)
        x = jnp.einsum('bhnm,bhmd->bhnd', attn, v)
        x = x.transpose(0, 2, 1, 3).reshape(query.shape)
        return x @ Wp.T + bp

    def _L3_ffn_ref(x, W, Wp, bp, sim, temp, Wd0, Wu0, Wd1, Wu1, Wd2, Wu2, Wd3, Wu3):
        import jax, jax.numpy as jnp
        import numpy as np
        B, C, D, O = (4, 512, 128, 128)
        PROJ = 32
        RANKS = [1, 2, 4, 8]
        E = len(RANKS)
        CLAMP_MAX = float(np.log(1.0 / 0.01))

        def _l2norm(v, axis):
            return v / jnp.maximum(jnp.linalg.norm(v, axis=axis, keepdims=True), 1e-12)
        base = jnp.einsum('bcd,od->bco', x, W)
        xf = x.reshape(-1, x.shape[-1])
        proj = _l2norm(xf @ Wp.T + bp, axis=1)
        simn = _l2norm(sim, axis=0)
        scale = jnp.exp(jnp.minimum(temp, CLAMP_MAX))
        logits = proj @ simn * scale
        lw = jax.nn.softmax(logits, axis=1)
        top1 = jnp.argmax(lw, axis=1)
        ret = jnp.where(jnp.arange(E)[None, :] == top1[:, None], lw, 0.0)
        ret = ret.reshape(x.shape[0], x.shape[1], E)
        downs = (Wd0, Wd1, Wd2, Wd3)
        ups = (Wu0, Wu1, Wu2, Wu3)
        l = jnp.stack([jnp.einsum('bcr,or->bco', jnp.einsum('bcd,rd->bcr', x, d), u) for d, u in zip(downs, ups)], axis=2)
        res = jnp.sum(ret[..., None] * l, axis=2)
        return base + res
    x = x + _L0_attn_ref(_layernorm(x, axis=-1), L0_attn_w_in, L0_attn_b_in, L0_attn_w_out, L0_attn_b_out)
    x = x + _L0_xattn_ref(_layernorm(x, axis=-1), ctx_1024, L0_xattn_Wq, L0_xattn_bq, L0_xattn_Wk, L0_xattn_bk, L0_xattn_Wv, L0_xattn_bv, L0_xattn_Wo, L0_xattn_bo)
    x = x + _L0_ffn_ref(_layernorm(x, axis=-1), L0_ffn_gate_w, L0_ffn_Wg, L0_ffn_Wu, L0_ffn_Wd, L0_ffn_Ws_g, L0_ffn_Ws_u, L0_ffn_Ws_d)
    x = x + _L1_attn_ref(_layernorm(x, axis=-1), L1_attn_Wq, L1_attn_Wk, L1_attn_Wvdown, L1_attn_Wvup)
    x = x + _L1_xattn_ref(_layernorm(x, axis=-1), ctx_1024, mask_BxS2_bf0, L1_xattn_Wq, L1_xattn_bq, L1_xattn_Wkv, L1_xattn_bkv, L1_xattn_Wout, L1_xattn_bout, 16)
    x = x + _L1_ffn_ref(_layernorm(x, axis=-1), L1_ffn_w1, L1_ffn_b1, L1_ffn_w2, L1_ffn_b2)
    x = x + _L2_attn_ref(_layernorm(x, axis=-1), L2_attn_w_in, L2_attn_b_in, L2_attn_w_out, L2_attn_b_out)
    x = x + _L2_xattn_ref(_layernorm(x, axis=-1), ctx_1024, L2_xattn_ln_g, L2_xattn_ln_b, L2_xattn_cln_g, L2_xattn_cln_b, L2_xattn_Wq, L2_xattn_Wkv, L2_xattn_Wo, L2_xattn_Wff1, L2_xattn_Wff2)
    x = x + _L2_ffn_ref(_layernorm(x, axis=-1), L2_ffn_W1, L2_ffn_b1, L2_ffn_W2, L2_ffn_b2, L2_ffn_Wr, L2_ffn_br)
    x = x + _L3_attn_ref(_layernorm(x, axis=-1), L3_attn_Wq, L3_attn_Wk, L3_attn_Wv, L3_attn_Wo, L3_attn_bo)
    x = x + _L3_xattn_ref(_layernorm(x, axis=-1), ctx_1024, ctx_1024, L3_xattn_Wq, L3_xattn_bq, L3_xattn_Wk, L3_xattn_bk, L3_xattn_Wv, L3_xattn_bv, L3_xattn_Wp, L3_xattn_bp, L3_xattn_scale)
    x = x + _L3_ffn_ref(_layernorm(x, axis=-1), L3_ffn_W, L3_ffn_Wp, L3_ffn_bp, L3_ffn_sim, L3_ffn_temp, L3_ffn_Wd0, L3_ffn_Wu0, L3_ffn_Wd1, L3_ffn_Wu1, L3_ffn_Wd2, L3_ffn_Wu2, L3_ffn_Wd3, L3_ffn_Wu3)
    return x

_drawn_inputs = setup_inputs


def setup_inputs(seed=0):
    import zlib

    import numpy as np

    out = dict(_drawn_inputs(seed))
    spreads = {'L0_attn_b_in': (0.0, 0.1),
     'L0_attn_b_out': (0.0, 0.1),
     'L1_xattn_bq': (0.0, 0.276),
     'L1_xattn_bkv': (0.0, 0.1),
     'L1_xattn_bout': (0.0, 0.1),
     'L2_xattn_ln_g': (1.0, 0.2),
     'L2_xattn_ln_b': (0.0, 0.1),
     'L2_xattn_cln_g': (1.0, 0.2),
     'L2_xattn_cln_b': (0.0, 0.1),
     'L2_ffn_b1': (0.0, 0.8),
     'L2_ffn_b2': (0.0, 0.1),
     'L2_ffn_br': (0.0, 0.1),
     'L3_attn_bo': (0.0, 0.1),
     'L3_xattn_bq': (0.0, 0.8),
     'L3_xattn_bk': (0.0, 0.8),
     'L3_xattn_bv': (0.0, 0.642),
     'L3_xattn_bp': (0.0, 0.1),
     'L3_ffn_bp': (0.0, 0.8)}
    factors = {'L0_xattn_Wq': 8.0,
     'L0_xattn_bq': 8.0,
     'L0_xattn_Wk': 8.0,
     'L0_xattn_bk': 8.0,
     'L0_xattn_bv': 4.747,
     'L0_ffn_gate_w': 7.472,
     'L0_ffn_Wg': 7.369,
     'L0_ffn_Wu': 7.084,
     'L0_ffn_Wd': 7.4,
     'L0_ffn_Ws_g': 3.799,
     'L0_ffn_Ws_u': 3.777,
     'L0_ffn_Ws_d': 3.753,
     'L1_attn_Wq': 3.941,
     'L1_attn_Wk': 3.9,
     'L2_attn_b_in': 8.0,
     'L2_attn_b_out': 3.588,
     'L3_attn_Wq': 8.0,
     'L3_attn_Wk': 8.0,
     'L3_attn_Wv': 3.335,
     'L3_attn_Wo': 3.17,
     'L3_xattn_Wq': 8.0,
     'L3_xattn_Wk': 8.0,
     'L3_xattn_Wv': 3.506,
     'L3_xattn_Wp': 2.959,
     'L3_ffn_Wp': 4.117,
     'L3_ffn_sim': 3.976,
     'L3_ffn_Wd0': 4.479,
     'L3_ffn_Wu0': 4.087,
     'L3_ffn_Wd1': 7.026,
     'L3_ffn_Wu1': 6.436,
     'L3_ffn_Wd2': 8.0,
     'L3_ffn_Wu2': 8.0,
     'L3_ffn_Wd3': 8.0,
     'L3_ffn_Wu3': 8.0}
    for name, (base, spread) in spreads.items():
        noise = np.random.default_rng([zlib.crc32(name.encode()), seed]).standard_normal(out[name].shape)
        drawn = base * np.exp(spread * noise) if base else spread * noise
        out[name] = jnp.asarray(drawn.astype(out[name].dtype))
    for name, factor in factors.items():
        out[name] = (out[name] * factor).astype(out[name].dtype)
    return out
```

```python
from contextlib import ExitStack

import concourse.bass as bass
from concourse import mybir

F32 = mybir.dt.float32
F16 = mybir.dt.float16
BF16 = mybir.dt.bfloat16
U8 = mybir.dt.uint8
ACT = mybir.ActivationFunctionType
ALU = mybir.AluOpType
X = mybir.AxisListType.X

P = 128
BATCH, SEQ, D = 16, 256, 128
KEYS = 64
STREAMS = 2
ROUNDS = BATCH // STREAMS
TILES = SEQ // P
BANK = 512
HEADS, HD = 16, 8
QUADS, SLOTS = 4, 4
EXPERTS, CAP, EXP_F = 16, 32, 256
MOE, MOE_H, MOE_C = 8, 512, 4
BIG = -1e30
LOWEST = -3.4028234663852886e38
ROUND = 12582912.0
EPS = 1e-5
HOTTEST = 4.605170185988092
GUARD = 64.0
OFFSET = 10

MHA = {
    "L0a": dict(nq=64, nk=64, ctx=False),
    "L0x": dict(nq=SEQ, nk=KEYS, ctx=True),
    "L1x": dict(nq=SEQ, nk=KEYS, ctx=True),
    "L2a": dict(nq=SEQ, nk=SEQ, ctx=False),
    "L3a": dict(nq=SEQ, nk=SEQ, ctx=False),
    "L3x": dict(nq=SEQ, nk=KEYS, ctx=True),
}
MHA_ORDER = list(MHA)
BIASED = ("L0a", "L0x", "L1x", "L2a", "L3x")
LAYERS = ["L0a", "L0x", "L0f", "L1a", "L1x", "L1f", "L2a", "L2x", "L2f", "L3a", "L3x", "L3f"]

GROUPS = {
    "base": [("ident", 128), ("lo_q", 1), ("lo_k", 1), ("slot", 1), ("part", 3), ("mask_qk", 64), ("mask_kq", 64),
             ("count", 32), ("spread", 512)],
    **{k: [("wq", 128), ("wk", 128), ("wv", 128), ("wo", 128), ("scale", 1)] for k in MHA},
    "L0f": [("gate", EXPERTS), ("wg", EXPERTS * EXP_F), ("wu", EXPERTS * EXP_F), ("wd", EXPERTS * 256),
            ("sg", EXP_F), ("su", EXP_F), ("sd", 256)],
    "L1a": [("wq", 32), ("wk", 32)],
    "L2x": [("wq", 1024), ("wk", 128), ("wv", 64), ("wo", 1024), ("w1", 1024), ("w2", 512),
            ("lg", 1), ("lb", 1), ("cg", 1), ("cb", 1)],
    "L2f": [("w1", MOE * MOE_H), ("w2", MOE * MOE_H), ("b1", MOE * MOE_C), ("wr", MOE)],
    "L3f": [("w", 128), ("wp", 32), ("bp", 1), ("sim", 4), ("temp", 1), ("down", 15), ("up", 128)],
}
RAW = {
    **{(k, "rows"): 256 for k in MHA},
    ("L2f", "rows"): 512,
    ("L1f", "w1"): 512, ("L1f", "w2"): 512, ("L1f", "b1"): 4, ("L1f", "b2"): 128,
    ("L1a", "vdown"): 128, ("L1a", "vup"): 128,
}
RAW_HALF = 2048
LOAD_ORDER = ["base", "L3x", "L3f", "L2a", "L0a", "L0x", "L0f", "L1a", "L1x", "L2x", "L2f", "L3a"]


def weight_columns():
    at, where, spans = 0, {}, {}
    for group in LOAD_ORDER:
        start = at
        for name, n in GROUPS[group]:
            where[group, name] = (at, n)
            at += n
        spans[group] = (start, at)
    return where, spans, at


def raw_columns():
    where, at = {}, 0
    for key, n in RAW.items():
        if at < RAW_HALF < at + n:
            at = RAW_HALF
        where[key] = (at, n)
        at += n
    assert at <= 2 * RAW_HALF
    return where


class Track:

    def __init__(self, sem):
        self.sem, self.value, self.reached = sem, {}, 0

    def plan(self, layer, names):
        for name in names:
            key = (layer,) + (name if isinstance(name, tuple) else (name,))
            assert key not in self.value, key
            self.value[key] = len(self.value) + 1

    def at(self, *key):
        return self.value[key]

    def hit(self, *key):
        self.reached += 1
        assert self.value[key] == self.reached, (key, self.value[key], self.reached)
        return 1


class Stream:
    pass


NORM = dict(vector=["var", "xn"], gpsimd=["rstd"], tensor=["xT"], scalar=["xnT"])


def norm_vector(nc, dve, link, S, L):
    for t in range(TILES):
        ins = nc.vector.bn_stats(S.stats[:, t], S.x[:, t])
    link(ins)
    for t in range(TILES):
        ins = nc.vector.bn_aggr(S.mv[:, t], S.stats[:, t])
    link(ins)
    nc.vector.tensor_scalar(S.var[:], S.mv[:, 0:TILES, 1], EPS, None, ALU.add).then_inc(S.V.sem, S.V.hit(L, "var"))
    dve.wait_ge(S.G.sem, S.G.at(L, "rstd"))
    for t in range(TILES):
        ins = nc.vector.tensor_scalar(S.xn[:, t], S.x[:, t], S.mv[:, t, 0:1], S.rstd[:, t:t + 1],
                                      ALU.subtract, ALU.mult)
    ins.then_inc(S.V.sem, S.V.hit(L, "xn"))


def norm_gpsimd(nc, pool, K, S, L):
    pool.wait_ge(S.V.sem, S.V.at(L, "var"))
    nc.gpsimd.tensor_tensor(S.rstd[:], S.var[:], K.neg_half[:], ALU.pow).then_inc(S.G.sem, S.G.hit(L, "rstd"))


def norm_tensor(nc, pe, K, S, L):
    pe.wait_ge(S.V.sem, S.V.at(L, "xn"))
    for t in range(TILES):
        ins = nc.tensor.transpose(S.bank(2)[:, t * P:(t + 1) * P], S.xn[:, t], K.ident)
    ins.then_inc(S.T.sem, S.T.hit(L, "xT"))


def norm_scalar(nc, act, S, L):
    act.wait_ge(S.T.sem, S.T.at(L, "xT"))
    nc.scalar.activation(S.xnT[:], S.bank(2)[:, 0:SEQ], ACT.Copy).then_inc(S.A.sem, S.A.hit(L, "xnT"))


def first_units(c):
    tiles = max(1, c["nq"] // P)
    blocks = [(t, g) for t in range(tiles) for g in range(QUADS)]
    per = min(BANK // c["nk"], len(blocks))
    return [(j, blocks[a:a + per]) for a in range(0, len(blocks), per) for j in range(SLOTS)]


def second_units(c):
    if c["nk"] == 64:
        return [(j, list(range(QUADS)), 0) for j in range(SLOTS)]
    per = min(BANK // c["nq"], QUADS)
    return [(j, list(range(a, a + per)), k) for a in range(0, QUADS, per) for j in range(SLOTS)
            for k in range(max(1, c["nk"] // P))]


def mha_plan(L):
    c = MHA[L]
    u1, u2 = len(first_units(c)), len(second_units(c))
    sets = u2 // max(1, c["nk"] // P)
    causal = L == "L0a"
    masked1 = [("sum", u) if part == 0 else ("max", u) for u in range(u1) for part in ((0, 1) if causal else (1,))]
    return dict(
        vector=["qop", "kop", "vaug"] + masked1 + ["negm", "qmax"] + [("masked", u) for u in range(u2) if causal]
        + ["on", "x"],
        scalar=["qh", "kh"] + [("e", u) for u in range(u2)] + ["oTc"],
        tensor=["q", "k", "v"] + [("s1", u) for u in range(u1)] + ["mT"]
        + second_order(c, lambda u: ("s2", u), lambda n: ("pv", n)) + ["oT", "y"],
        gpsimd=["wide"])


def second_order(c, score, value):
    units, tiles = len(second_units(c)), max(1, c["nk"] // P)
    out = []
    for n in range(units // tiles):
        out += [score(n * tiles + k) for k in range(tiles)]
        if n:
            out.append(value(n - 1))
    return out + [value(units // tiles - 1)]


def project(nc, pe, K, S, L, before):
    c = MHA[L]
    T, V, A, W = S.T, S.V, S.A, K.w
    nq, nk, ps = c["nq"], c["nk"], S.ps
    kt, mk = max(1, nk // P), min(nk, P)
    src = S.ctxT if c["ctx"] else S.xnT
    wq, wk, rows = S.wide[:, 0:512], S.wide[:, 512:1024], K.rows[L]
    K.loaded(pe, L)
    if L != MHA_ORDER[0]:
        pe.wait_ge(S.G.sem, S.G.at(MHA_ORDER[MHA_ORDER.index(L) - 1], "wide"))
    pe.wait_ge(A.sem, A.at(before, "xnT"))
    for name, w, part, act_in, n in (("q", wq, 0, S.xnT, nq), ("k", wk, 32, src, nk)):
        biased = L in BIASED or name == "k"
        for g in range(QUADS):
            out = ps[:, (0 if name == "q" else 2) * BANK + g * n:][:, 0:n]
            ins = nc.tensor.matmul(out, w[:, g * P:(g + 1) * P], act_in[:, 0:n], start=True, stop=not biased)
            if biased:
                ins = nc.tensor.matmul(out, rows[part:part + 3, g * P:(g + 1) * P], K.ones_bf[part:part + 3, 0:n],
                                       start=False, stop=True)
        ins.then_inc(T.sem, T.hit(L, name))
    pe.wait_ge(V.sem, V.at(L, "kop" if L == "L2a" else "qop"))
    if nk == 64:
        for half in range(2):
            out = ps[64 * half:64 * half + 64, 0:64].rearrange("p (i c) -> p i c", i=2)
            cols = lambda a: a.rearrange("p (i b c) -> p b i c", i=2, b=2)[:, half]
            ins = nc.tensor.matmul(out, src[:, 0:64], cols(W(L, "wv")), start=True, stop=L not in BIASED)
            if L in BIASED:
                ins = nc.tensor.matmul(out, K.ones_bf[64:67, 0:64], cols(rows[64:67, 0:P]), start=False, stop=True)
    for k in range(kt) if nk > 64 else ():
        out = (S.misc if L == "L2a" else ps)[0:mk, k * P:(k + 1) * P]
        ins = nc.tensor.matmul(out, src[:, k * P:k * P + mk], W(L, "wv"), start=True, stop=L not in BIASED)
        if L in BIASED:
            ins = nc.tensor.matmul(out, K.ones_bf[64:67, 0:mk], rows[64:67, 0:P], start=False, stop=True)
    ins.then_inc(T.sem, T.hit(L, "v"))


def output(nc, pe, K, S, L):
    c = MHA[L]
    T, V, A = S.T, S.V, S.A
    qt, mq, rows = max(1, c["nq"] // P), min(c["nq"], P), K.rows[L]
    pe.wait_ge(V.sem, V.at(L, "on"))
    for t in range(qt):
        ins = nc.tensor.transpose(S.bank(0)[:, t * P:t * P + mq], S.on[0:mq, t], K.ident[0:mq, 0:mq])
    ins.then_inc(T.sem, T.hit(L, "oT"))
    pe.wait_ge(A.sem, A.at(L, "oTc"))
    for t in range(qt):
        out = S.bank(1)[0:mq, t * P:(t + 1) * P]
        nc.tensor.matmul(out, S.oT[:, t * P:t * P + mq], K.w(L, "wo"), start=True, stop=False)
        ins = nc.tensor.matmul(out, K.ones_bf[64:67, 0:mq], rows[64:67, P:2 * P], start=False, stop=True)
    ins.then_inc(T.sem, T.hit(L, "y"))


def high_parts(nc, act, S, L):
    c = MHA[L]
    T, V, A = S.T, S.V, S.A
    nq, nk = c["nq"], c["nk"]
    act.wait_ge(T.sem, T.at(L, "q"))
    nc.scalar.activation(S.hi[:, 0:4 * nq], S.ps[:, 0:4 * nq], ACT.Copy).then_inc(A.sem, A.hit(L, "qh"))
    act.wait_ge(T.sem, T.at(L, "k"))
    act.wait_ge(V.sem, V.at(L, "qop"))
    nc.scalar.activation(S.hi[:, 0:4 * nk], S.ps[:, 2 * BANK:2 * BANK + 4 * nk], ACT.Copy)\
        .then_inc(A.sem, A.hit(L, "kh"))


def operands(nc, dve, K, S, L):
    c = MHA[L]
    nq, nk = c["nq"], c["nk"]
    V, A = S.V, S.A
    dve.wait_ge(A.sem, A.at(L, "qh"))
    nc.vector.scalar_tensor_tensor(S.qop[:, 0:4 * nq], S.hi[:, 0:4 * nq], K.w("base", "lo_q"),
                                   S.ps[:, 0:4 * nq], ALU.mult, ALU.add).then_inc(V.sem, V.hit(L, "qop"))
    dve.wait_ge(A.sem, A.at(L, "kh"))
    nc.vector.scalar_tensor_tensor(S.kop[:, 0:4 * nk], S.hi[:, 0:4 * nk], K.w("base", "lo_k"),
                                   S.ps[:, 2 * BANK:2 * BANK + 4 * nk], ALU.mult, ALU.add)\
        .then_inc(V.sem, V.hit(L, "kop"))


def output_turned(nc, act, S, L):
    nq = MHA[L]["nq"]
    act.wait_ge(S.T.sem, S.T.at(L, "oT"))
    nc.scalar.activation(S.oT[:, 0:nq], S.bank(0)[:, 0:nq], ACT.Copy).then_inc(S.A.sem, S.A.hit(L, "oTc"))


def mha_tensor(nc, pe, K, S, L, before):
    c = MHA[L]
    T, V, A, W = S.T, S.V, S.A, K.w
    nq, nk, ps = c["nq"], c["nk"], S.ps
    qt, kt, mq, mk = max(1, nq // P), max(1, nk // P), min(nq, P), min(nk, P)
    src = S.ctxT if c["ctx"] else S.xnT
    project(nc, pe, K, S, L, before)
    yield
    for u, (j, blocks) in enumerate(first_units(c)):
        bank, r = S.bank(u % 3), slice(32 * j, 32 * j + 32)
        if u < 3:
            pe.wait_ge(V.sem, V.at(L, "vaug"))
        else:
            pe.wait_ge(V.sem, V.at(L, "max", u - 3))
        for n, (t, g) in enumerate(blocks):
            out = bank[0:mq, n * nk:(n + 1) * nk]
            ins = nc.tensor.matmul(out, S.qop[r, g * nq + t * P:][:, 0:mq], S.kop[r, g * nk:(g + 1) * nk],
                                   start=True, stop=L != "L1x")
            if L == "L1x":
                ins = nc.tensor.matmul(out, K.ones_bf[r.start:r.start + 1, 0:mq], S.mask_row[r.start:r.start + 1, :],
                                       start=False, stop=True)
        ins.then_inc(T.sem, T.hit(L, "s1", u))
        if u % 2 == 1:
            yield
    pe.wait_ge(V.sem, V.at(L, "negm"))
    for t in range(qt):
        for g in range(QUADS):
            ins = nc.tensor.transpose(S.misc_h[:, g * nq + t * P:][:, 0:mq], S.nm[0:mq, t, g], K.ident_h[0:mq, 0:mq])
    ins.then_inc(T.sem, T.hit(L, "mT"))
    yield
    units = second_units(c)

    def score(u):
        j, groups, k = units[u]
        bank, r = S.bank(u % 3), slice(32 * j, 32 * j + 32)
        if u < 3:
            pe.wait_ge(V.sem, V.at(L, "qmax"))
        elif L == "L0a":
            pe.wait_ge(V.sem, V.at(L, "masked", u - 3))
        else:
            pe.wait_ge(A.sem, A.at(L, "e", u - 3))
        for n, g in enumerate(groups):
            if nk == 64:
                out = bank[64 * (g % 2):64 * (g % 2) + 64, g // 2 * nq:(g // 2 + 1) * nq]
            else:
                out = bank[:, n * nq:(n + 1) * nq]
            ins = nc.tensor.matmul(out, S.kop[r, g * nk + k * P:][:, 0:mk], S.qop[r, g * nq:(g + 1) * nq],
                                   start=True, stop=True)
        ins.then_inc(T.sem, T.hit(L, "s2", u))

    def value(n):
        j, groups, _ = units[n * kt]
        pe.wait_ge(A.sem, A.at(L, "e", n * kt + kt - 1))
        for i in range(2) if nk == 64 else ():
            for t in range(qt):
                out = S.misc[0:mq, t * 144 + (8 * i + j) * 9:][:, 0:72].rearrange("p (b d) -> p b d", b=2)[:, :, 0:9]
                ins = nc.tensor.matmul(out, S.e[:, n % 4, i * nq + t * P:][:, 0:mq],
                                       S.vstack[:, 4 * i + j].rearrange("p (b d) -> p b d", b=2), start=True, stop=True)
        for i, g in enumerate(groups) if nk > 64 else ():
            for t in range(qt):
                h = 4 * g + j
                out = S.misc[0:mq, t * 144 + h * 9:t * 144 + h * 9 + 9]
                for k in range(kt):
                    e = S.e[0:mk, (n * kt + k) % 4, i * nq + t * P:][:, 0:mq]
                    ins = nc.tensor.matmul(out, e, S.vaug[0:mk, k, h, :], start=k == 0, stop=k == kt - 1)
        ins.then_inc(T.sem, T.hit(L, "pv", n))

    for n in range(len(units) // kt):
        for k in range(kt):
            score(n * kt + k)
        if n:
            value(n - 1)
        yield
    value(len(units) // kt - 1)
    output(nc, pe, K, S, L)
    yield


def mha_scalar(nc, act, K, S, L, before):
    c = MHA[L]
    T, V, A = S.T, S.V, S.A
    nq, nk = c["nq"], c["nk"]
    kt = max(1, nk // P)
    scale = 1.0 if L == "L3x" else HD ** -0.5
    high_parts(nc, act, S, L)
    yield
    for u in range(1, len(first_units(c)), 2):
        yield
    yield
    units = second_units(c)
    for u, (j, groups, k) in enumerate(units):
        cols = 2 * nq
        if L == "L0a":
            act.wait_ge(V.sem, V.at(L, "masked", u))
            scores = S.masked[:, u % 2, 0:cols]
        else:
            act.wait_ge(T.sem, T.at(L, "s2", u))
            scores = S.bank(u % 3)[:, 0:cols]
        if u >= 4:
            act.wait_ge(T.sem, T.at(L, "pv", (u - 4) // kt))
        bias = S.mask_col[:, 0:1] if L == "L1x" else 0.0
        nc.scalar.activation(S.e[:, u % 4, 0:cols], scores, ACT.Exp, bias=bias, scale=scale)\
            .then_inc(A.sem, A.hit(L, "e", u))
        if k == kt - 1:
            yield
    output_turned(nc, act, S, L)
    yield


def mha_vector(nc, dve, link, K, S, L, before):
    c = MHA[L]
    T, V, A = S.T, S.V, S.A
    nq, nk = c["nq"], c["nk"]
    qt, kt, mq, mk = max(1, nq // P), max(1, nk // P), min(nq, P), min(nk, P)
    operands(nc, dve, K, S, L)
    dve.wait_ge(T.sem, T.at(L, "v"))
    if nk == 64:
        for half in range(2):
            r = slice(64 * half, 64 * half + 64)
            ins = nc.vector.tensor_copy(S.vstack[r, :, 9 * half:9 * half + HD],
                                        S.ps[r, 0:64].rearrange("p (n d) -> p n d", d=HD))
    else:
        ins = nc.vector.tensor_copy(S.vaug[:, 0:kt, :, 0:HD],
                                    S.ps[:, 0:kt * P].rearrange("p (k h d) -> p k h d", k=kt, d=HD))
    ins.then_inc(V.sem, V.hit(L, "vaug"))
    yield
    for u, (j, blocks) in enumerate(first_units(c)):
        dve.wait_ge(T.sem, T.at(L, "s1", u))
        n = len(blocks)
        scores = S.bank(u % 3)[0:mq, 0:n * nk].rearrange("p (n k) -> p n k", k=nk)
        if L == "L0a":
            if u >= 2:
                dve.wait_ge(V.sem, V.at(L, "max", u - 2))
            mask = K.w("base", "mask_qk")[0:mq].unsqueeze(1).to_broadcast([mq, n, nk])
            summed = S.masked[0:mq, u % 2, 0:n * nk].rearrange("p (n k) -> p n k", k=nk)
            nc.vector.tensor_tensor(summed, scores, mask, ALU.add).then_inc(V.sem, V.hit(L, "sum", u))
            dve.wait_ge(V.sem, V.at(L, "sum", u))
            scores = summed
        t0, g0 = blocks[0]
        if n <= QUADS:
            out = S.negm[0:mq, t0, g0:g0 + n, j]
        else:
            out = S.negm[0:mq, :, :, j]
            scores = scores.rearrange("p (t g) k -> p t g k", g=QUADS)
        nc.vector.tensor_reduce(out, scores, X, ALU.max, negate=True).then_inc(V.sem, V.hit(L, "max", u))
        if u % 2 == 1:
            yield
    dve.wait_ge(V.sem, V.at(L, "max", u))
    negm = S.negm[0:mq, 0:qt].rearrange("p t g j -> p (t g j)")
    high, rest = (S.nm[0:mq, 0:qt].rearrange("p t g (j s) -> p (t g j) s", s=32)[:, :, n] for n in (24, 25))
    link(nc.vector.tensor_scalar(high, negm, 1.0 / GUARD, None, ALU.mult))
    nc.vector.scalar_tensor_tensor(rest, negm, 1.0 / GUARD, high, ALU.mult, ALU.subtract)\
        .then_inc(V.sem, V.hit(L, "negm"))
    dve.wait_ge(T.sem, T.at(L, "mT"))
    nc.vector.tensor_tensor(S.qop[:, 0:4 * nq], S.misc_h[:, 0:4 * nq], S.qop[:, 0:4 * nq], ALU.add)\
        .then_inc(V.sem, V.hit(L, "qmax"))
    yield
    for u, (j, groups, k) in enumerate(second_units(c)):
        if L == "L0a":
            dve.wait_ge(T.sem, T.at(L, "s2", u))
            if u >= 2:
                dve.wait_ge(A.sem, A.at(L, "e", u - 2))
            mask = K.w("base", "mask_kq").unsqueeze(1).to_broadcast([P, 2, nq])
            nc.vector.tensor_tensor(S.masked[:, u % 2, 0:2 * nq].rearrange("p (n q) -> p n q", q=nq),
                                    S.bank(u % 3)[:, 0:2 * nq].rearrange("p (n q) -> p n q", q=nq), mask, ALU.add)\
                .then_inc(V.sem, V.hit(L, "masked", u))
        if k == kt - 1:
            yield
    dve.wait_ge(T.sem, T.at(L, "pv", len(second_units(c)) // kt - 1))
    o = S.misc[0:mq, 0:qt * 144].rearrange("p (t h d) -> p t h d", t=qt, d=9)
    den = o[:, :, :, HD]
    if L == "L3a":
        link(nc.vector.tensor_scalar(S.rden[0:mq, 0:qt], den, 1e-8, None, ALU.add))
        den = S.rden[0:mq, 0:qt]
    link(nc.vector.reciprocal(S.rden[0:mq, 0:qt], den))
    nc.vector.tensor_tensor(S.on[0:mq, 0:qt].rearrange("p t (h d) -> p t h d", d=HD), o[:, :, :, 0:HD],
                            S.rden[0:mq, 0:qt].unsqueeze(3).to_broadcast([mq, qt, HEADS, HD]), ALU.mult)\
        .then_inc(V.sem, V.hit(L, "on"))
    dve.wait_ge(T.sem, T.at(L, "y"))
    nc.vector.tensor_tensor(S.x[0:mq, 0:qt], S.bank(1)[0:mq, 0:qt * P].rearrange("p (t d) -> p t d", d=P),
                            S.x[0:mq, 0:qt], ALU.add).then_inc(V.sem, V.hit(L, "x"))
    yield


def l2a_plan():
    n = len(first_units(MHA["L2a"]))
    return dict(vector=["qop", "kop"] + [("max", u) for u in range(n)] + ["on", "x"],
                scalar=["qh", "kh"] + [("e", u) for u in range(n)] + ["oTc"],
                tensor=["q", "k", "v"] + [("s1", u) for u in range(n)] + ["oT", "y"], gpsimd=["wide"])


def l2a_tensor(nc, pe, K, S, L, before):
    T, V, A = S.T, S.V, S.A
    project(nc, pe, K, S, L, before)
    yield
    for u, (j, blocks) in enumerate(first_units(MHA[L])):
        r = slice(32 * j, 32 * j + 32)
        if u < 3:
            pe.wait_ge(V.sem, V.at(L, "kop"))
        else:
            pe.wait_ge(A.sem, A.at(L, "e", u - 3))
        for n, (t, g) in enumerate(blocks):
            ins = nc.tensor.matmul(S.bank(u % 3)[:, n * SEQ:(n + 1) * SEQ], S.qop[r, g * SEQ + t * P:][:, 0:P],
                                   S.kop[r, g * SEQ:(g + 1) * SEQ], start=True, stop=True)
        ins.then_inc(T.sem, T.hit(L, "s1", u))
        if u % 2 == 1:
            yield
    output(nc, pe, K, S, L)
    yield


def l2a_scalar(nc, act, K, S, L, before):
    high_parts(nc, act, S, L)
    yield
    for u, (j, blocks) in enumerate(first_units(MHA[L])):
        act.wait_ge(S.V.sem, S.V.at(L, "max", u))
        for n, (t, g) in enumerate(blocks):
            ins = nc.scalar.activation(S.e[:, u % 4, n * SEQ:(n + 1) * SEQ], S.bank(u % 3)[:, n * SEQ:(n + 1) * SEQ],
                                       ACT.Exp, bias=S.negm[:, t, g, j:j + 1], accum_out=S.den[:, t, 4 * g + j:][:, 0:1])
        ins.then_inc(S.A.sem, S.A.hit(L, "e", u))
        if u % 2 == 1:
            yield
    output_turned(nc, act, S, L)
    yield


def l2a_vector(nc, dve, link, K, S, L, before):
    T, V, A = S.T, S.V, S.A
    operands(nc, dve, K, S, L)
    yield
    units = first_units(MHA[L])
    for u, (j, blocks) in enumerate(units):
        dve.wait_ge(T.sem, T.at(L, "s1", u))
        t, g = blocks[0]
        nc.vector.tensor_reduce(S.negm[:, t, g:g + 2, j], S.bank(u % 3).rearrange("p (n k) -> p n k", k=SEQ), X,
                                ALU.max, negate=True).then_inc(V.sem, V.hit(L, "max", u))
        if u % 2 == 1:
            yield
    dve.wait_ge(A.sem, A.at(L, "e", len(units) - 1))
    link(nc.vector.reciprocal(S.rden[:], S.den[:]))
    link(nc.vector.tensor_tensor(S.rden[:], S.rden[:], S.den[:], ALU.mult))
    nc.vector.tensor_tensor(S.on[:].rearrange("p t (h d) -> p t h d", d=HD),
                            S.misc[:, 0:SEQ].rearrange("p (t h d) -> p t h d", t=TILES, d=HD),
                            S.rden[:].unsqueeze(3).to_broadcast([P, TILES, HEADS, HD]), ALU.mult)\
        .then_inc(V.sem, V.hit(L, "on"))
    add_output(nc, dve, S, L, S.bank(1))
    yield


def l2a_gpsimd(nc, pool, K, S, L, before):
    yield
    widen_next(nc, pool, K, S, L)
    for _ in range(1 + len(first_units(MHA[L])) // 2):
        yield


def widen(nc, pool, K, S, L):
    for i, name in enumerate(("wq", "wk")):
        ins = nc.gpsimd.tensor_copy(
            S.wide[:, i * 512:(i + 1) * 512].rearrange("p (h r d) -> p h r d", r=4, d=HD)[:, :, 0:3],
            K.w(L, name).rearrange("p (h d) -> p h d", d=HD).unsqueeze(2).to_broadcast([P, HEADS, 3, HD]))
    return ins


def widen_next(nc, pool, K, S, L):
    following = MHA_ORDER[(MHA_ORDER.index(L) + 1) % len(MHA_ORDER)]
    K.loaded(pool, following)
    pool.wait_ge(S.T.sem, S.T.at(L, "k"))
    widen(nc, pool, K, S, following).then_inc(S.G.sem, S.G.hit(L, "wide"))


def mha_gpsimd(nc, pool, K, S, L, before):
    c = MHA[L]
    yield
    widen_next(nc, pool, K, S, L)
    for _ in range(1 + len(first_units(c)) // 2 + len(second_units(c)) // max(1, c["nk"] // P) + 1):
        yield


L1A_PLAN = dict(tensor=["qk", "v", "s", "pT", "y"], scalar=["qkc", "e", "pTc"], vector=["vc", "max", "x"], gpsimd=[])


def l1a_tensor(nc, pe, K, S, L, before):
    T, V, A, W = S.T, S.V, S.A, K.w
    K.loaded(pe, L)
    pe.wait_ge(A.sem, A.at(before, "xnT"))
    nc.tensor.matmul(S.bank(0)[0:32, 0:SEQ], W(L, "wq"), S.xnT[:], start=True, stop=True)
    nc.tensor.matmul(S.bank(0)[0:32, SEQ:2 * SEQ], W(L, "wk"), S.xnT[:], start=True, stop=True)\
        .then_inc(T.sem, T.hit(L, "qk"))
    for t in range(TILES):
        ins = nc.tensor.matmul(S.bank(1)[:, t * P:(t + 1) * P], S.xnT[:, t * P:(t + 1) * P], K.wv_1a[:],
                               start=True, stop=True)
    ins.then_inc(T.sem, T.hit(L, "v"))
    yield
    pe.wait_ge(A.sem, A.at(L, "qkc"))
    for t in range(TILES):
        ins = nc.tensor.matmul(S.bank(0)[:, t * SEQ:(t + 1) * SEQ], S.ef[0:32, 1024 + t * P:1024 + (t + 1) * P],
                               S.ef[0:32, 1024 + SEQ:1024 + 2 * SEQ], start=True, stop=True)
    ins.then_inc(T.sem, T.hit(L, "s"))
    yield
    pe.wait_ge(A.sem, A.at(L, "e"))
    pe.wait_ge(V.sem, V.at(L, "vc"))
    for t in range(TILES):
        for k in range(TILES):
            ins = nc.tensor.transpose(S.bank(1)[:, k * SEQ + t * P:][:, 0:P],
                                      S.scratch[:, 512 + t * SEQ + k * P:][:, 0:P], K.ident)
    ins.then_inc(T.sem, T.hit(L, "pT"))
    yield
    pe.wait_ge(A.sem, A.at(L, "pTc"))
    for t in range(TILES):
        for k in range(TILES):
            ins = nc.tensor.matmul(S.misc[:, t * P:(t + 1) * P], S.scratch[:, 1024 + k * SEQ + t * P:][:, 0:P],
                                   S.scratch[:, 1536 + k * P:][:, 0:P], start=k == 0, stop=k == TILES - 1)
    ins.then_inc(T.sem, T.hit(L, "y"))
    yield


def l1a_scalar(nc, act, K, S, L, before):
    T, V, A = S.T, S.V, S.A
    act.wait_ge(T.sem, T.at(L, "qk"))
    nc.scalar.activation(S.ef[0:32, 1024:1536], S.bank(0)[0:32], ACT.Copy).then_inc(A.sem, A.hit(L, "qkc"))
    yield
    yield
    act.wait_ge(V.sem, V.at(L, "max"))
    for t in range(TILES):
        ins = nc.scalar.activation(S.scratch[:, 512 + t * SEQ:512 + (t + 1) * SEQ],
                                   S.scratch[:, t * SEQ:(t + 1) * SEQ], ACT.Exp, bias=S.small[:, t:t + 1],
                                   accum_out=S.small[:, 2 + t:3 + t])
    ins.then_inc(A.sem, A.hit(L, "e"))
    yield
    act.wait_ge(T.sem, T.at(L, "pT"))
    nc.scalar.activation(S.scratch[:, 1024:1536], S.bank(1), ACT.Copy).then_inc(A.sem, A.hit(L, "pTc"))
    yield


def l1a_vector(nc, dve, link, K, S, L, before):
    T, V, A = S.T, S.V, S.A
    dve.wait_ge(T.sem, T.at(L, "v"))
    nc.vector.tensor_copy(S.scratch[:, 1536:1792], S.bank(1)[:, 0:SEQ]).then_inc(V.sem, V.hit(L, "vc"))
    yield
    z, zero, masked = S.ef[:, 0:512], S.ef[:, 512:1024], S.scratch[:, 0:512]
    dve.wait_ge(T.sem, T.at(L, "s"))
    link(nc.vector.scalar_tensor_tensor(z, S.bank(0), 32.0 ** -0.5, K.causal[:], ALU.mult, ALU.mult))
    link(nc.vector.tensor_scalar(zero, z, 0.0, LOWEST, ALU.is_equal, ALU.mult))
    link(nc.vector.tensor_tensor(masked, z, zero, ALU.add))
    nc.vector.tensor_reduce(S.small[:, 0:2], masked.rearrange("p (t k) -> p t k", t=TILES), X, ALU.max, negate=True)\
        .then_inc(V.sem, V.hit(L, "max"))
    yield
    dve.wait_ge(A.sem, A.at(L, "e"))
    link(nc.vector.reciprocal(S.small[:, 4:6], S.small[:, 2:4]))
    yield
    dve.wait_ge(T.sem, T.at(L, "y"))
    for t in range(TILES):
        ins = nc.vector.scalar_tensor_tensor(S.x[:, t], S.misc[:, t * P:(t + 1) * P], S.small[:, 4 + t:5 + t],
                                             S.x[:, t], ALU.mult, ALU.add)
    ins.then_inc(V.sem, V.hit(L, "x"))
    yield


def l1a_gpsimd(nc, pool, K, S, L, before):
    for _ in range(4):
        yield


L0F_PLAN = dict(
    tensor=["lg", "sT", "sel", "rank", "xt", "sb", "rb", "g", "u", "eo", "sg", "su", "y"],
    scalar=["ex", "sTc", "xtc", "sbc", "gl", "eoc", "sgl"],
    vector=["d", "sc", "selT", "selc", "P", "rmT", "pw", "h", "sh", "x"], gpsimd=[])


def l0f_tensor(nc, pe, K, S, L, before):
    T, V, A, W = S.T, S.V, S.A, K.w
    K.loaded(pe, L)
    pe.wait_ge(A.sem, A.at(before, "xnT"))
    for t in range(TILES):
        ins = nc.tensor.matmul(S.misc[:, t * EXPERTS:(t + 1) * EXPERTS], S.xnT[:, t * P:(t + 1) * P], W(L, "gate"),
                               start=True, stop=True)
    ins.then_inc(T.sem, T.hit(L, "lg"))
    yield
    pe.wait_ge(V.sem, V.at(L, "sc"))
    for t in range(TILES):
        ins = nc.tensor.transpose(S.bank(0)[0:EXPERTS, t * P:(t + 1) * P], S.score[:, t], K.ident)
    ins.then_inc(T.sem, T.hit(L, "sT"))
    yield
    pe.wait_ge(V.sem, V.at(L, "selT"))
    for t in range(TILES):
        ins = nc.tensor.transpose(S.bank(1)[:, t * EXPERTS:(t + 1) * EXPERTS], S.selT[0:EXPERTS, t * P:(t + 1) * P],
                                  K.ident[0:EXPERTS, 0:EXPERTS])
    ins.then_inc(T.sem, T.hit(L, "sel"))
    pe.wait_ge(V.sem, V.at(L, "selc"))
    for t in range(TILES):
        for k in range(TILES):
            nc.tensor.matmul(S.bank(2)[:, t * EXPERTS:(t + 1) * EXPERTS], K.upto[:, k, t * P:(t + 1) * P],
                             S.sel_bf[:, k], start=k == 0, stop=k == TILES - 1)
    for k in range(TILES):
        ins = nc.tensor.matmul(S.bank(0)[0:EXPERTS, 0:SEQ], S.sel_bf[:, k], K.upto[:, k], start=k == 0,
                               stop=k == TILES - 1)
    ins.then_inc(T.sem, T.hit(L, "rank"))
    yield
    pe.wait_ge(V.sem, V.at(L, "P"))
    for t in range(TILES):
        ins = nc.tensor.matmul(S.bank(1), S.xn[:, t], S.ef[:, t * 512:(t + 1) * 512], start=t == 0,
                               stop=t == TILES - 1)
    ins.then_inc(T.sem, T.hit(L, "xt"))
    for c in range(4):
        ins = nc.tensor.matmul(S.ps[:, 1024 + c * SEQ:1024 + (c + 1) * SEQ], W("base", "spread")[0:EXPERTS, c * P:(c + 1) * P],
                               S.sT[0:EXPERTS], start=True, stop=True)
    ins.then_inc(T.sem, T.hit(L, "sb"))
    pe.wait_ge(A.sem, A.at(L, "xtc"))
    pe.wait_ge(V.sem, V.at(L, "rmT"))
    for c in range(4):
        ins = nc.tensor.matmul(S.ps[:, c * SEQ:(c + 1) * SEQ], K.spread_bf[0:EXPERTS, c * P:(c + 1) * P],
                               S.rmT[0:EXPERTS], start=True, stop=True)
    ins.then_inc(T.sem, T.hit(L, "rb"))
    yield
    pe.wait_ge(A.sem, A.at(L, "sbc"))
    for name, w, base in (("g", "wg", 1024), ("u", "wu", 0)):
        if name == "u":
            pe.wait_ge(V.sem, V.at(L, "pw"))
        for e in range(EXPERTS):
            for f in range(2):
                ins = nc.tensor.matmul(S.ps[:, base + f * 512 + e * CAP:][:, 0:CAP],
                                       W(L, w)[:, e * EXP_F + f * P:][:, 0:P],
                                       S.ef[:, 1024 + e * CAP:1024 + (e + 1) * CAP], start=True, stop=True)
            if e % 8 == 7:
                if e == EXPERTS - 1:
                    ins.then_inc(T.sem, T.hit(L, name))
                yield
    pe.wait_ge(V.sem, V.at(L, "h"))
    for e in range(EXPERTS):
        for f in range(2):
            ins = nc.tensor.matmul(S.bank(2)[32 * (e % 4):32 * (e % 4) + 32, e // 4 * P:(e // 4 + 1) * P],
                                   S.ef[:, f * 512 + e * CAP:][:, 0:CAP], W(L, "wd")[:, e * 256 + f * P:][:, 0:P],
                                   start=f == 0, stop=f == 1)
        if e % 8 == 7:
            if e == EXPERTS - 1:
                ins.then_inc(T.sem, T.hit(L, "eo"))
            yield
    for name, b, w in (("sg", 3, "sg"), ("su", 0, "su")):
        for f in range(2):
            ins = nc.tensor.matmul(S.bank(b)[:, f * SEQ:(f + 1) * SEQ], W(L, w)[:, f * P:(f + 1) * P], S.xnT[:],
                                   start=True, stop=True)
        ins.then_inc(T.sem, T.hit(L, name))
    yield
    pe.wait_ge(A.sem, A.at(L, "eoc"))
    pe.wait_ge(V.sem, V.at(L, "sh"))
    for t in range(TILES):
        out = S.bank(1)[:, t * P:(t + 1) * P]
        for c in range(4):
            nc.tensor.matmul(out, S.scratch[:, c * SEQ + t * P:][:, 0:P], S.ef[:, 1536 + c * P:][:, 0:P],
                             start=c == 0, stop=False)
        for f in range(2):
            ins = nc.tensor.matmul(out, S.scratch[:, 1536 + f * SEQ + t * P:][:, 0:P], W(L, "sd")[:, f * P:(f + 1) * P],
                                   start=False, stop=f == 1)
    ins.then_inc(T.sem, T.hit(L, "y"))
    yield


def l0f_scalar(nc, act, K, S, L, before):
    T, V, A = S.T, S.V, S.A
    act.wait_ge(V.sem, V.at(L, "d"))
    nc.scalar.activation(S.score[:], S.dist[:], ACT.Exp).then_inc(A.sem, A.hit(L, "ex"))
    yield
    act.wait_ge(T.sem, T.at(L, "sT"))
    nc.scalar.activation(S.sT[0:EXPERTS], S.bank(0)[0:EXPERTS, 0:SEQ], ACT.Copy).then_inc(A.sem, A.hit(L, "sTc"))
    yield
    yield
    act.wait_ge(T.sem, T.at(L, "xt"))
    nc.scalar.activation(S.ef[:, 1024:1536], S.bank(1), ACT.Copy).then_inc(A.sem, A.hit(L, "xtc"))
    act.wait_ge(T.sem, T.at(L, "sb"))
    nc.scalar.activation(S.scratch[:, 1024:2048], S.ps[:, 1024:2048], ACT.Copy).then_inc(A.sem, A.hit(L, "sbc"))
    yield
    yield
    act.wait_ge(T.sem, T.at(L, "g"))
    act.wait_ge(V.sem, V.at(L, "pw"))
    nc.scalar.activation(S.scratch[:, 1024:2048], S.ps[:, 1024:2048], ACT.Gelu).then_inc(A.sem, A.hit(L, "gl"))
    yield
    yield
    yield
    yield
    act.wait_ge(T.sem, T.at(L, "eo"))
    nc.scalar.activation(S.ef[:, 1536:2048], S.bank(2), ACT.Copy).then_inc(A.sem, A.hit(L, "eoc"))
    yield
    act.wait_ge(T.sem, T.at(L, "sg"))
    act.wait_ge(V.sem, V.at(L, "h"))
    nc.scalar.activation(S.scratch[:, 1024:1536], S.bank(3), ACT.Gelu).then_inc(A.sem, A.hit(L, "sgl"))
    yield
    yield


def l0f_vector(nc, dve, link, K, S, L, before):
    T, V, A = S.T, S.V, S.A
    natural = "p (r i) -> p i r"
    dve.wait_ge(T.sem, T.at(L, "lg"))
    logits = S.misc[:, 0:2 * EXPERTS].rearrange("p (t e) -> p t e", t=TILES)
    link(nc.vector.tensor_reduce(S.small[:, 0:2], logits, X, ALU.max, negate=True))
    nc.vector.tensor_tensor(S.dist[:], logits, S.small[:, 0:2].unsqueeze(2).to_broadcast([P, 2, EXPERTS]), ALU.add)\
        .then_inc(V.sem, V.hit(L, "d"))
    yield
    dve.wait_ge(A.sem, A.at(L, "ex"))
    link(nc.vector.tensor_reduce(S.small[:, 2:4], S.score[:], X, ALU.add))
    link(nc.vector.reciprocal(S.small[:, 4:6], S.small[:, 2:4]))
    nc.vector.tensor_tensor(S.score[:], S.score[:], S.small[:, 4:6].unsqueeze(2).to_broadcast([P, 2, EXPERTS]),
                            ALU.mult).then_inc(V.sem, V.hit(L, "sc"))
    dve.wait_ge(A.sem, A.at(L, "sTc"))
    link(nc.vector.tensor_copy(S.work[0:EXPERTS, 0].rearrange("p (i r) -> p i r", r=4),
                               S.sT[0:EXPERTS].rearrange(natural, r=4)))
    for n in range(CAP // 8):
        link(nc.vector.max(S.best[0:EXPERTS], S.work[0:EXPERTS, n % 2]))
        link(nc.vector.match_replace(out=S.work[0:EXPERTS, 1 - n % 2], in_to_replace=S.best[0:EXPERTS],
                                     in_values=S.work[0:EXPERTS, n % 2], imm_value=-1.0))
    yield
    nc.vector.tensor_scalar(S.selT[0:EXPERTS].rearrange(natural, r=4),
                            S.work[0:EXPERTS, 0].rearrange("p (i r) -> p i r", r=4), 0.0, None, ALU.is_lt)\
        .then_inc(V.sem, V.hit(L, "selT"))
    dve.wait_ge(T.sem, T.at(L, "sel"))
    nc.vector.tensor_copy(S.sel_bf[:], S.bank(1)[:, 0:2 * EXPERTS].rearrange("p (t e) -> p t e", t=TILES))\
        .then_inc(V.sem, V.hit(L, "selc"))
    dve.wait_ge(T.sem, T.at(L, "rank"))
    dve.wait_ge(V.sem, V.at(L, "selc"))
    link(nc.vector.tensor_tensor(S.rank[:], S.bank(2)[:, 0:2 * EXPERTS].rearrange("p (t e) -> p t e", t=TILES),
                                 S.sel_bf[:], ALU.mult))
    yield
    for t in range(TILES):
        ins = nc.vector.tensor_tensor(
            S.ef[:, t * 512:(t + 1) * 512].rearrange("p (e s) -> p e s", s=CAP),
            K.w("base", "count").unsqueeze(1).to_broadcast([P, EXPERTS, CAP]),
            S.rank[:, t].unsqueeze(2).to_broadcast([P, EXPERTS, CAP]), ALU.is_equal)
    ins.then_inc(V.sem, V.hit(L, "P"))
    nc.vector.tensor_tensor(S.rmT[0:EXPERTS], S.bank(0)[0:EXPERTS, 0:SEQ], S.selT[0:EXPERTS], ALU.mult)\
        .then_inc(V.sem, V.hit(L, "rmT"))
    yield
    dve.wait_ge(T.sem, T.at(L, "rb"))
    dve.wait_ge(A.sem, A.at(L, "sbc"))
    nc.vector.scalar_tensor_tensor(S.scratch[:, 0:1024], S.ps[:, 0:1024], K.w("base", "slot"),
                                   S.scratch[:, 1024:2048], ALU.is_equal, ALU.mult).then_inc(V.sem, V.hit(L, "pw"))
    yield
    yield
    yield
    yield
    dve.wait_ge(T.sem, T.at(L, "u"))
    dve.wait_ge(A.sem, A.at(L, "gl"))
    nc.vector.tensor_tensor(S.ef[:, 0:1024], S.ps[:, 0:1024], S.scratch[:, 1024:2048], ALU.mult)\
        .then_inc(V.sem, V.hit(L, "h"))
    yield
    yield
    dve.wait_ge(T.sem, T.at(L, "su"))
    dve.wait_ge(A.sem, A.at(L, "sgl"))
    nc.vector.tensor_tensor(S.scratch[:, 1536:2048], S.bank(0), S.scratch[:, 1024:1536], ALU.mult)\
        .then_inc(V.sem, V.hit(L, "sh"))
    yield
    add_output(nc, dve, S, L, S.bank(1))
    yield


def l0f_gpsimd(nc, pool, K, S, L, before):
    for _ in range(12):
        yield


def add_output(nc, dve, S, L, y):
    dve.wait_ge(S.T.sem, S.T.at(L, "y"))
    nc.vector.tensor_tensor(S.x[:], y[:, 0:SEQ].rearrange("p (t d) -> p t d", d=P), S.x[:], ALU.add)\
        .then_inc(S.V.sem, S.V.hit(L, "x"))


L1F_PLAN = dict(tensor=["up0", "up1", "y"], scalar=["r0", "r1"], vector=["xq", "h0", "h1", "x"], gpsimd=[])


def l1f_tensor(nc, pe, K, S, L, before):
    T, V, A = S.T, S.V, S.A
    pe.wait_ge(V.sem, V.at(L, "xq"))
    for c in range(4):
        ins = nc.tensor.matmul(S.ps[:, c * SEQ:(c + 1) * SEQ], K.w1q[:, c * P:(c + 1) * P], S.hi_bf[:, 0:SEQ],
                               start=True, stop=True)
        if c % 2:
            ins.then_inc(T.sem, T.hit(L, "up%d" % (c // 2)))
    yield
    pe.wait_ge(V.sem, V.at(L, "h1"))
    for t in range(TILES):
        out = S.misc[:, t * P:(t + 1) * P]
        for c in range(4):
            nc.tensor.matmul(out, S.kop_bf[:, c * SEQ + t * P:][:, 0:P], K.w2q[:, c * P:(c + 1) * P],
                             start=c == 0, stop=False)
        ins = nc.tensor.matmul(out, K.ones_bf[0:1, 0:P], K.b2q[0:1], start=False, stop=True)
    ins.then_inc(T.sem, T.hit(L, "y"))
    yield


def l1f_scalar(nc, act, K, S, L, before):
    T, V, A = S.T, S.V, S.A
    for n in range(2):
        act.wait_ge(T.sem, T.at(L, "up%d" % n))
        for c in (2 * n, 2 * n + 1):
            ins = nc.scalar.activation(S.scratch[:, c * SEQ:(c + 1) * SEQ], S.ps[:, c * SEQ:(c + 1) * SEQ], ACT.Relu,
                                       bias=K.b1q[:, c:c + 1], scale=1.0 / 64)
        ins.then_inc(A.sem, A.hit(L, "r%d" % n))
    yield
    yield


def l1f_vector(nc, dve, link, K, S, L, before):
    T, V, A = S.T, S.V, S.A
    dve.wait_ge(A.sem, A.at(before, "xnT"))
    link(nc.vector.tensor_scalar(S.scratch[:, 1024:1280], S.xnT[:], 16.0, 127.0, ALU.mult, ALU.min))
    link(nc.vector.tensor_scalar(S.scratch[:, 1280:1536], S.scratch[:, 1024:1280], -128.0, ROUND, ALU.max, ALU.add))
    nc.vector.tensor_scalar(S.hi_bf[:, 0:SEQ], S.scratch[:, 1280:1536], -ROUND, None, ALU.add)\
        .then_inc(V.sem, V.hit(L, "xq"))
    yield
    for n in range(2):
        dve.wait_ge(A.sem, A.at(L, "r%d" % n))
        part = slice(n * 512, (n + 1) * 512)
        link(nc.vector.tensor_scalar(S.scratch[:, 1024:1536], S.scratch[:, part], 127.0, ROUND, ALU.min, ALU.add))
        nc.vector.tensor_scalar(S.kop_bf[:, part], S.scratch[:, 1024:1536], -ROUND, None, ALU.add)\
            .then_inc(V.sem, V.hit(L, "h%d" % n))
        dve.wait_ge(V.sem, V.at(L, "h%d" % n))
    dve.wait_ge(T.sem, T.at(L, "y"))
    for t in range(TILES):
        ins = nc.vector.scalar_tensor_tensor(S.x[:, t], S.misc[:, t * P:(t + 1) * P], 1.0 / 1024, S.x[:, t],
                                             ALU.mult, ALU.add)
    ins.then_inc(V.sem, V.hit(L, "x"))
    yield


def l1f_gpsimd(nc, pool, K, S, L, before):
    yield
    yield


L2X_PLAN = dict(
    gpsimd=["rstd2"],
    vector=["var2", "xn2", "vaug"] + [("max", u) for u in range(4)] + ["negm"]
    + [("on", u) for u in range(6)] + [("h", c) for c in range(4)] + ["x"],
    scalar=["xn2T", "kc", ("qc", 0), ("qc", 1), "nmT"] + [("e", u) for u in range(4)] + ["oT0", "oT1"] + [("g", c) for c in range(4)],
    tensor=["nT", "kv", ("q", 0), ("q", 1)] + [("s1", u) for u in range(4)] + ["mT"] + [("s2", u) for u in range(4)]
    + ["pv0", "pv1", "pv2", "oT0", "pv3", "pv4", "pv5", "oT1"] + [("ff", c) for c in range(4)] + ["y"])
PAIR_BANKS = [(0, 3), (3, 6), (6, 8)]


def l2x_gpsimd(nc, pool, K, S, L, before):
    pool.wait_ge(S.V.sem, S.V.at(L, "var2"))
    nc.gpsimd.tensor_tensor(S.rstd3[:], S.var3[:], K.neg_half3[:], ALU.pow).then_inc(S.G.sem, S.G.hit(L, "rstd2"))
    for _ in range(15):
        yield


def l2x_tensor(nc, pe, K, S, L, before):
    T, V, A, W = S.T, S.V, S.A, K.w
    K.loaded(pe, L)
    pe.wait_ge(V.sem, V.at(L, "xn2"))
    pe.wait_ge(A.sem, A.at(before, "xnT"))
    for t in range(TILES):
        nc.tensor.transpose(S.bank(0)[:, t * P:(t + 1) * P], S.xn2[:, t], K.ident)
    nc.tensor.transpose(S.bank(0)[:, SEQ:SEQ + KEYS], S.cn[0:KEYS], K.ident[0:KEYS, 0:KEYS])\
        .then_inc(T.sem, T.hit(L, "nT"))
    yield
    pe.wait_ge(A.sem, A.at(L, "xn2T"))
    nc.tensor.matmul(S.misc[:, 0:KEYS], W(L, "wk"), S.cnT[:], start=True, stop=True)
    nc.tensor.matmul(S.bank(0)[0:64, 0:64], S.cnT[:], W(L, "wv"), start=True, stop=True)
    nc.tensor.matmul(S.bank(0)[64:128, 0:64], S.cnT[:], W(L, "wv"), start=True, stop=True)\
        .then_inc(T.sem, T.hit(L, "kv"))
    for n in range(2):
        if n:
            pe.wait_ge(A.sem, A.at(L, "qc", 0))
        for a in range(4):
            ins = nc.tensor.matmul(S.ps[:, BANK + a * SEQ:BANK + (a + 1) * SEQ], W(L, "wq")[:, (4 * n + a) * P:][:, 0:P],
                                   S.xn2T[:], start=True, stop=True)
        ins.then_inc(T.sem, T.hit(L, "q", n))
        yield
    for u in range(4):
        t, half = u // 2, u % 2
        r = slice(64 * half, 64 * half + 64)
        pe.wait_ge(A.sem, A.at(L, "qc", 1))
        if u == 0:
            pe.wait_ge(V.sem, V.at(L, "vaug"))
        if u == 3:
            pe.wait_ge(V.sem, V.at(L, "max", 0))
        for a in range(8):
            ins = nc.tensor.matmul(S.bank(u % 3)[:, a * KEYS:(a + 1) * KEYS], S.scratch[r, a * SEQ + t * P:][:, 0:P],
                                   S.kT[r], start=True, stop=True)
        ins.then_inc(T.sem, T.hit(L, "s1", u))
        if u % 2:
            yield
    pe.wait_ge(V.sem, V.at(L, "negm"))
    for t in range(TILES):
        ins = nc.tensor.transpose(S.misc_bf[:, t * P:(t + 1) * P], S.nm2[:, t].rearrange("p j s -> p (j s)"),
                                  K.ident_bf)
    ins.then_inc(T.sem, T.hit(L, "mT"))
    yield
    for u in range(4):
        if u == 0:
            pe.wait_ge(A.sem, A.at(L, "nmT"))
        if u == 3:
            pe.wait_ge(A.sem, A.at(L, "e", 0))
        for half in range(2):
            r = slice(64 * half, 64 * half + 64)
            for i in range(2):
                a = 2 * u + i
                out = S.bank(u % 3)[r, i * SEQ:(i + 1) * SEQ]
                nc.tensor.matmul(out, S.kT[r], S.scratch[r, a * SEQ:(a + 1) * SEQ], start=True, stop=False)
                ins = nc.tensor.matmul(out, K.sel2[r, a], S.nmT[r], start=False, stop=True)
        ins.then_inc(T.sem, T.hit(L, "s2", u))
        if u % 2:
            yield
    for t in range(TILES):
        if t == 0:
            pe.wait_ge(A.sem, A.at(L, "e", 3))
        else:
            pe.wait_ge(A.sem, A.at(L, "oT0"))
        for n, (a0, a1) in enumerate(PAIR_BANKS):
            for a in range(a0, a1):
                ins = nc.tensor.matmul(S.bank(n)[:, (a - a0) * 130:(a - a0 + 1) * 130], S.ef[:, a * SEQ + t * P:][:, 0:P],
                                       S.vpair[:], start=True, stop=True)
            ins.then_inc(T.sem, T.hit(L, "pv%d" % (3 * t + n)))
        yield
        pe.wait_ge(V.sem, V.at(L, "on", 3 * t + 2))
        for a in range(8):
            ins = nc.tensor.transpose(S.ps[:, a * P:(a + 1) * P], S.scratch[:, t * 1024 + a * P:][:, 0:P], K.ident)
        ins.then_inc(T.sem, T.hit(L, "oT%d" % t))
        yield
    for c in range(4):
        if c == 0:
            pe.wait_ge(A.sem, A.at(L, "oT1"))
        if c == 3:
            pe.wait_ge(V.sem, V.at(L, "h", 0))
        for i in range(2):
            ins = nc.tensor.matmul(S.bank(c % 3)[:, i * SEQ:(i + 1) * SEQ], W(L, "w1")[:, i * 512 + c * P:][:, 0:P],
                                   S.xn2T[:], start=True, stop=True)
        ins.then_inc(T.sem, T.hit(L, "ff", c))
        if c % 2:
            yield
    pe.wait_ge(V.sem, V.at(L, "h", 3))
    for t in range(TILES):
        out = S.misc[:, t * P:(t + 1) * P]
        for a in range(8):
            nc.tensor.matmul(out, S.oT2(t, a), W(L, "wo")[:, a * P:(a + 1) * P], start=a == 0, stop=False)
        for c in range(4):
            ins = nc.tensor.matmul(out, S.scratch[:, 1024 + c * SEQ + t * P:][:, 0:P], W(L, "w2")[:, c * P:(c + 1) * P],
                                   start=False, stop=c == 3)
    ins.then_inc(T.sem, T.hit(L, "y"))
    yield


def l2x_scalar(nc, act, K, S, L, before):
    T, V, A, W = S.T, S.V, S.A, K.w
    yield
    act.wait_ge(T.sem, T.at(L, "nT"))
    nc.scalar.activation(S.cnT[:], S.bank(0)[:, SEQ:SEQ + KEYS], ACT.Identity, bias=W(L, "cb"), scale=W(L, "cg"))
    nc.scalar.activation(S.xn2T[:], S.bank(0)[:, 0:SEQ], ACT.Identity, bias=W(L, "lb"), scale=W(L, "lg"))\
        .then_inc(A.sem, A.hit(L, "xn2T"))
    act.wait_ge(T.sem, T.at(L, "kv"))
    nc.scalar.activation(S.kT[:], S.misc[:, 0:KEYS], ACT.Copy).then_inc(A.sem, A.hit(L, "kc"))
    for n in range(2):
        act.wait_ge(T.sem, T.at(L, "q", n))
        nc.scalar.activation(S.scratch[:, n * 1024:(n + 1) * 1024], S.ps[:, BANK:BANK + 1024], ACT.Copy)\
            .then_inc(A.sem, A.hit(L, "qc", n))
        yield
    yield
    yield
    act.wait_ge(T.sem, T.at(L, "mT"))
    nc.scalar.activation(S.nmT[:], S.misc_bf[:, 0:SEQ], ACT.Copy).then_inc(A.sem, A.hit(L, "nmT"))
    yield
    for u in range(4):
        act.wait_ge(T.sem, T.at(L, "s2", u))
        nc.scalar.activation(S.e[:, u], S.bank(u % 3), ACT.Exp, scale=64.0 ** -0.5).then_inc(A.sem, A.hit(L, "e", u))
        if u % 2:
            yield
    for t in range(TILES):
        yield
        act.wait_ge(T.sem, T.at(L, "oT%d" % t))
        nc.scalar.activation(S.oT2_all(t), S.ps[:, 0:1024], ACT.Copy).then_inc(A.sem, A.hit(L, "oT%d" % t))
        yield
    for c in range(4):
        act.wait_ge(T.sem, T.at(L, "ff", c))
        nc.scalar.activation(S.scratch[:, c * SEQ:(c + 1) * SEQ], S.bank(c % 3)[:, SEQ:2 * SEQ], ACT.Silu)\
            .then_inc(A.sem, A.hit(L, "g", c))
        if c % 2:
            yield
    yield


def l2x_vector(nc, dve, link, K, S, L, before):
    T, V, A = S.T, S.V, S.A
    dve.wait_ge(V.sem, V.at(before, "xn"))
    for t in range(TILES):
        nc.vector.bn_stats(S.stats[:, t], S.xn[:, t])
    link(nc.vector.bn_stats(S.stats[0:KEYS, 2], S.ctx[0:KEYS]))
    for t in range(TILES):
        nc.vector.bn_aggr(S.mv[:, t], S.stats[:, t])
    link(nc.vector.bn_aggr(S.mv[0:KEYS, 2], S.stats[0:KEYS, 2]))
    nc.vector.tensor_scalar(S.var3[:], S.mv[:, :, 1], EPS, None, ALU.add).then_inc(V.sem, V.hit(L, "var2"))
    dve.wait_ge(S.G.sem, S.G.at(L, "rstd2"))
    for t in range(TILES):
        nc.vector.tensor_scalar(S.xn2[:, t], S.xn[:, t], S.mv[:, t, 0:1], S.rstd3[:, t:t + 1],
                                ALU.subtract, ALU.mult)
    nc.vector.tensor_scalar(S.cn[0:KEYS], S.ctx[0:KEYS], S.mv[0:KEYS, 2, 0:1], S.rstd3[0:KEYS, 2:3],
                            ALU.subtract, ALU.mult).then_inc(V.sem, V.hit(L, "xn2"))
    yield
    dve.wait_ge(T.sem, T.at(L, "kv"))
    dve.wait_ge(A.sem, A.at(L, "kc"))
    nc.vector.tensor_copy(S.vpair[0:64, 0:64], S.bank(0)[0:64, 0:64])
    nc.vector.tensor_copy(S.vpair[64:128, 65:129], S.bank(0)[64:128, 0:64]).then_inc(V.sem, V.hit(L, "vaug"))
    yield
    yield
    for u in range(4):
        dve.wait_ge(T.sem, T.at(L, "s1", u))
        nc.vector.tensor_reduce(S.negm2[:, u // 2, u % 2], S.bank(u % 3).rearrange("p (a k) -> p a k", k=KEYS), X,
                                ALU.max, negate=True).then_inc(V.sem, V.hit(L, "max", u))
        if u % 2:
            yield
    dve.wait_ge(V.sem, V.at(L, "max", 3))
    link(nc.vector.tensor_copy(S.nm2[:, :, :, 0:8], S.negm2[:]))
    nc.vector.tensor_tensor(S.nm2[:, :, :, 8:16], S.negm2[:], S.nm2[:, :, :, 0:8], ALU.subtract)\
        .then_inc(V.sem, V.hit(L, "negm"))
    yield
    yield
    yield
    for t in range(TILES):
        for n, (a0, a1) in enumerate(PAIR_BANKS):
            m = 2 * (a1 - a0)
            dve.wait_ge(T.sem, T.at(L, "pv%d" % (3 * t + n)))
            o = S.bank(n)[:, 0:65 * m].rearrange("p (h d) -> p h d", d=65)
            link(nc.vector.reciprocal(S.small[:, 0:m], o[:, :, 64]))
            nc.vector.tensor_tensor(
                S.scratch[:, t * 1024 + a0 * P:t * 1024 + a1 * P].rearrange("p (h d) -> p h d", d=64), o[:, :, 0:64],
                S.small[:, 0:m].unsqueeze(2).to_broadcast([P, m, 64]), ALU.mult).then_inc(V.sem, V.hit(L, "on", 3 * t + n))
            dve.wait_ge(V.sem, V.at(L, "on", 3 * t + n))
        yield
        yield
    for c in range(4):
        dve.wait_ge(A.sem, A.at(L, "g", c))
        nc.vector.tensor_tensor(S.scratch[:, 1024 + c * SEQ:1024 + (c + 1) * SEQ], S.bank(c % 3)[:, 0:SEQ],
                                S.scratch[:, c * SEQ:(c + 1) * SEQ], ALU.mult).then_inc(V.sem, V.hit(L, "h", c))
        if c % 2:
            yield
    add_output(nc, dve, S, L, S.misc)
    yield


L2F_PLAN = dict(
    gpsimd=[],
    tensor=["lg"] + [k for e in range(MOE) for k in
                     [("up", e, 0), ("up", e, 1)] + ([("dn", e - 1)] if e else [])] + [("dn", MOE - 1)],
    scalar=["ex"] + [("h", e, i) for e in range(MOE) for i in range(2)],
    vector=["d", "w"] + [("acc", e) for e in range(MOE)])


def l2f_tensor(nc, pe, K, S, L, before):
    T, V, A, W = S.T, S.V, S.A, K.w
    K.loaded(pe, L)
    rows = K.rows[L]
    pe.wait_ge(A.sem, A.at(before, "xnT"))
    for t in range(TILES):
        out = S.misc[:, t * MOE:(t + 1) * MOE]
        nc.tensor.matmul(out, S.xnT[:, t * P:(t + 1) * P], W(L, "wr"), start=True, stop=False)
        ins = nc.tensor.matmul(out, K.ones_bf[96:99, 0:P], rows[96:99, 0:MOE], start=False, stop=True)
    ins.then_inc(T.sem, T.hit(L, "lg"))
    yield

    def down(e):
        if e == 0:
            pe.wait_ge(V.sem, V.at(L, "d"))
        else:
            pe.wait_ge(V.sem, V.at(L, "acc", e - 1))
        pe.wait_ge(A.sem, A.at(L, "h", e, 1))
        part = 32 * (e // 4)
        for t in range(TILES):
            out = S.misc[:, t * P:(t + 1) * P]
            for c in range(MOE_C):
                nc.tensor.matmul(out, S.scratch[:, (e % 2) * 1024 + c * SEQ + t * P:][:, 0:P],
                                 W(L, "w2")[:, (e * MOE_C + c) * P:][:, 0:P], start=c == 0, stop=False)
            ins = nc.tensor.matmul(out, K.ones_bf[part:part + 3, 0:P], rows[part:part + 3, e % 4 * P:(e % 4 + 1) * P],
                                   start=False, stop=True)
        ins.then_inc(T.sem, T.hit(L, "dn", e))

    for e in range(MOE):
        for i in range(2):
            n = 2 * e + i
            if n >= 3:
                pe.wait_ge(A.sem, A.at(L, "h", (n - 3) // 2, (n - 3) % 2))
            for c in range(2):
                ins = nc.tensor.matmul(S.bank(n % 3)[:, c * SEQ:(c + 1) * SEQ],
                                       W(L, "w1")[:, e * MOE_H + (2 * i + c) * P:][:, 0:P], S.xnT[:],
                                       start=True, stop=True)
            ins.then_inc(T.sem, T.hit(L, "up", e, i))
        if e:
            down(e - 1)
        yield
    down(MOE - 1)
    yield


def l2f_scalar(nc, act, K, S, L, before):
    T, V, A, W = S.T, S.V, S.A, K.w
    act.wait_ge(V.sem, V.at(L, "d"))
    nc.scalar.activation(S.gate[:], S.gate_d[:], ACT.Exp).then_inc(A.sem, A.hit(L, "ex"))
    yield
    for e in range(MOE):
        for i in range(2):
            n = 2 * e + i
            act.wait_ge(T.sem, T.at(L, "up", e, i))
            if e >= 2 and i == 0:
                act.wait_ge(T.sem, T.at(L, "dn", e - 2))
            for c in range(2):
                ins = nc.scalar.activation(S.scratch[:, (e % 2) * 1024 + (2 * i + c) * SEQ:][:, 0:SEQ],
                                           S.bank(n % 3)[:, c * SEQ:(c + 1) * SEQ], ACT.Gelu,
                                           bias=W(L, "b1")[:, e * MOE_C + 2 * i + c:][:, 0:1])
            ins.then_inc(A.sem, A.hit(L, "h", e, i))
        yield
    yield


def l2f_vector(nc, dve, link, K, S, L, before):
    T, V, A = S.T, S.V, S.A
    dve.wait_ge(T.sem, T.at(L, "lg"))
    link(nc.vector.tensor_copy(S.logit[:], S.misc[:, 0:2 * MOE].rearrange("p (t e) -> p t e", t=TILES)))
    for t in range(TILES):
        ins = nc.vector.max(S.best8[:, t], S.logit[:, t])
    link(ins)
    nc.vector.tensor_tensor(S.gate_d[:], S.logit[:], S.best8[:, :, 0:1].to_broadcast([P, 2, MOE]), ALU.subtract)\
        .then_inc(V.sem, V.hit(L, "d"))
    link(nc.vector.tensor_tensor(S.kept[:], S.logit[:], S.best8[:, :, 1:2].to_broadcast([P, 2, MOE]), ALU.is_ge))
    dve.wait_ge(A.sem, A.at(L, "ex"))
    link(nc.vector.tensor_tensor(S.gate[:], S.gate[:], S.kept[:], ALU.mult))
    link(nc.vector.tensor_reduce(S.small[:, 0:2], S.gate[:], X, ALU.add))
    link(nc.vector.reciprocal(S.small[:, 2:4], S.small[:, 0:2]))
    nc.vector.tensor_tensor(S.gate[:], S.gate[:], S.small[:, 2:4].unsqueeze(2).to_broadcast([P, 2, MOE]), ALU.mult)\
        .then_inc(V.sem, V.hit(L, "w"))
    dve.wait_ge(V.sem, V.at(L, "w"))
    yield
    for e in range(MOE + 1):
        if e:
            dve.wait_ge(T.sem, T.at(L, "dn", e - 1))
            for t in range(TILES):
                ins = nc.vector.scalar_tensor_tensor(S.x[:, t], S.misc[:, t * P:(t + 1) * P], S.gate[:, t, e - 1:e],
                                                     S.x[:, t], ALU.mult, ALU.add)
            ins.then_inc(V.sem, V.hit(L, "acc", e - 1))
            dve.wait_ge(V.sem, V.at(L, "acc", e - 1))
        yield


def l2f_gpsimd(nc, pool, K, S, L, before):
    for _ in range(MOE + 2):
        yield


RANKS = [1, 2, 4, 8]
L3F_PLAN = dict(gpsimd=["nrm"], tensor=["pj", "lg", "zT", "y"], scalar=["pjc", "ex", "zTc"],
                vector=["sq", "ss", "d", "zs", "x"])


def l3f_gpsimd(nc, pool, K, S, L, before):
    yield
    pool.wait_ge(S.V.sem, S.V.at(L, "ss"))
    nc.gpsimd.tensor_tensor(S.small[:, 2:4], S.small[:, 0:2], K.half[:], ALU.pow).then_inc(S.G.sem, S.G.hit(L, "nrm"))
    for _ in range(3):
        yield


def l3f_tensor(nc, pe, K, S, L, before):
    T, V, A, W = S.T, S.V, S.A, K.w
    K.loaded(pe, L)
    pe.wait_ge(A.sem, A.at(before, "xnT"))
    nc.tensor.matmul(S.bank(0)[0:32, 0:SEQ], W(L, "wp"), S.xnT[:], start=True, stop=True)\
        .then_inc(T.sem, T.hit(L, "pj"))
    yield
    pe.wait_ge(A.sem, A.at(L, "pjc"))
    pe.wait_ge(V.sem, V.at(L, "sq"))
    for t in range(TILES):
        tok = slice(t * P, (t + 1) * P)
        nc.tensor.matmul(S.bank(2)[:, 5 * t:5 * t + 4], S.scratch[0:32, tok], W(L, "sim")[0:32], start=True, stop=True)
        nc.tensor.matmul(S.bank(2)[:, 5 * t + 4:5 * t + 5], S.scratch[0:32, SEQ + t * P:][:, 0:P], K.ones[0:32, 0:1],
                         start=True, stop=True)
        ins = nc.tensor.matmul(S.misc[:, 15 * t:15 * t + 15], S.xnT[:, tok], W(L, "down"), start=True, stop=True)
    ins.then_inc(T.sem, T.hit(L, "lg"))
    yield
    pe.wait_ge(V.sem, V.at(L, "zs"))
    for t in range(TILES):
        ins = nc.tensor.transpose(S.bank(0)[0:15, t * P:(t + 1) * P], S.scratch[:, 1024 + 15 * t:1024 + 15 * t + 15],
                                  K.ident)
    ins.then_inc(T.sem, T.hit(L, "zT"))
    yield
    pe.wait_ge(A.sem, A.at(L, "zTc"))
    for t in range(TILES):
        tok = slice(t * P, (t + 1) * P)
        nc.tensor.matmul(S.bank(1)[:, tok], S.xnT[:, tok], W(L, "w"), start=True, stop=False)
        ins = nc.tensor.matmul(S.bank(1)[:, tok], S.scratch[0:15, 512 + t * P:][:, 0:P], W(L, "up")[0:15],
                               start=False, stop=True)
    ins.then_inc(T.sem, T.hit(L, "y"))
    yield


def l3f_scalar(nc, act, K, S, L, before):
    T, V, A, W = S.T, S.V, S.A, K.w
    act.wait_ge(T.sem, T.at(L, "pj"))
    nc.scalar.activation(S.scratch[0:32, 0:SEQ], S.bank(0)[0:32, 0:SEQ], ACT.Identity, bias=W(L, "bp")[0:32])\
        .then_inc(A.sem, A.hit(L, "pjc"))
    yield
    act.wait_ge(V.sem, V.at(L, "d"))
    nc.scalar.activation(S.top4[:, 1], S.top4[:, 0], ACT.Exp).then_inc(A.sem, A.hit(L, "ex"))
    yield
    act.wait_ge(T.sem, T.at(L, "zT"))
    nc.scalar.activation(S.scratch[0:15, 512:768], S.bank(0)[0:15, 0:SEQ], ACT.Copy).then_inc(A.sem, A.hit(L, "zTc"))
    yield
    yield


def l3f_vector(nc, dve, link, K, S, L, before):
    T, V, A = S.T, S.V, S.A
    dve.wait_ge(A.sem, A.at(L, "pjc"))
    nc.vector.tensor_tensor(S.scratch[0:32, SEQ:2 * SEQ], S.scratch[0:32, 0:SEQ], S.scratch[0:32, 0:SEQ], ALU.mult)\
        .then_inc(V.sem, V.hit(L, "sq"))
    yield
    dve.wait_ge(T.sem, T.at(L, "lg"))
    raw = S.bank(2)[:, 0:10].rearrange("p (t e) -> p t e", t=TILES)
    nc.vector.tensor_copy(S.small[:, 0:2], raw[:, :, 4]).then_inc(V.sem, V.hit(L, "ss"))
    lg, ex, eq = S.top4[:, 0], S.top4[:, 1], S.top4[:, 2]
    dve.wait_ge(S.G.sem, S.G.at(L, "nrm"))
    link(nc.vector.tensor_scalar(S.small[:, 4:6], S.small[:, 2:4], 1e-12, None, ALU.max))
    link(nc.vector.reciprocal(S.small[:, 6:8], S.small[:, 4:6]))
    link(nc.vector.tensor_tensor(lg, raw[:, :, 0:4], S.small[:, 6:8].unsqueeze(2).to_broadcast([P, 2, 4]), ALU.mult))
    link(nc.vector.tensor_tensor(lg, lg, K.route[:].unsqueeze(1).to_broadcast([P, 2, 4]), ALU.mult))
    link(nc.vector.tensor_reduce(S.small[:, 8:10], lg, X, ALU.max, negate=True))
    nc.vector.tensor_tensor(lg, lg, S.small[:, 8:10].unsqueeze(2).to_broadcast([P, 2, 4]), ALU.add)\
        .then_inc(V.sem, V.hit(L, "d"))
    dve.wait_ge(V.sem, V.at(L, "d"))
    link(nc.vector.tensor_scalar(eq, lg, 0.0, None, ALU.is_equal))
    first, seen = S.top4[:, 3], S.small[:, 10:12].unsqueeze(2)
    link(nc.vector.tensor_copy(first[:, :, 0:1], eq[:, :, 0:1]))
    link(nc.vector.tensor_copy(seen, eq[:, :, 0:1]))
    for e in range(1, 4):
        link(nc.vector.tensor_tensor(first[:, :, e:e + 1], eq[:, :, e:e + 1], seen, ALU.is_gt))
        link(nc.vector.tensor_tensor(seen, seen, eq[:, :, e:e + 1], ALU.max))
    dve.wait_ge(A.sem, A.at(L, "ex"))
    link(nc.vector.tensor_reduce(S.small[:, 12:14], ex, X, ALU.add))
    link(nc.vector.reciprocal(S.small[:, 14:16], S.small[:, 12:14]))
    link(nc.vector.tensor_tensor(first, first, ex, ALU.mult))
    link(nc.vector.tensor_tensor(first, first, S.small[:, 14:16].unsqueeze(2).to_broadcast([P, 2, 4]), ALU.mult))
    z = S.misc[:, 0:30].rearrange("p (t r) -> p t r", t=TILES)
    zs = S.scratch[:, 1024:1054].rearrange("p (t r) -> p t r", t=TILES)
    at = 0
    for e, r in enumerate(RANKS):
        ins = nc.vector.tensor_tensor(zs[:, :, at:at + r], z[:, :, at:at + r],
                                      first[:, :, e:e + 1].to_broadcast([P, 2, r]), ALU.mult)
        at += r
    ins.then_inc(V.sem, V.hit(L, "zs"))
    yield
    yield
    add_output(nc, dve, S, L, S.bank(1))
    yield


LAYER = {
    **{L: dict(tensor=mha_tensor, scalar=mha_scalar, vector=mha_vector, gpsimd=mha_gpsimd) for L in MHA},
    "L2a": dict(tensor=l2a_tensor, scalar=l2a_scalar, vector=l2a_vector, gpsimd=l2a_gpsimd),
    "L1a": dict(tensor=l1a_tensor, scalar=l1a_scalar, vector=l1a_vector, gpsimd=l1a_gpsimd),
    "L0f": dict(tensor=l0f_tensor, scalar=l0f_scalar, vector=l0f_vector, gpsimd=l0f_gpsimd),
    "L1f": dict(tensor=l1f_tensor, scalar=l1f_scalar, vector=l1f_vector, gpsimd=l1f_gpsimd),
    "L2x": dict(tensor=l2x_tensor, scalar=l2x_scalar, vector=l2x_vector, gpsimd=l2x_gpsimd),
    "L2f": dict(tensor=l2f_tensor, scalar=l2f_scalar, vector=l2f_vector, gpsimd=l2f_gpsimd),
    "L3f": dict(tensor=l3f_tensor, scalar=l3f_scalar, vector=l3f_vector, gpsimd=l3f_gpsimd),
}
PLAN = {**{L: mha_plan(L) for L in MHA}, "L2a": l2a_plan(), "L1a": L1A_PLAN, "L0f": L0F_PLAN, "L1f": L1F_PLAN, "L2x": L2X_PLAN,
        "L2f": L2F_PLAN, "L3f": L3F_PLAN}


class Shared:
    pass


def decoder(nc, x, ctx, ctx_t, mask_row, mask_col, weights, raw, sel2, upto, causal, out):
    where, spans, columns = weight_columns()
    with ExitStack() as stack:
        def sb(name, shape, dt=F32):
            return stack.enter_context(nc.sbuf_tensor(name, shape, dt))

        def sem(name):
            return stack.enter_context(nc.semaphore(name))

        K = Shared()
        weights_sb = sb("weights_sb", [P, columns])
        K.ones = sb("ones", [P, P])
        K.ones_bf = sb("ones_bf", [P, SEQ], BF16)
        K.causal = sb("causal", [P, TILES * SEQ], BF16)
        K.rows = {L: sb("rows_" + L, [P, 512], BF16) for L in (*MHA, "L2f")}
        K.ident_bf = sb("ident_bf", [P, P], BF16)[:, :]
        K.spread_bf = sb("spread_bf", [P, 512], BF16)
        K.ident_h = sb("ident_h", [P, P], F16)
        K.sel2 = sb("sel2", [P, 8, 64], BF16)
        K.upto = sb("upto", [P, TILES, SEQ], BF16)
        K.neg_half = sb("neg_half", [P, 2])
        K.neg_half3 = sb("neg_half3", [P, 3])
        K.half = sb("half", [P, 2])
        K.wv_1a = sb("wv_1a", [P, P])
        K.w1q = sb("w1q", [P, 512], BF16)
        K.w2q = sb("w2q", [P, 512], BF16)
        K.b1q = sb("b1q", [P, 4])
        K.b2q = sb("b2q", [P, P], BF16)
        K.route = sb("route", [P, 4])
        K.tmp, K.half4 = sb("tmp", [P, 8]), sb("half4", [P, 4])
        K.temp_cut, K.sim2, K.route_scale = sb("temp_cut", [P, 1]), sb("sim2", [P, 4]), sb("route_scale", [P, 1])
        x_sb = sb("x_sb", [P, STREAMS, TILES, P])
        weights_loaded = {g: sem("loaded_" + g) for g in LOAD_ORDER}

        def w(group, name):
            at, n = where[group, name]
            return weights_sb[:, at:at + n]

        def loaded(eng, group):
            eng.wait_ge(weights_loaded[group], 16)

        K.w, K.loaded = w, loaded
        K.ident = w("base", "ident")

        inputs_loaded, outputs_stored, setup_chain, setup_done = (
            sem("inputs_loaded"), sem("outputs_stored"), sem("setup_chain"), sem("setup_done"))
        consts_loaded, pool_ready, setup_tensor, setup_scalar, chain = (
            sem("consts_loaded"), sem("pool_ready"), sem("setup_tensor"), sem("setup_scalar"), sem("vector_chain"))

        streams = []
        for n in range(STREAMS):
            S = Stream()

            def tile(name, shape, dt=F32):
                return sb("%s_%d" % (name, n), shape, dt)

            S.x = x_sb[:, n]
            S.xn, S.xnT = tile("xn", [P, TILES, P]), tile("xnT", [P, SEQ])
            ops = tile("operands", [P, 2048], F16)
            S.qop, S.kop = ops[:, 0:1024], ops[:, 1024:2048]
            S.kop_bf = ops[:, 1024:2048].bitcast(BF16)
            ops32 = ops[:, :].bitcast(F32)
            S.wide = tile("wide", [P, 1024])
            S.e = tile("e", [P, 4, 512])
            S.ef = S.e[:, :, :].rearrange("p a b -> p (a b)")
            S.scratch = tile("scratch", [P, 2048])
            S.hi, S.hi_bf = S.scratch[:, 1536:2048].bitcast(F16), S.scratch[:, 1536:2048].bitcast(BF16)
            S.masked = S.scratch[:, 0:1024].rearrange("p (a b) -> p a b", a=2)
            S.on, S.oT = tile("on", [P, TILES, P]), tile("oT", [P, SEQ])
            S.xn2, S.xn2T = S.on, S.oT
            S.oT2_all = lambda t, a=ops32, b=S.ef: (a, b)[t][:, 0:1024]
            S.oT2 = lambda t, i, f=S.oT2_all: f(t)[:, i * P:(i + 1) * P]
            S.vaug, S.vstack = tile("vaug", [P, TILES, HEADS, HD + 1]), tile("vstack", [P, HEADS // 2, 2 * (HD + 1)])
            S.negm, S.negm2 = tile("negm", [P, TILES, QUADS, SLOTS]), tile("negm2", [P, TILES, 2, 8])
            S.nm, S.nm2 = tile("nm", [P, TILES, QUADS, P], F16), tile("nm2", [P, TILES, 2, 64], BF16)
            S.nmT = tile("nmT", [P, SEQ], BF16)
            S.rden, S.den = tile("rden", [P, TILES, HEADS]), tile("den", [P, TILES, HEADS])
            S.ctx, S.ctxT = tile("ctx", [KEYS, P]), tile("ctxT", [P, KEYS])
            S.cn, S.cnT, S.kT = tile("cn", [KEYS, P]), tile("cnT", [P, KEYS]), tile("kT", [P, KEYS])
            S.vpair = tile("vpair", [P, 130])
            S.mask_row_u8, S.mask_col_u8 = tile("mask_row_u8", [P, KEYS], U8), tile("mask_col_u8", [P, 1], U8)
            S.mask_row, S.mask_col = tile("mask_row", [P, KEYS], BF16), tile("mask_col", [P, 1])
            S.stats, S.mv = tile("stats", [P, 3, 6]), tile("mv", [P, 3, 2])
            S.var, S.rstd, S.var3, S.rstd3 = (tile("var", [P, 2]), tile("rstd", [P, 2]), tile("var3", [P, 3]),
                                              tile("rstd3", [P, 3]))
            S.small = tile("small", [P, 16])
            S.score, S.dist = tile("score", [P, TILES, EXPERTS]), tile("dist", [P, TILES, EXPERTS])
            S.sT, S.selT = S.scratch[:, 0:256], S.scratch[:, 256:512]
            S.work = S.scratch[:, 512:1024].rearrange("p (a b) -> p a b", a=2)
            S.rmT = S.nmT
            S.best, S.best8 = tile("best", [P, 8]), tile("best8", [P, TILES, 8])
            S.sel_bf, S.rank = tile("sel_bf", [P, TILES, EXPERTS], BF16), tile("rank", [P, TILES, EXPERTS])
            S.logit, S.gate_d, S.gate, S.kept = (tile(k, [P, TILES, MOE]) for k in ("logit", "gate_d", "gate", "kept"))
            S.top4 = tile("top4", [P, 4, TILES, 4])
            S.ps = stack.enter_context(nc.psum_tensor("ps_%d" % n, [P, 4 * BANK], F32))
            S.bank = lambda i, ps=S.ps: ps[:, i * BANK:(i + 1) * BANK]
            S.misc = S.bank(3)
            S.misc_bf, S.misc_h = S.misc.bitcast(BF16), S.misc.bitcast(F16)
            S.T, S.V, S.A, S.G = (Track(sem("%s_done_%d" % (k, n))) for k in ("tensor", "vector", "scalar", "gpsimd"))
            for kind, track in (("tensor", S.T), ("vector", S.V), ("scalar", S.A), ("gpsimd", S.G)):
                track.plan("start", NORM[kind])
                for L in LAYERS:
                    track.plan(L, PLAN[L][kind])
                    if L != LAYERS[-1]:
                        track.plan(L, NORM[kind])
            streams.append(S)

        setup(nc, K, streams, w, weights_sb, spans, weights_loaded, weights, raw, (sel2, upto, causal), consts_loaded,
              setup_chain, setup_tensor, setup_scalar, setup_done, pool_ready)

        steps = {}

        def run(kind, eng, link=None):
            def program(S):
                norm(S, "start", kind, eng, link)
                yield
                before = "start"
                for L in LAYERS:
                    count = 0
                    args = (nc, eng, link, K, S, L, before) if kind == "vector" else (nc, eng, K, S, L, before)
                    for _ in LAYER[L][kind](*args):
                        count += 1
                        yield
                    assert steps.setdefault(L, count) == count, (L, kind, count, steps[L])
                    before = L
                    if L != LAYERS[-1]:
                        norm(S, L, kind, eng, link)
                        yield

            programs = [program(S) for S in streams]
            live, k = [True] * STREAMS, 0
            while any(live):
                for n in range(STREAMS):
                    if live[n] and k >= n * OFFSET:
                        live[n] = next(programs[n], "end") != "end"
                k += 1
            for S in streams:
                track = dict(tensor=S.T, vector=S.V, scalar=S.A, gpsimd=S.G)[kind]
                assert track.reached == len(track.value), (kind, track.reached)

        def norm(S, L, kind, eng, link):
            if kind == "vector":
                if L != "start":
                    last = ("acc", MOE - 1) if L == "L2f" else ("x",)
                    eng.wait_ge(S.V.sem, S.V.at(L, *last))
                norm_vector(nc, eng, link, S, L)
            elif kind == "gpsimd":
                norm_gpsimd(nc, eng, K, S, L)
            elif kind == "tensor":
                norm_tensor(nc, eng, K, S, L)
            else:
                norm_scalar(nc, eng, S, L)

        with nc.Fori(0, ROUNDS) as r:
            with nc.Block() as block:
                @block.sync
                def _(sp):
                    sp.dma_start(x_sb[:], x[r]).then_inc(inputs_loaded, 16)
                    for n, S in enumerate(streams):
                        sp.dma_start(S.ctx[:], ctx[r * STREAMS + n]).then_inc(inputs_loaded, 16)
                        sp.dma_start(S.ctxT[:], ctx_t[r * STREAMS + n]).then_inc(inputs_loaded, 16)
                        sp.dma_start(S.mask_row_u8[:], mask_row[r * STREAMS + n]).then_inc(inputs_loaded, 16)
                        sp.dma_start(S.mask_col_u8[:], mask_col[r * STREAMS + n]).then_inc(inputs_loaded, 16)
                    for S in streams:
                        sp.wait_ge(S.V.sem, S.V.at(LAYERS[-1], "x"))
                    sp.dma_start(out[r], x_sb[:]).then_inc(outputs_stored, 16)
                    sp.wait_ge(outputs_stored, 16)

                @block.tensor
                def _(pe):
                    run("tensor", pe)

                @block.scalar
                def _(act):
                    run("scalar", act)

                @block.gpsimd
                def _(pool):
                    run("gpsimd", pool)

                @block.vector
                def _(dve):
                    links = [0]

                    def link(ins):
                        links[0] += 1
                        ins.then_inc(chain, 1)
                        dve.wait_ge(chain, links[0])

                    dve.wait_ge(inputs_loaded, 16 * (1 + 4 * STREAMS))
                    for S in streams:
                        link(nc.vector.tensor_scalar(S.mask_row[:], S.mask_row_u8[:], BIG, None, ALU.mult))
                        link(nc.vector.tensor_scalar(S.mask_col[:], S.mask_col_u8[:], BIG, None, ALU.mult))
                    run("vector", dve, link)

            for s in [inputs_loaded, outputs_stored, chain] + [t.sem for S in streams for t in (S.T, S.V, S.A, S.G)]:
                nc.gpsimd.sem_clear(s)
            nc.all_engine_barrier()


def setup(nc, K, streams, w, weights_sb, spans, weights_loaded, weights, raw, consts, consts_loaded,
          setup_chain, setup_tensor, setup_scalar, setup_done, pool_ready):
    early = ["base", "L3x", "L3f", "L2a"]
    raw_at = raw_columns()

    def raw_sb(*key):
        at, n = raw_at[key]
        return streams[at // RAW_HALF].scratch[:, at % RAW_HALF:at % RAW_HALF + n]

    with nc.Block() as block:
        @block.sync
        def _(sp):
            for g in LOAD_ORDER:
                a, b = spans[g]
                sp.dma_start(weights_sb[:, a:b], weights[:, a:b]).then_inc(weights_loaded[g], 16)
                if g == "base":
                    for dst, src in zip((K.sel2, K.upto, K.causal), consts):
                        sp.dma_start(dst[:], src).then_inc(consts_loaded, 16)
                    for n, S in enumerate(streams):
                        sp.dma_start(S.scratch[:], raw[:, n * RAW_HALF:(n + 1) * RAW_HALF]).then_inc(consts_loaded, 16)
            sp.wait_ge(consts_loaded, 16 * (3 + STREAMS))

        @block.gpsimd
        def _(pool):
            nc.gpsimd.memset(K.neg_half[:], -0.5)
            nc.gpsimd.memset(K.neg_half3[:], -0.5)
            nc.gpsimd.memset(K.half[:], 0.5)
            nc.gpsimd.memset(K.half4[:], 0.5).then_inc(pool_ready, 1)
            for S in streams:
                nc.gpsimd.memset(S.nm[:], 0.0)
                nc.gpsimd.memset(S.nm2[:], 0.0)
                nc.gpsimd.memset(S.wide[:], 0.0).then_inc(pool_ready, 1)
                nc.gpsimd.memset(S.vaug[:], 1.0)
                nc.gpsimd.memset(S.mv[:], 1.0)
            pool.wait_ge(pool_ready, 1 + STREAMS)
            K.loaded(pool, MHA_ORDER[0])
            for S in streams:
                widen(nc, pool, K, S, MHA_ORDER[0])
            pool.wait_ge(setup_done, 1)
            nc.gpsimd.tensor_tensor(K.tmp[:, 4:8], K.tmp[:, 0:4], K.half4[:], ALU.pow).then_inc(setup_done, 1)

        @block.tensor
        def _(pe):
            pe.wait_ge(consts_loaded, 16 * (3 + STREAMS))
            nc.tensor.matmul(streams[0].bank(0)[:, 0:P], raw_sb("L1a", "vdown")[0:32], raw_sb("L1a", "vup")[0:32],
                             start=True, stop=True).then_inc(setup_tensor, 1)
            pe.wait_ge(setup_chain, 3 + 6 * STREAMS)
            nc.tensor.matmul(streams[0].bank(1)[:, 0:4], K.ones[0:32, 0:P], K.sim2[0:32], start=True, stop=True)\
                .then_inc(setup_tensor, 1)

        @block.scalar
        def _(act):
            K.loaded(act, "L3f")
            act.wait_ge(setup_chain, 2 + 6 * STREAMS)
            nc.scalar.activation(K.route_scale[:], K.temp_cut[:], ACT.Exp).then_inc(setup_scalar, 1)

        @block.vector
        def _(dve):
            links = [0]

            def link(ins):
                links[0] += 1
                ins.then_inc(setup_chain, 1)
                dve.wait_ge(setup_chain, links[0])

            for g in early:
                K.loaded(dve, g)
            link(nc.vector.memset(K.ones[:], 1.0))
            for S in streams:
                link(nc.vector.memset(S.vstack[:], 0.0))
                for half in range(2):
                    link(nc.vector.memset(S.vstack[64 * half:64 * half + 64, :, 9 * half + HD:9 * half + HD + 1], 1.0))
                link(nc.vector.memset(S.vpair[:], 0.0))
                link(nc.vector.memset(S.vpair[0:64, 64:65], 1.0))
                link(nc.vector.memset(S.vpair[64:128, 129:130], 1.0))
            link(nc.vector.tensor_scalar(K.temp_cut[:], w("L3f", "temp"), HOTTEST, None, ALU.min))
            link(nc.vector.tensor_tensor(K.sim2[0:32], w("L3f", "sim")[0:32], w("L3f", "sim")[0:32], ALU.mult))
            dve.wait_ge(setup_tensor, 2)
            nc.vector.tensor_copy(K.tmp[:, 0:4], streams[0].bank(1)[:, 0:4]).then_inc(setup_done, 1)
            dve.wait_ge(setup_done, 2)
            link(nc.vector.tensor_scalar(K.tmp[:, 0:4], K.tmp[:, 4:8], 1e-12, None, ALU.max))
            link(nc.vector.reciprocal(K.tmp[:, 4:8], K.tmp[:, 0:4]))
            dve.wait_ge(setup_scalar, 1)
            link(nc.vector.tensor_scalar(K.route[:], K.tmp[:, 4:8], K.route_scale[:, 0:1], None, ALU.mult))
            link(nc.vector.tensor_copy(K.wv_1a[:], streams[0].bank(0)[:, 0:P]))
            link(nc.vector.tensor_scalar(w("L3x", "wq"), w("L3x", "wq"), w("L3x", "scale"), None, ALU.mult))
            dve.wait_ge(consts_loaded, 16 * (3 + STREAMS))
            for a in (w("L2a", "wq"), raw_sb("L2a", "rows")[0:3, 0:P]):
                link(nc.vector.tensor_scalar(a, a, HD ** -0.5, None, ALU.mult))
            link(nc.vector.tensor_scalar(raw_sb("L3x", "rows")[0:3, 0:P], raw_sb("L3x", "rows")[0:3, 0:P],
                                         w("L3x", "scale")[0:3], None, ALU.mult))
            for L in (*MHA, "L2f"):
                src = raw_sb(L, "rows")
                n = src.shape[1]
                part, rest, total = (streams[0].ef[:, i * 512:i * 512 + n] for i in range(3))
                bf = streams[1].ef[:, 0:256].bitcast(BF16)[:, 0:n]
                link(nc.vector.tensor_copy(rest, src))
                for i in range(3):
                    link(nc.vector.tensor_copy(bf, rest))
                    link(nc.vector.tensor_copy(part, bf))
                    link(nc.vector.tensor_tensor(rest, rest, part, ALU.subtract))
                    if i == 0:
                        link(nc.vector.tensor_scalar(total, part, w("base", "part")[:, 0:1], None, ALU.mult))
                    else:
                        link(nc.vector.scalar_tensor_tensor(total, part, w("base", "part")[:, i:i + 1], total,
                                                            ALU.mult, ALU.add))
                if L == "L2f":
                    link(nc.vector.tensor_copy(K.rows[L][:], total))
                    continue
                for p in (0, 32):
                    copies = K.rows[L][p:p + 3].rearrange("p (h r d) -> p h r d", r=4, d=HD)
                    link(nc.vector.memset(copies[:, :, 3], 0.0))
                    link(nc.vector.tensor_copy(
                        copies[:, :, 0:3], total[p:p + 3, 0:P].rearrange("p (h d) -> p h d", d=HD).unsqueeze(2)
                        .to_broadcast([3, HEADS, 3, HD])))
                link(nc.vector.memset(copies[0:1, :, 3, 0:2], GUARD))
                link(nc.vector.tensor_copy(K.rows[L][64:67, 0:256], total[64:67]))
            for src, dst, n, part, factor in (("w1", K.w1q, 512, P, 1.0), ("w2", K.w2q, 512, P, 1.0),
                                              ("b1", K.b1q, 4, P, 0.25), ("b2", K.b2q, P, 1, 16.0)):
                a, b = streams[0].ef[0:part, 0:n], streams[0].ef[0:part, 1024:1024 + n]
                link(nc.vector.tensor_scalar(a, raw_sb("L1f", src)[0:part], 64.0, 127.0, ALU.mult, ALU.min))
                link(nc.vector.tensor_scalar(b, a, -128.0, ROUND, ALU.max, ALU.add))
                link(nc.vector.tensor_scalar(dst[0:part], b, -ROUND, factor, ALU.add, ALU.mult))
            link(nc.vector.memset(K.ones_bf[:], 1.0))
            link(nc.vector.tensor_copy(K.ident_bf[:], K.ident))
            link(nc.vector.tensor_copy(K.ident_h[:], K.ident))
            link(nc.vector.tensor_copy(K.spread_bf[:], w("base", "spread")))


def packed_weights(v, np):
    where, _, columns = weight_columns()
    raw_at = raw_columns()
    out, raw = np.zeros((P, columns), np.float32), np.zeros((P, 2 * RAW_HALF), np.float32)

    def put(group, name, a, row=0, col=0):
        a = np.asarray(a)
        to, at = (out, where[group, name]) if (group, name) in where else (raw, raw_at[group, name])
        to[row:row + a.shape[0], at[0] + col:at[0] + col + a.shape[1]] = a

    put("base", "ident", np.eye(P))
    rep = (np.arange(P) // HD) % 4
    put("base", "lo_q", -(rep == 1).astype(np.float32)[:, None])
    put("base", "lo_k", -(rep == 2).astype(np.float32)[:, None])
    put("base", "slot", (np.arange(P) % CAP + 1)[:, None])
    i64 = np.arange(64)
    put("base", "mask_qk", np.where(i64[None, :] > i64[:, None], BIG, 0.0))
    put("base", "mask_kq", np.where((np.arange(P) % 64)[:, None] > i64[None, :], BIG, 0.0))
    for n in range(3):
        put("base", "part", (np.arange(P) % 32 == n)[:, None], col=n)
    put("base", "count", np.tile(np.arange(1, CAP + 1), (P, 1)))
    cols = np.arange(512)
    put("base", "spread", np.arange(EXPERTS)[:, None] == (cols // CAP)[None, :])

    def mha(L, wq, wk, wv, wo, bq=None, bk=None, bv=None, bo=None):
        for name, a in (("wq", wq), ("wk", wk), ("wv", wv), ("wo", wo)):
            put(L, name, a)
        for a, row, col in ((bq, 0, 0), (bk, 32, 0), (bv, 64, 0), (bo, 64, P)):
            if a is not None:
                put(L, "rows", np.broadcast_to(a.reshape(1, P), (3, P)), row, col)

    w, b = v["L0_attn_w_in"], v["L0_attn_b_in"]
    mha("L0a", w[0:P].T, w[P:2 * P].T, w[2 * P:].T, v["L0_attn_w_out"].T, b[0:P], b[P:2 * P], b[2 * P:], v["L0_attn_b_out"])
    q = {k: v["L0_xattn_W" + k].transpose(1, 0, 2).reshape(P, P) for k in "qkv"}
    mha("L0x", q["q"], q["k"], q["v"], v["L0_xattn_Wo"].T, v["L0_xattn_bq"], v["L0_xattn_bk"], v["L0_xattn_bv"],
        v["L0_xattn_bo"])
    w, b = v["L1_xattn_Wkv"], v["L1_xattn_bkv"]
    mha("L1x", v["L1_xattn_Wq"], w[:, 0:P], w[:, P:], v["L1_xattn_Wout"], v["L1_xattn_bq"], b[0:P], b[P:],
        v["L1_xattn_bout"])
    w = v["L2_attn_w_in"].reshape(HEADS, 3, HD, P).transpose(1, 3, 0, 2).reshape(3, P, P)
    b = v["L2_attn_b_in"].reshape(HEADS, 3, HD).transpose(1, 0, 2).reshape(3, P)
    mha("L2a", w[0], w[1], w[2], v["L2_attn_w_out"].T, b[0], b[1], b[2], v["L2_attn_b_out"])
    mha("L3a", v["L3_attn_Wq"].T, v["L3_attn_Wk"].T, v["L3_attn_Wv"].T, v["L3_attn_Wo"].T, bo=v["L3_attn_bo"])
    mha("L3x", v["L3_xattn_Wq"].T, v["L3_xattn_Wk"].T, v["L3_xattn_Wv"].T, v["L3_xattn_Wp"].T, v["L3_xattn_bq"],
        v["L3_xattn_bk"], v["L3_xattn_bv"], v["L3_xattn_bp"])
    put("L3x", "scale", np.broadcast_to(v["L3_xattn_scale"], (P, 1)))

    def halves(a):
        return a.reshape(-1, P, a.shape[1]).transpose(1, 0, 2).reshape(P, -1)

    put("L0f", "gate", v["L0_ffn_gate_w"].T)
    put("L0f", "wg", v["L0_ffn_Wg"].transpose(2, 0, 1).reshape(P, -1))
    put("L0f", "wu", v["L0_ffn_Wu"].transpose(2, 0, 1).reshape(P, -1))
    put("L0f", "wd", halves(v["L0_ffn_Wd"].transpose(0, 2, 1).reshape(-1, P)))
    put("L0f", "sg", v["L0_ffn_Ws_g"].T)
    put("L0f", "su", v["L0_ffn_Ws_u"].T)
    put("L0f", "sd", halves(v["L0_ffn_Ws_d"].T))
    put("L1a", "wq", v["L1_attn_Wq"])
    put("L1a", "wk", v["L1_attn_Wk"])
    put("L1a", "vdown", v["L1_attn_Wvdown"].T)
    put("L1a", "vup", v["L1_attn_Wvup"])
    put("L1f", "w1", v["L1_ffn_w1"].T)
    put("L1f", "w2", halves(v["L1_ffn_w2"].T))
    put("L1f", "b1", v["L1_ffn_b1"].reshape(4, P).T)
    put("L1f", "b2", v["L1_ffn_b2"].reshape(1, P))
    put("L2x", "wq", v["L2_xattn_Wq"])
    kv = v["L2_xattn_Wkv"]
    put("L2x", "wk", kv[:, 0:64])
    put("L2x", "wk", kv[:, 0:64], col=64)
    put("L2x", "wv", kv[:, 64:128])
    put("L2x", "wo", halves(v["L2_xattn_Wo"]))
    put("L2x", "w1", v["L2_xattn_Wff1"])
    put("L2x", "w2", halves(v["L2_xattn_Wff2"]))
    for name, key in (("lg", "ln_g"), ("lb", "ln_b"), ("cg", "cln_g"), ("cb", "cln_b")):
        put("L2x", name, v["L2_xattn_" + key].reshape(P, 1))
    put("L2f", "w1", v["L2_ffn_W1"].transpose(1, 0, 2).reshape(P, -1))
    put("L2f", "w2", halves(v["L2_ffn_W2"].reshape(-1, P)))
    put("L2f", "b1", v["L2_ffn_b1"].reshape(MOE, MOE_C, P).transpose(2, 0, 1).reshape(P, -1))
    put("L2f", "wr", v["L2_ffn_Wr"])
    for e in range(MOE):
        put("L2f", "rows", np.broadcast_to(v["L2_ffn_b2"][e:e + 1], (3, P)), row=32 * (e // 4), col=e % 4 * P)
    put("L2f", "rows", np.broadcast_to(v["L2_ffn_br"].reshape(1, MOE), (3, MOE)), row=96)
    put("L3f", "w", v["L3_ffn_W"].T)
    put("L3f", "wp", v["L3_ffn_Wp"].T)
    put("L3f", "bp", v["L3_ffn_bp"].reshape(32, 1))
    put("L3f", "sim", v["L3_ffn_sim"])
    put("L3f", "temp", np.broadcast_to(v["L3_ffn_temp"], (P, 1)))
    at = 0
    for e, r in enumerate(RANKS):
        put("L3f", "down", v["L3_ffn_Wd%d" % e].T, col=at)
        put("L3f", "up", v["L3_ffn_Wu%d" % e].T, row=at)
        at += r
    return out, raw


def kernel(**inputs):
    import ml_dtypes as _ml
    import numpy as _np
    import concourse.bacc as _bacc
    from concourse import mybir as _mybir
    from concourse.bass_utils import run_bass_kernel_spmd as _run

    v = {k: _np.asarray(a) for k, a in inputs.items()}
    x = v["x"].reshape(ROUNDS, STREAMS, 64, TILES, 2, D).transpose(0, 4, 2, 1, 3, 5).reshape(ROUNDS, P, STREAMS, TILES, D)
    ctx = v["ctx_1024"]
    mask = v["mask_BxS2_bf0"]
    part = _np.arange(P)
    sel2 = _np.zeros((P, 8, 64), _ml.bfloat16)
    for a in range(8):
        sel2[(part % 64 == a) | (part % 64 == 8 + a), a] = 1
    upto = (_np.arange(SEQ).reshape(TILES, P).T[:, :, None] <= _np.arange(SEQ)).astype(_ml.bfloat16)
    order = _np.array([4 * i + r for r in range(4) for i in range(64)])
    causal = (order.reshape(TILES, P).T[:, :, None] >= order).astype(_ml.bfloat16).reshape(P, TILES * SEQ)
    weights, raw = packed_weights(v, _np)
    arrays = {
        "x": x, "ctx": ctx, "ctx_t": ctx.transpose(0, 2, 1), "mask_row": _np.broadcast_to(mask[:, None], (BATCH, P, KEYS)),
        "mask_col": _np.concatenate([mask, mask], 1)[:, :, None], "weights": weights, "raw": raw, "sel2": sel2, "upto": upto,
        "causal": causal,
    }
    nc = _bacc.Bacc("TRN2", target_bir_lowering=False, num_devices=1)
    arrays = {"in_" + k: _np.ascontiguousarray(a) for k, a in arrays.items()}
    args = [nc.dram_tensor(k, a.shape, _mybir.dt.from_np(a.dtype), kind="ExternalInput").ap() for k, a in arrays.items()]
    out = nc.dram_tensor("out_x", x.shape, _mybir.dt.float32, kind="ExternalOutput").ap()
    decoder(nc, *args, out)
    y = _run(nc, [arrays], core_ids=[0]).results[0]["out_x"]
    y = y.reshape(ROUNDS, 2, 64, STREAMS, TILES, D).transpose(0, 3, 2, 4, 1, 5)
    return _np.ascontiguousarray(y.reshape(BATCH, SEQ, D))
```

```python
from contextlib import ExitStack

import concourse.bass as bass
from concourse import mybir

F32 = mybir.dt.float32
F16 = mybir.dt.float16
BF16 = mybir.dt.bfloat16
U8 = mybir.dt.uint8
ACT = mybir.ActivationFunctionType
ALU = mybir.AluOpType
X = mybir.AxisListType.X

P = 128
BATCH, SEQ, D = 16, 256, 128
KEYS = 64
STREAMS = 2
ROUNDS = BATCH // STREAMS
TILES = SEQ // P
BANK = 512
HEADS, HD = 16, 8
QUADS, SLOTS = 4, 4
EXPERTS, CAP, EXP_F = 16, 32, 256
MOE, MOE_H, MOE_C = 8, 512, 4
BIG = -1e30
LOWEST = -3.4028234663852886e38
ROUND = 12582912.0
EPS = 1e-5
HOTTEST = 4.605170185988092
GUARD = 64.0
OFFSET = 8

MHA = {
    "L0a": dict(nq=64, nk=64, ctx=False),
    "L0x": dict(nq=SEQ, nk=KEYS, ctx=True),
    "L1x": dict(nq=SEQ, nk=KEYS, ctx=True),
    "L2a": dict(nq=SEQ, nk=SEQ, ctx=False),
    "L3a": dict(nq=SEQ, nk=SEQ, ctx=False),
    "L3x": dict(nq=SEQ, nk=KEYS, ctx=True),
}
MHA_ORDER = list(MHA)
BIASED = ("L0a", "L0x", "L1x", "L2a", "L3x")
LAYERS = ["L0a", "L0x", "L0f", "L1a", "L1x", "L1f", "L2a", "L2x", "L2f", "L3a", "L3x", "L3f"]

GROUPS = {
    "base": [("ident", 128), ("lo_q", 1), ("lo_k", 1), ("slot", 1), ("part", 3), ("mask_qk", 64), ("mask_kq", 64),
             ("count", 32), ("spread", 512)],
    **{k: [("wq", 128), ("wk", 128), ("wv", 128), ("wo", 128), ("scale", 1)] for k in MHA},
    "L0f": [("gate", EXPERTS), ("wg", EXPERTS * EXP_F), ("wu", EXPERTS * EXP_F), ("wd", EXPERTS * 256),
            ("sg", EXP_F), ("su", EXP_F), ("sd", 256)],
    "L1a": [("wq", 32), ("wk", 32)],
    "L2x": [("wq", 1024), ("wk", 128), ("wv", 64), ("wo", 1024), ("w1", 1024), ("w2", 512),
            ("lg", 1), ("lb", 1), ("cg", 1), ("cb", 1)],
    "L2f": [("w1", MOE * MOE_H), ("w2", MOE * MOE_H), ("b1", MOE * MOE_C), ("wr", MOE)],
    "L3f": [("w", 128), ("wp", 32), ("bp", 1), ("sim", 4), ("temp", 1), ("down", 15), ("up", 128)],
}
RAW = {
    **{(k, "rows"): 256 for k in MHA},
    ("L2f", "rows"): 512,
    ("L1f", "w1"): 512, ("L1f", "w2"): 512, ("L1f", "b1"): 4, ("L1f", "b2"): 128,
    ("L1a", "vdown"): 128, ("L1a", "vup"): 128,
}
RAW_HALF = 2048
LOAD_ORDER = ["base", "L3x", "L3f", "L2a", "L0a", "L0x", "L0f", "L1a", "L1x", "L2x", "L2f", "L3a"]


def weight_columns():
    at, where, spans = 0, {}, {}
    for group in LOAD_ORDER:
        start = at
        for name, n in GROUPS[group]:
            where[group, name] = (at, n)
            at += n
        spans[group] = (start, at)
    return where, spans, at


def raw_columns():
    where, at = {}, 0
    for key, n in RAW.items():
        if at < RAW_HALF < at + n:
            at = RAW_HALF
        where[key] = (at, n)
        at += n
    assert at <= 2 * RAW_HALF
    return where


class Track:

    def __init__(self, sem):
        self.sem, self.value, self.reached = sem, {}, 0

    def plan(self, layer, names):
        for name in names:
            key = (layer,) + (name if isinstance(name, tuple) else (name,))
            assert key not in self.value, key
            self.value[key] = len(self.value) + 1

    def at(self, *key):
        return self.value[key]

    def hit(self, *key):
        self.reached += 1
        assert self.value[key] == self.reached, (key, self.value[key], self.reached)
        return 1


class Stream:
    pass


NORM_STEPS = 4
NORM = dict(vector=["var", "xn"], gpsimd=["rstd"], tensor=["xT"], scalar=["xnT"])


def norm_vector(nc, dve, link, S, L):
    for t in range(TILES):
        ins = nc.vector.bn_stats(S.stats[:, t], S.x[:, t])
    link(ins)
    for t in range(TILES):
        ins = nc.vector.bn_aggr(S.mv[:, t], S.stats[:, t])
    link(ins)
    nc.vector.tensor_scalar(S.var[:], S.mv[:, 0:TILES, 1], EPS, None, ALU.add).then_inc(S.V.sem, S.V.hit(L, "var"))
    yield
    dve.wait_ge(S.G.sem, S.G.at(L, "rstd"))
    for t in range(TILES):
        ins = nc.vector.tensor_scalar(S.xn[:, t], S.x[:, t], S.mv[:, t, 0:1], S.rstd[:, t:t + 1],
                                      ALU.subtract, ALU.mult)
    ins.then_inc(S.V.sem, S.V.hit(L, "xn"))
    yield
    yield
    yield


def norm_gpsimd(nc, pool, K, S, L):
    pool.wait_ge(S.V.sem, S.V.at(L, "var"))
    nc.gpsimd.tensor_tensor(S.rstd[:], S.var[:], K.neg_half[:], ALU.pow).then_inc(S.G.sem, S.G.hit(L, "rstd"))
    for _ in range(NORM_STEPS):
        yield


def norm_tensor(nc, pe, K, S, L):
    yield
    yield
    pe.wait_ge(S.V.sem, S.V.at(L, "xn"))
    for t in range(TILES):
        ins = nc.tensor.transpose(S.bank(2)[:, t * P:(t + 1) * P], S.xn[:, t], K.ident)
    ins.then_inc(S.T.sem, S.T.hit(L, "xT"))
    yield
    yield


def norm_scalar(nc, act, S, L):
    yield
    yield
    yield
    act.wait_ge(S.T.sem, S.T.at(L, "xT"))
    nc.scalar.activation(S.xnT[:], S.bank(2)[:, 0:SEQ], ACT.Copy).then_inc(S.A.sem, S.A.hit(L, "xnT"))
    yield


def first_units(c):
    tiles = max(1, c["nq"] // P)
    blocks = [(t, g) for t in range(tiles) for g in range(QUADS)]
    per = min(BANK // c["nk"], len(blocks))
    return [(j, blocks[a:a + per]) for a in range(0, len(blocks), per) for j in range(SLOTS)]


def second_units(c):
    if c["nk"] == 64:
        return [(j, list(range(QUADS)), 0) for j in range(SLOTS)]
    per = min(BANK // c["nq"], QUADS)
    return [(j, list(range(a, a + per)), k) for a in range(0, QUADS, per) for j in range(SLOTS)
            for k in range(max(1, c["nk"] // P))]


SECOND_BANKS = 2


def mha_plan(L):
    c = MHA[L]
    u1, u2 = len(first_units(c)), len(second_units(c))
    sets = u2 // max(1, c["nk"] // P)
    causal = L == "L0a"
    masked1 = [("sum", u) if part == 0 else ("max", u) for u in range(u1) for part in ((0, 1) if causal else (1,))]
    return dict(
        vector=["qop", "kop", "vaug"] + masked1 + ["negm", "qmax"] + [k for u in range(u2) for k in ([("masked", u)] if causal else []) + [("rest", u)]]
        + ["on", "x"],
        scalar=["qh", "kh"] + [("e", u) for u in range(u2)] + ["oTc"],
        tensor=["q", "k", "v"] + [("s1", u) for u in range(u1)] + ["mT"]
        + second_order(c, lambda u: ("s2", u), lambda n: ("pv", n)) + ["oT", "y"],
        gpsimd=["wide"])


def second_order(c, score, value):
    units, tiles = len(second_units(c)), max(1, c["nk"] // P)
    out = []
    for n in range(units // tiles):
        out += [score(n * tiles + k) for k in range(tiles)]
        if n:
            out.append(value(n - 1))
    return out + [value(units // tiles - 1)]


def project(nc, pe, K, S, L, before):
    c = MHA[L]
    T, V, A, W = S.T, S.V, S.A, K.w
    nq, nk, ps = c["nq"], c["nk"], S.ps
    kt = max(1, nk // P)
    src = S.ctxT if c["ctx"] else S.xnT
    wq, wk, rows = S.wide[:, 0:512], S.wide[:, 512:1024], K.rows[L]
    K.loaded(pe, L)
    if L != MHA_ORDER[0]:
        pe.wait_ge(S.G.sem, S.G.at(MHA_ORDER[MHA_ORDER.index(L) - 1], "wide"))
    pe.wait_ge(A.sem, A.at(before, "xnT"))
    for name, w, part, act_in, n in (("q", wq, 0, S.xnT, nq), ("k", wk, 32, src, nk)):
        biased = L in BIASED or name == "k"
        for g in range(QUADS):
            out = ps[:, (0 if name == "q" else 2) * BANK + g * n:][:, 0:n]
            ins = nc.tensor.matmul(out, w[:, g * P:(g + 1) * P], act_in[:, 0:n], start=True, stop=not biased)
            if biased:
                ins = nc.tensor.matmul(out, rows[part:part + 3, g * P:(g + 1) * P], K.ones_bf[part:part + 3, 0:n],
                                       start=False, stop=True)
        ins.then_inc(T.sem, T.hit(L, name))
    yield
    yield
    yield
    pe.wait_ge(V.sem, V.at(L, "kop"))
    if nk == 64:
        for half in range(2):
            out = S.misc[64 * half:64 * half + 64, 0:64].rearrange("p (i c) -> p i c", i=2)
            cols = lambda a: a.rearrange("p (i b c) -> p b i c", i=2, b=2)[:, half]
            ins = nc.tensor.matmul(out, src[:, 0:64], cols(W(L, "wv")), start=True, stop=L not in BIASED)
            if L in BIASED:
                ins = nc.tensor.matmul(out, K.ones_bf[64:67, 0:64], cols(rows[64:67, 0:P]), start=False, stop=True)
    for k in range(kt) if nk > 64 else ():
        out = S.misc[:, k * P:(k + 1) * P]
        ins = nc.tensor.matmul(out, src[:, k * P:(k + 1) * P], W(L, "wv"), start=True, stop=L not in BIASED)
        if L in BIASED:
            ins = nc.tensor.matmul(out, K.ones_bf[64:67, 0:P], rows[64:67, 0:P], start=False, stop=True)
    ins.then_inc(T.sem, T.hit(L, "v"))


def output(nc, pe, K, S, L):
    c = MHA[L]
    T, V, A = S.T, S.V, S.A
    qt, mq, rows = max(1, c["nq"] // P), min(c["nq"], P), K.rows[L]
    yield
    yield
    pe.wait_ge(V.sem, V.at(L, "on"))
    for t in range(qt):
        ins = nc.tensor.transpose(S.bank(0)[:, t * P:t * P + mq], S.on[0:mq, t], K.ident[0:mq, 0:mq])
    ins.then_inc(T.sem, T.hit(L, "oT"))
    yield
    yield
    pe.wait_ge(A.sem, A.at(L, "oTc"))
    for t in range(qt):
        out = S.bank(1)[0:mq, t * P:(t + 1) * P]
        nc.tensor.matmul(out, S.oT[:, t * P:t * P + mq], K.w(L, "wo"), start=True, stop=False)
        ins = nc.tensor.matmul(out, K.ones_bf[64:67, 0:mq], rows[64:67, P:2 * P], start=False, stop=True)
    ins.then_inc(T.sem, T.hit(L, "y"))
    yield
    yield


def high_parts(nc, act, S, L):
    c = MHA[L]
    T, V, A = S.T, S.V, S.A
    nq, nk = c["nq"], c["nk"]
    yield
    act.wait_ge(T.sem, T.at(L, "q"))
    nc.scalar.activation(S.hi[:, 0:4 * nq], S.ps[:, 0:4 * nq], ACT.Copy).then_inc(A.sem, A.hit(L, "qh"))
    act.wait_ge(T.sem, T.at(L, "k"))
    nc.scalar.activation(S.hi_k[:, 0:4 * nk], S.ps[:, 2 * BANK:2 * BANK + 4 * nk], ACT.Copy)\
        .then_inc(A.sem, A.hit(L, "kh"))
    yield
    yield


def operands(nc, dve, K, S, L):
    c = MHA[L]
    nq, nk = c["nq"], c["nk"]
    V, A = S.V, S.A
    yield
    yield
    dve.wait_ge(A.sem, A.at(L, "qh"))
    nc.vector.scalar_tensor_tensor(S.qop[:, 0:4 * nq], S.hi[:, 0:4 * nq], K.w("base", "lo_q"),
                                   S.ps[:, 0:4 * nq], ALU.mult, ALU.add).then_inc(V.sem, V.hit(L, "qop"))
    dve.wait_ge(A.sem, A.at(L, "kh"))
    nc.vector.scalar_tensor_tensor(S.kop[:, 0:4 * nk], S.hi_k[:, 0:4 * nk], K.w("base", "lo_k"),
                                   S.ps[:, 2 * BANK:2 * BANK + 4 * nk], ALU.mult, ALU.add)\
        .then_inc(V.sem, V.hit(L, "kop"))
    yield


def output_turned(nc, act, S, L):
    nq = MHA[L]["nq"]
    yield
    yield
    yield
    act.wait_ge(S.T.sem, S.T.at(L, "oT"))
    nc.scalar.activation(S.oT[:, 0:nq], S.bank(0)[:, 0:nq], ACT.Copy).then_inc(S.A.sem, S.A.hit(L, "oTc"))
    yield
    yield
    yield


def mha_tensor(nc, pe, K, S, L, before):
    c = MHA[L]
    T, V, A, W = S.T, S.V, S.A, K.w
    nq, nk, ps = c["nq"], c["nk"], S.ps
    qt, kt, mq, mk = max(1, nq // P), max(1, nk // P), min(nq, P), min(nk, P)
    src = S.ctxT if c["ctx"] else S.xnT
    yield from project(nc, pe, K, S, L, before)
    for u, (j, blocks) in enumerate(first_units(c)):
        bank, r = S.bank(u % 3), slice(32 * j, 32 * j + 32)
        if u >= 3:
            pe.wait_ge(V.sem, V.at(L, "max", u - 3))
        for n, (t, g) in enumerate(blocks):
            out = bank[0:mq, n * nk:(n + 1) * nk]
            ins = nc.tensor.matmul(out, S.qop[r, g * nq + t * P:][:, 0:mq], S.kop[r, g * nk:(g + 1) * nk],
                                   start=True, stop=L != "L1x")
            if L == "L1x":
                ins = nc.tensor.matmul(out, K.ones_bf[r.start:r.start + 1, 0:mq], S.mask_row[r.start:r.start + 1, :],
                                       start=False, stop=True)
        ins.then_inc(T.sem, T.hit(L, "s1", u))
        if u % 2 == 1:
            yield
    yield
    pe.wait_ge(V.sem, V.at(L, "negm"))
    for t in range(qt):
        for g in range(QUADS):
            ins = nc.tensor.transpose(S.misc_h[:, g * nq + t * P:][:, 0:mq], S.nm[0:mq, t, g], K.ident_h[0:mq, 0:mq])
    ins.then_inc(T.sem, T.hit(L, "mT"))
    yield
    yield
    units, banks = second_units(c), SECOND_BANKS

    def score(u):
        j, groups, k = units[u]
        bank, r = S.bank(u % banks), slice(32 * j, 32 * j + 32)
        if u < banks:
            pe.wait_ge(V.sem, V.at(L, "qmax"))
        elif L == "L0a":
            pe.wait_ge(V.sem, V.at(L, "masked", u - banks))
        else:
            pe.wait_ge(A.sem, A.at(L, "e", u - banks))
        for n, g in enumerate(groups):
            if nk == 64:
                out = bank[64 * (g % 2):64 * (g % 2) + 64, g // 2 * nq:(g // 2 + 1) * nq]
            else:
                out = bank[:, n * nq:(n + 1) * nq]
            ins = nc.tensor.matmul(out, S.kop[r, g * nk + k * P:][:, 0:mk], S.qop[r, g * nq:(g + 1) * nq],
                                   start=True, stop=True)
        ins.then_inc(T.sem, T.hit(L, "s2", u))

    def value(n):
        j, groups, _ = units[n * kt]
        pe.wait_ge(V.sem, V.at(L, "rest", n * kt + kt - 1))
        for i in range(2):
            for t in range(qt):
                if nk == 64:
                    out = S.ps[0:mq, (2 + t) * BANK + (8 * i + j) * 18:][:, 0:144]\
                        .rearrange("p (b d) -> p b d", b=2)[:, :, 0:18]
                else:
                    out = S.ps[:, (2 + t) * BANK + (4 * groups[i] + j) * 18:][:, 0:18]
                for k in range(kt):
                    values = (S.vstack[:, 4 * i + j].rearrange("p (b d) -> p b d", b=2) if nk == 64
                              else S.vaug[:, k, 4 * groups[i] + j])
                    for part in range(2):
                        e = S.e_pair[:, (n * kt + k) % 4, part, i * nq + t * P:][:, 0:mq]
                        ins = nc.tensor.matmul(out, e, values, start=k == 0 and part == 0,
                                               stop=k == kt - 1 and part == 1)
        ins.then_inc(T.sem, T.hit(L, "pv", n))

    for n in range(len(units) // kt):
        for k in range(kt):
            score(n * kt + k)
        if n:
            value(n - 1)
        yield
    value(len(units) // kt - 1)
    yield from output(nc, pe, K, S, L)


def whole(S, L, u, cols):
    at = 256 if L == "L0a" else 0
    return S.masked[:, u % 2, at:at + cols]


def mha_scalar(nc, act, K, S, L, before):
    c = MHA[L]
    T, V, A = S.T, S.V, S.A
    nq, nk = c["nq"], c["nk"]
    kt = max(1, nk // P)
    banks = SECOND_BANKS
    scale = 1.0 if L == "L3x" else HD ** -0.5
    yield from high_parts(nc, act, S, L)
    for u in range(1, len(first_units(c)), 2):
        yield
    yield
    yield
    yield
    units = second_units(c)
    for u, (j, groups, k) in enumerate(units):
        cols = 2 * nq
        if L == "L0a":
            act.wait_ge(V.sem, V.at(L, "masked", u))
            scores = S.masked[:, u % 2, 0:cols]
        else:
            act.wait_ge(T.sem, T.at(L, "s2", u))
            scores = S.bank(u % banks)[:, 0:cols]
        if u >= 4:
            act.wait_ge(T.sem, T.at(L, "pv", (u - 4) // kt))
        bias = S.mask_col[:, 0:1] if L == "L1x" else 0.0
        nc.scalar.activation(S.e_pair[:, u % 4, 0, 0:cols], scores, ACT.Exp, bias=bias, scale=scale)
        if u >= 2:
            act.wait_ge(V.sem, V.at(L, "rest", u - 2))
        nc.scalar.activation(whole(S, L, u, cols), scores, ACT.Exp, bias=bias, scale=scale)\
            .then_inc(A.sem, A.hit(L, "e", u))
        if k == kt - 1:
            yield
    yield from output_turned(nc, act, S, L)


def mha_vector(nc, dve, link, K, S, L, before):
    c = MHA[L]
    T, V, A = S.T, S.V, S.A
    nq, nk = c["nq"], c["nk"]
    qt, kt, mq, mk = max(1, nq // P), max(1, nk // P), min(nq, P), min(nk, P)
    yield from operands(nc, dve, K, S, L)
    dve.wait_ge(T.sem, T.at(L, "v"))
    if nk == 64:
        for half in range(2):
            r = slice(64 * half, 64 * half + 64)
            values = S.misc[r, 0:64].rearrange("p (n d) -> p n d", d=HD)
            high, rest = (S.vstack[r, :, at:at + HD] for at in (18 * half, 18 * half + 9))
            link(nc.vector.tensor_copy(high, values))
            ins = nc.vector.tensor_tensor(rest, values, high, ALU.subtract)
    else:
        values = S.misc[:, 0:kt * P].rearrange("p (k d) -> p k d", d=HD)
        parts = S.vaug[:].rearrange("p k h d -> p (k h) d")
        link(nc.vector.tensor_copy(parts[:, :, 0:HD], values))
        ins = nc.vector.tensor_tensor(parts[:, :, 9:9 + HD], values, parts[:, :, 0:HD], ALU.subtract)
    ins.then_inc(V.sem, V.hit(L, "vaug"))
    for u, (j, blocks) in enumerate(first_units(c)):
        dve.wait_ge(T.sem, T.at(L, "s1", u))
        n = len(blocks)
        scores = S.bank(u % 3)[0:mq, 0:n * nk].rearrange("p (n k) -> p n k", k=nk)
        if L == "L0a":
            if u >= 2:
                dve.wait_ge(V.sem, V.at(L, "max", u - 2))
            mask = K.w("base", "mask_qk")[0:mq].unsqueeze(1).to_broadcast([mq, n, nk])
            summed = S.masked[0:mq, u % 2, 0:n * nk].rearrange("p (n k) -> p n k", k=nk)
            nc.vector.tensor_tensor(summed, scores, mask, ALU.add).then_inc(V.sem, V.hit(L, "sum", u))
            dve.wait_ge(V.sem, V.at(L, "sum", u))
            scores = summed
        t0, g0 = blocks[0]
        if n <= QUADS:
            out = S.negm[0:mq, t0, g0:g0 + n, j]
        else:
            out = S.negm[0:mq, :, :, j]
            scores = scores.rearrange("p (t g) k -> p t g k", g=QUADS)
        nc.vector.tensor_reduce(out, scores, X, ALU.max, negate=True).then_inc(V.sem, V.hit(L, "max", u))
        if u % 2 == 1:
            yield
    dve.wait_ge(V.sem, V.at(L, "max", u))
    negm = S.negm[0:mq, 0:qt].rearrange("p t g j -> p (t g j)")
    high, rest = (S.nm[0:mq, 0:qt].rearrange("p t g (j s) -> p (t g j) s", s=32)[:, :, n] for n in (24, 25))
    link(nc.vector.tensor_scalar(high, negm, 1.0 / GUARD, None, ALU.mult))
    nc.vector.scalar_tensor_tensor(rest, negm, 1.0 / GUARD, high, ALU.mult, ALU.subtract)\
        .then_inc(V.sem, V.hit(L, "negm"))
    yield
    yield
    dve.wait_ge(T.sem, T.at(L, "mT"))
    nc.vector.tensor_tensor(S.qop[:, 0:4 * nq], S.misc_h[:, 0:4 * nq], S.qop[:, 0:4 * nq], ALU.add)\
        .then_inc(V.sem, V.hit(L, "qmax"))
    yield
    for u, (j, groups, k) in enumerate(second_units(c)):
        if L == "L0a":
            dve.wait_ge(T.sem, T.at(L, "s2", u))
            if u >= 2:
                dve.wait_ge(A.sem, A.at(L, "e", u - 2))
            mask = K.w("base", "mask_kq").unsqueeze(1).to_broadcast([P, 2, nq])
            nc.vector.tensor_tensor(S.masked[:, u % 2, 0:2 * nq].rearrange("p (n q) -> p n q", q=nq),
                                    S.bank(u % SECOND_BANKS)[:, 0:2 * nq].rearrange("p (n q) -> p n q", q=nq), mask, ALU.add)\
                .then_inc(V.sem, V.hit(L, "masked", u))
        dve.wait_ge(A.sem, A.at(L, "e", u))
        nc.vector.tensor_tensor(S.e_pair[:, u % 4, 1, 0:2 * nq], whole(S, L, u, 2 * nq),
                                S.e_pair[:, u % 4, 0, 0:2 * nq], ALU.subtract).then_inc(V.sem, V.hit(L, "rest", u))
        if k == kt - 1:
            yield
    yield
    dve.wait_ge(T.sem, T.at(L, "pv", len(second_units(c)) // kt - 1))
    on = S.on[0:mq, 0:qt].rearrange("p t (h d) -> p t h d", d=HD)
    o = S.ps[0:mq, 2 * BANK:4 * BANK].rearrange("p (t c) -> p t c", t=2)[:, 0:qt, 0:18 * HEADS]\
        .rearrange("p t (h d) -> p t h d", d=18)
    den, rden = o[:, :, :, HD], S.rden[0:mq, 0:qt]
    if L == "L3a":
        link(nc.vector.tensor_scalar(rden, den, 1e-8, None, ALU.add))
        den = rden
    link(nc.vector.reciprocal(rden, den))
    link(nc.vector.tensor_copy(on, o[:, :, :, 9:9 + HD]))
    link(nc.vector.tensor_tensor(on, o[:, :, :, 0:HD], on, ALU.add))
    nc.vector.tensor_tensor(on, on, rden.unsqueeze(3).to_broadcast([mq, qt, HEADS, HD]), ALU.mult)\
        .then_inc(V.sem, V.hit(L, "on"))
    for _ in range(4):
        yield
    dve.wait_ge(T.sem, T.at(L, "y"))
    nc.vector.tensor_tensor(S.x[0:mq, 0:qt], S.bank(1)[0:mq, 0:qt * P].rearrange("p (t d) -> p t d", d=P),
                            S.x[0:mq, 0:qt], ALU.add).then_inc(V.sem, V.hit(L, "x"))
    yield


def l2a_plan():
    n = len(first_units(MHA["L2a"]))
    return dict(vector=["qop", "kop"] + [("max", u) for u in range(n)] + ["on", "x"],
                scalar=["qh", "kh"] + [("e", u) for u in range(n)] + ["oTc"],
                tensor=["q", "k", "v"] + [("s1", u) for u in range(n)] + ["oT", "y"], gpsimd=["wide"])


def l2a_tensor(nc, pe, K, S, L, before):
    T, V, A = S.T, S.V, S.A
    yield from project(nc, pe, K, S, L, before)
    for u, (j, blocks) in enumerate(first_units(MHA[L])):
        r = slice(32 * j, 32 * j + 32)
        if u >= 3:
            pe.wait_ge(A.sem, A.at(L, "e", u - 3))
        for n, (t, g) in enumerate(blocks):
            ins = nc.tensor.matmul(S.bank(u % 3)[:, n * SEQ:(n + 1) * SEQ], S.qop[r, g * SEQ + t * P:][:, 0:P],
                                   S.kop[r, g * SEQ:(g + 1) * SEQ], start=True, stop=True)
        ins.then_inc(T.sem, T.hit(L, "s1", u))
        if u % 2 == 1:
            yield
    yield from output(nc, pe, K, S, L)


def l2a_scalar(nc, act, K, S, L, before):
    yield from high_parts(nc, act, S, L)
    for u, (j, blocks) in enumerate(first_units(MHA[L])):
        act.wait_ge(S.V.sem, S.V.at(L, "max", u))
        for n, (t, g) in enumerate(blocks):
            ins = nc.scalar.activation(S.e[:, u % 4, n * SEQ:(n + 1) * SEQ], S.bank(u % 3)[:, n * SEQ:(n + 1) * SEQ],
                                       ACT.Exp, bias=S.negm[:, t, g, j:j + 1], accum_out=S.den[:, t, 4 * g + j:][:, 0:1])
        ins.then_inc(S.A.sem, S.A.hit(L, "e", u))
        if u % 2 == 1:
            yield
    yield from output_turned(nc, act, S, L)


def l2a_vector(nc, dve, link, K, S, L, before):
    T, V, A = S.T, S.V, S.A
    yield from operands(nc, dve, K, S, L)
    units = first_units(MHA[L])
    for u, (j, blocks) in enumerate(units):
        dve.wait_ge(T.sem, T.at(L, "s1", u))
        t, g = blocks[0]
        nc.vector.tensor_reduce(S.negm[:, t, g:g + 2, j], S.bank(u % 3).rearrange("p (n k) -> p n k", k=SEQ), X,
                                ALU.max, negate=True).then_inc(V.sem, V.hit(L, "max", u))
        if u % 2 == 1:
            yield
    yield
    dve.wait_ge(A.sem, A.at(L, "e", len(units) - 1))
    link(nc.vector.reciprocal(S.rden[:], S.den[:]))
    link(nc.vector.tensor_tensor(S.rden[:], S.rden[:], S.den[:], ALU.mult))
    nc.vector.tensor_tensor(S.on[:].rearrange("p t (h d) -> p t h d", d=HD),
                            S.misc[:, 0:SEQ].rearrange("p (t h d) -> p t h d", t=TILES, d=HD),
                            S.rden[:].unsqueeze(3).to_broadcast([P, TILES, HEADS, HD]), ALU.mult)\
        .then_inc(V.sem, V.hit(L, "on"))
    for _ in range(4):
        yield
    add_output(nc, dve, S, L, S.bank(1))
    yield


def l2a_gpsimd(nc, pool, K, S, L, before):
    yield
    widen_next(nc, pool, K, S, L)
    for _ in range(8 + len(first_units(MHA[L])) // 2):
        yield


def widen(nc, pool, K, S, L):
    for i, name in enumerate(("wq", "wk")):
        ins = nc.gpsimd.tensor_copy(
            S.wide[:, i * 512:(i + 1) * 512].rearrange("p (h r d) -> p h r d", r=4, d=HD)[:, :, 0:3],
            K.w(L, name).rearrange("p (h d) -> p h d", d=HD).unsqueeze(2).to_broadcast([P, HEADS, 3, HD]))
    return ins


def widen_next(nc, pool, K, S, L):
    following = MHA_ORDER[(MHA_ORDER.index(L) + 1) % len(MHA_ORDER)]
    K.loaded(pool, following)
    pool.wait_ge(S.T.sem, S.T.at(L, "k"))
    widen(nc, pool, K, S, following).then_inc(S.G.sem, S.G.hit(L, "wide"))


def mha_gpsimd(nc, pool, K, S, L, before):
    c = MHA[L]
    yield
    widen_next(nc, pool, K, S, L)
    for _ in range(11 + len(first_units(c)) // 2 + len(second_units(c)) // max(1, c["nk"] // P)):
        yield


L1A_PLAN = dict(tensor=["qk", "v", "s", "pT", "y"], scalar=["qkc", "e", "pTc"], vector=["vc", "max", "x"], gpsimd=[])


def l1a_tensor(nc, pe, K, S, L, before):
    T, V, A, W = S.T, S.V, S.A, K.w
    K.loaded(pe, L)
    pe.wait_ge(A.sem, A.at(before, "xnT"))
    nc.tensor.matmul(S.bank(0)[0:32, 0:SEQ], W(L, "wq"), S.xnT[:], start=True, stop=True)
    nc.tensor.matmul(S.bank(0)[0:32, SEQ:2 * SEQ], W(L, "wk"), S.xnT[:], start=True, stop=True)\
        .then_inc(T.sem, T.hit(L, "qk"))
    for t in range(TILES):
        ins = nc.tensor.matmul(S.bank(1)[:, t * P:(t + 1) * P], S.xnT[:, t * P:(t + 1) * P], K.wv_1a[:],
                               start=True, stop=True)
    ins.then_inc(T.sem, T.hit(L, "v"))
    yield
    yield
    pe.wait_ge(A.sem, A.at(L, "qkc"))
    for t in range(TILES):
        ins = nc.tensor.matmul(S.bank(0)[:, t * SEQ:(t + 1) * SEQ], S.ef[0:32, 1024 + t * P:1024 + (t + 1) * P],
                               S.ef[0:32, 1024 + SEQ:1024 + 2 * SEQ], start=True, stop=True)
    ins.then_inc(T.sem, T.hit(L, "s"))
    for _ in range(3):
        yield
    pe.wait_ge(A.sem, A.at(L, "e"))
    pe.wait_ge(V.sem, V.at(L, "vc"))
    for t in range(TILES):
        for k in range(TILES):
            ins = nc.tensor.transpose(S.bank(1)[:, k * SEQ + t * P:][:, 0:P],
                                      S.scratch[:, 512 + t * SEQ + k * P:][:, 0:P], K.ident)
    ins.then_inc(T.sem, T.hit(L, "pT"))
    yield
    yield
    pe.wait_ge(A.sem, A.at(L, "pTc"))
    for t in range(TILES):
        for k in range(TILES):
            ins = nc.tensor.matmul(S.misc[:, t * P:(t + 1) * P], S.scratch[:, 1024 + k * SEQ + t * P:][:, 0:P],
                                   S.scratch[:, 1536 + k * P:][:, 0:P], start=k == 0, stop=k == TILES - 1)
    ins.then_inc(T.sem, T.hit(L, "y"))
    yield
    yield


def l1a_scalar(nc, act, K, S, L, before):
    T, V, A = S.T, S.V, S.A
    yield
    act.wait_ge(T.sem, T.at(L, "qk"))
    nc.scalar.activation(S.ef[0:32, 1024:1536], S.bank(0)[0:32], ACT.Copy).then_inc(A.sem, A.hit(L, "qkc"))
    for _ in range(3):
        yield
    act.wait_ge(V.sem, V.at(L, "max"))
    for t in range(TILES):
        ins = nc.scalar.activation(S.scratch[:, 512 + t * SEQ:512 + (t + 1) * SEQ],
                                   S.scratch[:, t * SEQ:(t + 1) * SEQ], ACT.Exp, bias=S.small[:, t:t + 1],
                                   accum_out=S.small[:, 2 + t:3 + t])
    ins.then_inc(A.sem, A.hit(L, "e"))
    yield
    yield
    act.wait_ge(T.sem, T.at(L, "pT"))
    nc.scalar.activation(S.scratch[:, 1024:1536], S.bank(1), ACT.Copy).then_inc(A.sem, A.hit(L, "pTc"))
    for _ in range(3):
        yield


def l1a_vector(nc, dve, link, K, S, L, before):
    T, V, A = S.T, S.V, S.A
    yield
    dve.wait_ge(T.sem, T.at(L, "v"))
    nc.vector.tensor_copy(S.scratch[:, 1536:1792], S.bank(1)[:, 0:SEQ]).then_inc(V.sem, V.hit(L, "vc"))
    yield
    yield
    z, zero, masked = S.ef[:, 0:512], S.ef[:, 512:1024], S.scratch[:, 0:512]
    dve.wait_ge(T.sem, T.at(L, "s"))
    link(nc.vector.scalar_tensor_tensor(z, S.bank(0), 32.0 ** -0.5, K.causal[:], ALU.mult, ALU.mult))
    link(nc.vector.tensor_scalar(zero, z, 0.0, LOWEST, ALU.is_equal, ALU.mult))
    link(nc.vector.tensor_tensor(masked, z, zero, ALU.add))
    nc.vector.tensor_reduce(S.small[:, 0:2], masked.rearrange("p (t k) -> p t k", t=TILES), X, ALU.max, negate=True)\
        .then_inc(V.sem, V.hit(L, "max"))
    yield
    yield
    dve.wait_ge(A.sem, A.at(L, "e"))
    link(nc.vector.reciprocal(S.small[:, 4:6], S.small[:, 2:4]))
    for _ in range(3):
        yield
    dve.wait_ge(T.sem, T.at(L, "y"))
    for t in range(TILES):
        ins = nc.vector.scalar_tensor_tensor(S.x[:, t], S.misc[:, t * P:(t + 1) * P], S.small[:, 4 + t:5 + t],
                                             S.x[:, t], ALU.mult, ALU.add)
    ins.then_inc(V.sem, V.hit(L, "x"))
    yield


def l1a_gpsimd(nc, pool, K, S, L, before):
    for _ in range(9):
        yield


L0F_PLAN = dict(
    tensor=["lg", "sT", "sel", "rank", "xt", "sb", "rb", "g", "u", "sg", "eo", "su", "y"],
    scalar=["ex", "sTc", "xtc", "sbc", "gl", "sgl", "eoc"],
    vector=["d", "sc", "selT", "selc", "P", "rmT", "pw", "h", "sh", "x"], gpsimd=[])


def l0f_tensor(nc, pe, K, S, L, before):
    T, V, A, W = S.T, S.V, S.A, K.w
    K.loaded(pe, L)
    pe.wait_ge(A.sem, A.at(before, "xnT"))
    for t in range(TILES):
        ins = nc.tensor.matmul(S.misc[:, t * EXPERTS:(t + 1) * EXPERTS], S.xnT[:, t * P:(t + 1) * P], W(L, "gate"),
                               start=True, stop=True)
    ins.then_inc(T.sem, T.hit(L, "lg"))
    for _ in range(4):
        yield
    pe.wait_ge(V.sem, V.at(L, "sc"))
    for t in range(TILES):
        ins = nc.tensor.transpose(S.bank(0)[0:EXPERTS, t * P:(t + 1) * P], S.score[:, t], K.ident)
    ins.then_inc(T.sem, T.hit(L, "sT"))
    for _ in range(4):
        yield
    pe.wait_ge(V.sem, V.at(L, "selT"))
    for t in range(TILES):
        ins = nc.tensor.transpose(S.bank(1)[:, t * EXPERTS:(t + 1) * EXPERTS], S.selT[0:EXPERTS, t * P:(t + 1) * P],
                                  K.ident[0:EXPERTS, 0:EXPERTS])
    ins.then_inc(T.sem, T.hit(L, "sel"))
    yield
    yield
    pe.wait_ge(V.sem, V.at(L, "selc"))
    for t in range(TILES):
        for k in range(TILES):
            nc.tensor.matmul(S.bank(2)[:, t * EXPERTS:(t + 1) * EXPERTS], K.upto[:, k, t * P:(t + 1) * P],
                             S.sel_bf[:, k], start=k == 0, stop=k == TILES - 1)
    for k in range(TILES):
        ins = nc.tensor.matmul(S.bank(0)[0:EXPERTS, 0:SEQ], S.sel_bf[:, k], K.upto[:, k], start=k == 0,
                               stop=k == TILES - 1)
    ins.then_inc(T.sem, T.hit(L, "rank"))
    yield
    yield
    pe.wait_ge(V.sem, V.at(L, "P"))
    for t in range(TILES):
        ins = nc.tensor.matmul(S.bank(1), S.xn[:, t], S.ef[:, t * 512:(t + 1) * 512], start=t == 0,
                               stop=t == TILES - 1)
    ins.then_inc(T.sem, T.hit(L, "xt"))
    for c in range(4):
        ins = nc.tensor.matmul(S.ps[:, 1024 + c * SEQ:1024 + (c + 1) * SEQ], W("base", "spread")[0:EXPERTS, c * P:(c + 1) * P],
                               S.sT[0:EXPERTS], start=True, stop=True)
    ins.then_inc(T.sem, T.hit(L, "sb"))
    yield
    yield
    pe.wait_ge(A.sem, A.at(L, "xtc"))
    pe.wait_ge(V.sem, V.at(L, "rmT"))
    for c in range(4):
        ins = nc.tensor.matmul(S.ps[:, c * SEQ:(c + 1) * SEQ], K.spread_bf[0:EXPERTS, c * P:(c + 1) * P],
                               S.rmT[0:EXPERTS], start=True, stop=True)
    ins.then_inc(T.sem, T.hit(L, "rb"))
    yield
    pe.wait_ge(A.sem, A.at(L, "sbc"))
    for name, w, base in (("g", "wg", 1024), ("u", "wu", 0)):
        if name == "u":
            pe.wait_ge(V.sem, V.at(L, "pw"))
        for e in range(EXPERTS):
            for f in range(2):
                ins = nc.tensor.matmul(S.ps[:, base + f * 512 + e * CAP:][:, 0:CAP],
                                       W(L, w)[:, e * EXP_F + f * P:][:, 0:P],
                                       S.ef[:, 1024 + e * CAP:1024 + (e + 1) * CAP], start=True, stop=True)
            if e % 8 == 7:
                if e == EXPERTS - 1:
                    ins.then_inc(T.sem, T.hit(L, name))
                yield
    pe.wait_ge(A.sem, A.at(L, "gl"))
    for f in range(2):
        ins = nc.tensor.matmul(S.bank(3)[:, f * SEQ:(f + 1) * SEQ], W(L, "sg")[:, f * P:(f + 1) * P], S.xnT[:],
                               start=True, stop=True)
    ins.then_inc(T.sem, T.hit(L, "sg"))
    yield
    pe.wait_ge(V.sem, V.at(L, "h"))
    for e in range(EXPERTS):
        for f in range(2):
            ins = nc.tensor.matmul(S.bank(2)[32 * (e % 4):32 * (e % 4) + 32, e // 4 * P:(e // 4 + 1) * P],
                                   S.ef[:, f * 512 + e * CAP:][:, 0:CAP], W(L, "wd")[:, e * 256 + f * P:][:, 0:P],
                                   start=f == 0, stop=f == 1)
        if e % 8 == 7:
            if e == EXPERTS - 1:
                ins.then_inc(T.sem, T.hit(L, "eo"))
            yield
    for f in range(2):
        ins = nc.tensor.matmul(S.bank(0)[:, f * SEQ:(f + 1) * SEQ], W(L, "su")[:, f * P:(f + 1) * P], S.xnT[:],
                               start=True, stop=True)
    ins.then_inc(T.sem, T.hit(L, "su"))
    yield
    yield
    pe.wait_ge(A.sem, A.at(L, "eoc"))
    pe.wait_ge(V.sem, V.at(L, "sh"))
    for t in range(TILES):
        out = S.bank(1)[:, t * P:(t + 1) * P]
        for c in range(4):
            nc.tensor.matmul(out, S.scratch[:, c * SEQ + t * P:][:, 0:P], S.ef[:, 1536 + c * P:][:, 0:P],
                             start=c == 0, stop=False)
        for f in range(2):
            ins = nc.tensor.matmul(out, S.scratch[:, 1536 + f * SEQ + t * P:][:, 0:P], W(L, "sd")[:, f * P:(f + 1) * P],
                                   start=False, stop=f == 1)
    ins.then_inc(T.sem, T.hit(L, "y"))
    yield
    yield


def l0f_scalar(nc, act, K, S, L, before):
    T, V, A = S.T, S.V, S.A
    yield
    yield
    act.wait_ge(V.sem, V.at(L, "d"))
    nc.scalar.activation(S.score[:], S.dist[:], ACT.Exp).then_inc(A.sem, A.hit(L, "ex"))
    for _ in range(3):
        yield
    act.wait_ge(T.sem, T.at(L, "sT"))
    nc.scalar.activation(S.sT[0:EXPERTS], S.bank(0)[0:EXPERTS, 0:SEQ], ACT.Copy).then_inc(A.sem, A.hit(L, "sTc"))
    for _ in range(8):
        yield
    act.wait_ge(T.sem, T.at(L, "xt"))
    nc.scalar.activation(S.ef[:, 1024:1536], S.bank(1), ACT.Copy).then_inc(A.sem, A.hit(L, "xtc"))
    act.wait_ge(T.sem, T.at(L, "sb"))
    nc.scalar.activation(S.scratch[:, 1024:2048], S.ps[:, 1024:2048], ACT.Copy).then_inc(A.sem, A.hit(L, "sbc"))
    for _ in range(4):
        yield
    act.wait_ge(T.sem, T.at(L, "g"))
    act.wait_ge(V.sem, V.at(L, "pw"))
    nc.scalar.activation(S.scratch[:, 1024:2048], S.ps[:, 1024:2048], ACT.Gelu).then_inc(A.sem, A.hit(L, "gl"))
    for _ in range(4):
        yield
    act.wait_ge(T.sem, T.at(L, "sg"))
    act.wait_ge(V.sem, V.at(L, "h"))
    nc.scalar.activation(S.scratch[:, 1024:1536], S.bank(3), ACT.Gelu).then_inc(A.sem, A.hit(L, "sgl"))
    yield
    act.wait_ge(T.sem, T.at(L, "eo"))
    nc.scalar.activation(S.ef[:, 1536:2048], S.bank(2), ACT.Copy).then_inc(A.sem, A.hit(L, "eoc"))
    for _ in range(4):
        yield


def l0f_vector(nc, dve, link, K, S, L, before):
    T, V, A = S.T, S.V, S.A
    natural = "p (r i) -> p i r"
    yield
    dve.wait_ge(T.sem, T.at(L, "lg"))
    logits = S.misc[:, 0:2 * EXPERTS].rearrange("p (t e) -> p t e", t=TILES)
    link(nc.vector.tensor_reduce(S.small[:, 0:2], logits, X, ALU.max, negate=True))
    nc.vector.tensor_tensor(S.dist[:], logits, S.small[:, 0:2].unsqueeze(2).to_broadcast([P, 2, EXPERTS]), ALU.add)\
        .then_inc(V.sem, V.hit(L, "d"))
    yield
    yield
    dve.wait_ge(A.sem, A.at(L, "ex"))
    link(nc.vector.tensor_reduce(S.small[:, 2:4], S.score[:], X, ALU.add))
    link(nc.vector.reciprocal(S.small[:, 4:6], S.small[:, 2:4]))
    nc.vector.tensor_tensor(S.score[:], S.score[:], S.small[:, 4:6].unsqueeze(2).to_broadcast([P, 2, EXPERTS]),
                            ALU.mult).then_inc(V.sem, V.hit(L, "sc"))
    for _ in range(3):
        yield
    dve.wait_ge(A.sem, A.at(L, "sTc"))
    link(nc.vector.tensor_copy(S.work[0:EXPERTS, 0].rearrange("p (i r) -> p i r", r=4),
                               S.sT[0:EXPERTS].rearrange(natural, r=4)))
    for n in range(CAP // 8):
        link(nc.vector.max(S.best[0:EXPERTS], S.work[0:EXPERTS, n % 2]))
        link(nc.vector.match_replace(out=S.work[0:EXPERTS, 1 - n % 2], in_to_replace=S.best[0:EXPERTS],
                                     in_values=S.work[0:EXPERTS, n % 2], imm_value=-1.0))
        if n == 1:
            yield
    nc.vector.tensor_scalar(S.selT[0:EXPERTS].rearrange(natural, r=4),
                            S.work[0:EXPERTS, 0].rearrange("p (i r) -> p i r", r=4), 0.0, None, ALU.is_lt)\
        .then_inc(V.sem, V.hit(L, "selT"))
    yield
    yield
    dve.wait_ge(T.sem, T.at(L, "sel"))
    nc.vector.tensor_copy(S.sel_bf[:], S.bank(1)[:, 0:2 * EXPERTS].rearrange("p (t e) -> p t e", t=TILES))\
        .then_inc(V.sem, V.hit(L, "selc"))
    yield
    yield
    dve.wait_ge(T.sem, T.at(L, "rank"))
    dve.wait_ge(V.sem, V.at(L, "selc"))
    link(nc.vector.tensor_tensor(S.rank[:], S.bank(2)[:, 0:2 * EXPERTS].rearrange("p (t e) -> p t e", t=TILES),
                                 S.sel_bf[:], ALU.mult))
    for t in range(TILES):
        ins = nc.vector.tensor_tensor(
            S.ef[:, t * 512:(t + 1) * 512].rearrange("p (e s) -> p e s", s=CAP),
            K.w("base", "count").unsqueeze(1).to_broadcast([P, EXPERTS, CAP]),
            S.rank[:, t].unsqueeze(2).to_broadcast([P, EXPERTS, CAP]), ALU.is_equal)
    ins.then_inc(V.sem, V.hit(L, "P"))
    nc.vector.tensor_tensor(S.rmT[0:EXPERTS], S.bank(0)[0:EXPERTS, 0:SEQ], S.selT[0:EXPERTS], ALU.mult)\
        .then_inc(V.sem, V.hit(L, "rmT"))
    for _ in range(4):
        yield
    dve.wait_ge(T.sem, T.at(L, "rb"))
    dve.wait_ge(A.sem, A.at(L, "sbc"))
    nc.vector.scalar_tensor_tensor(S.scratch[:, 0:1024], S.ps[:, 0:1024], K.w("base", "slot"),
                                   S.scratch[:, 1024:2048], ALU.is_equal, ALU.mult).then_inc(V.sem, V.hit(L, "pw"))
    for _ in range(4):
        yield
    dve.wait_ge(T.sem, T.at(L, "u"))
    dve.wait_ge(A.sem, A.at(L, "gl"))
    nc.vector.tensor_tensor(S.ef[:, 0:1024], S.ps[:, 0:1024], S.scratch[:, 1024:2048], ALU.mult)\
        .then_inc(V.sem, V.hit(L, "h"))
    for _ in range(4):
        yield
    dve.wait_ge(T.sem, T.at(L, "su"))
    dve.wait_ge(A.sem, A.at(L, "sgl"))
    nc.vector.tensor_tensor(S.scratch[:, 1536:2048], S.bank(0), S.scratch[:, 1024:1536], ALU.mult)\
        .then_inc(V.sem, V.hit(L, "sh"))
    yield
    yield
    add_output(nc, dve, S, L, S.bank(1))
    yield


def l0f_gpsimd(nc, pool, K, S, L, before):
    for _ in range(26):
        yield


def add_output(nc, dve, S, L, y):
    dve.wait_ge(S.T.sem, S.T.at(L, "y"))
    nc.vector.tensor_tensor(S.x[:], y[:, 0:SEQ].rearrange("p (t d) -> p t d", d=P), S.x[:], ALU.add)\
        .then_inc(S.V.sem, S.V.hit(L, "x"))


L1F_PLAN = dict(tensor=["up0", "up1", "y"], scalar=["r0", "r1"], vector=["xq", "h0", "h1", "x"], gpsimd=[])


def l1f_tensor(nc, pe, K, S, L, before):
    T, V, A = S.T, S.V, S.A
    yield
    pe.wait_ge(V.sem, V.at(L, "xq"))
    for c in range(4):
        ins = nc.tensor.matmul(S.ps[:, c * SEQ:(c + 1) * SEQ], K.w1q[:, c * P:(c + 1) * P], S.hi_bf[:, 0:SEQ],
                               start=True, stop=True)
        if c % 2:
            ins.then_inc(T.sem, T.hit(L, "up%d" % (c // 2)))
    for _ in range(3):
        yield
    pe.wait_ge(V.sem, V.at(L, "h1"))
    for t in range(TILES):
        out = S.misc[:, t * P:(t + 1) * P]
        for c in range(4):
            nc.tensor.matmul(out, S.kop_bf[:, c * SEQ + t * P:][:, 0:P], K.w2q[:, c * P:(c + 1) * P],
                             start=c == 0, stop=False)
        ins = nc.tensor.matmul(out, K.ones_bf[0:1, 0:P], K.b2q[0:1], start=False, stop=True)
    ins.then_inc(T.sem, T.hit(L, "y"))
    yield
    yield


def l1f_scalar(nc, act, K, S, L, before):
    T, V, A = S.T, S.V, S.A
    yield
    yield
    for n in range(2):
        act.wait_ge(T.sem, T.at(L, "up%d" % n))
        for c in (2 * n, 2 * n + 1):
            ins = nc.scalar.activation(S.scratch[:, c * SEQ:(c + 1) * SEQ], S.ps[:, c * SEQ:(c + 1) * SEQ], ACT.Relu,
                                       bias=K.b1q[:, c:c + 1], scale=1.0 / 64)
        ins.then_inc(A.sem, A.hit(L, "r%d" % n))
    for _ in range(4):
        yield


def l1f_vector(nc, dve, link, K, S, L, before):
    T, V, A = S.T, S.V, S.A
    dve.wait_ge(A.sem, A.at(before, "xnT"))
    link(nc.vector.tensor_scalar(S.scratch[:, 1024:1280], S.xnT[:], 16.0, 127.0, ALU.mult, ALU.min))
    link(nc.vector.tensor_scalar(S.scratch[:, 1280:1536], S.scratch[:, 1024:1280], -128.0, ROUND, ALU.max, ALU.add))
    nc.vector.tensor_scalar(S.hi_bf[:, 0:SEQ], S.scratch[:, 1280:1536], -ROUND, None, ALU.add)\
        .then_inc(V.sem, V.hit(L, "xq"))
    for _ in range(3):
        yield
    for n in range(2):
        dve.wait_ge(A.sem, A.at(L, "r%d" % n))
        part = slice(n * 512, (n + 1) * 512)
        link(nc.vector.tensor_scalar(S.scratch[:, 1024:1536], S.scratch[:, part], 127.0, ROUND, ALU.min, ALU.add))
        nc.vector.tensor_scalar(S.kop_bf[:, part], S.scratch[:, 1024:1536], -ROUND, None, ALU.add)\
            .then_inc(V.sem, V.hit(L, "h%d" % n))
        dve.wait_ge(V.sem, V.at(L, "h%d" % n))
    yield
    yield
    dve.wait_ge(T.sem, T.at(L, "y"))
    for t in range(TILES):
        ins = nc.vector.scalar_tensor_tensor(S.x[:, t], S.misc[:, t * P:(t + 1) * P], 1.0 / 1024, S.x[:, t],
                                             ALU.mult, ALU.add)
    ins.then_inc(V.sem, V.hit(L, "x"))
    yield


def l1f_gpsimd(nc, pool, K, S, L, before):
    for _ in range(6):
        yield


L2X_PLAN = dict(
    gpsimd=["rstd2"],
    vector=["var2", "xn2", "vaug"] + [("max", u) for u in range(4)] + ["negm"]
    + [("on", u) for u in range(6)] + [("h", c) for c in range(4)] + ["x"],
    scalar=["xn2T", "kc", ("qc", 0), ("qc", 1), "nmT"] + [("e", u) for u in range(4)] + ["oT0", "oT1"] + [("g", c) for c in range(4)],
    tensor=["nT", "kv", ("q", 0), ("q", 1)] + [("s1", u) for u in range(4)] + ["mT"] + [("s2", u) for u in range(4)]
    + ["pv0", "pv1", "pv2", "oT0", "pv3", "pv4", "pv5", "oT1"] + [("ff", c) for c in range(4)] + ["y"])
PAIR_BANKS = [(0, 3), (3, 6), (6, 8)]


def l2x_gpsimd(nc, pool, K, S, L, before):
    pool.wait_ge(S.V.sem, S.V.at(L, "var2"))
    nc.gpsimd.tensor_tensor(S.rstd3[:], S.var3[:], K.neg_half3[:], ALU.pow).then_inc(S.G.sem, S.G.hit(L, "rstd2"))
    for _ in range(28):
        yield


def l2x_tensor(nc, pe, K, S, L, before):
    T, V, A, W = S.T, S.V, S.A, K.w
    K.loaded(pe, L)
    yield
    yield
    pe.wait_ge(V.sem, V.at(L, "xn2"))
    pe.wait_ge(A.sem, A.at(before, "xnT"))
    for t in range(TILES):
        nc.tensor.transpose(S.bank(0)[:, t * P:(t + 1) * P], S.xn2[:, t], K.ident)
    nc.tensor.transpose(S.bank(0)[:, SEQ:SEQ + KEYS], S.cn[0:KEYS], K.ident[0:KEYS, 0:KEYS])\
        .then_inc(T.sem, T.hit(L, "nT"))
    yield
    yield
    pe.wait_ge(A.sem, A.at(L, "xn2T"))
    nc.tensor.matmul(S.misc[:, 0:KEYS], W(L, "wk"), S.cnT[:], start=True, stop=True)
    nc.tensor.matmul(S.bank(0)[0:64, 0:64], S.cnT[:], W(L, "wv"), start=True, stop=True)
    nc.tensor.matmul(S.bank(0)[64:128, 0:64], S.cnT[:], W(L, "wv"), start=True, stop=True)\
        .then_inc(T.sem, T.hit(L, "kv"))
    for n in range(2):
        if n:
            yield
            yield
            pe.wait_ge(A.sem, A.at(L, "qc", 0))
        for a in range(4):
            ins = nc.tensor.matmul(S.ps[:, BANK + a * SEQ:BANK + (a + 1) * SEQ], W(L, "wq")[:, (4 * n + a) * P:][:, 0:P],
                                   S.xn2T[:], start=True, stop=True)
        ins.then_inc(T.sem, T.hit(L, "q", n))
    yield
    yield
    for u in range(4):
        t, first = u // 2, 4 * (u % 2)
        pe.wait_ge(A.sem, A.at(L, "qc", 1))
        if u == 0:
            pe.wait_ge(V.sem, V.at(L, "vaug"))
        if u == 3:
            pe.wait_ge(V.sem, V.at(L, "max", 0))
        for a in range(4):
            ins = nc.tensor.matmul(S.bank(u % 3)[:, a * P:(a + 1) * P],
                                   S.scratch[:, (first + a) * SEQ + t * P:][:, 0:P], S.kpair[:], start=True, stop=True)
        ins.then_inc(T.sem, T.hit(L, "s1", u))
        if u % 2:
            yield
    yield
    pe.wait_ge(V.sem, V.at(L, "negm"))
    for t in range(TILES):
        ins = nc.tensor.transpose(S.misc_bf[:, t * P:(t + 1) * P], S.nm2[:, t].rearrange("p j s -> p (j s)"),
                                  K.ident_bf)
    ins.then_inc(T.sem, T.hit(L, "mT"))
    yield
    yield
    for u in range(4):
        if u == 0:
            pe.wait_ge(A.sem, A.at(L, "nmT"))
        if u == 3:
            pe.wait_ge(A.sem, A.at(L, "e", 0))
        for i in range(2):
            a, out = 2 * u + i, S.bank(u % 3)[:, i * SEQ:(i + 1) * SEQ]
            nc.tensor.matmul(out, S.kpair[:], S.scratch[:, a * SEQ:(a + 1) * SEQ], start=True, stop=False)
            ins = nc.tensor.matmul(out, K.sel2[:, a], S.nmT[:], start=False, stop=True)
        ins.then_inc(T.sem, T.hit(L, "s2", u))
        if u % 2:
            yield
    for t in range(TILES):
        if t == 0:
            pe.wait_ge(A.sem, A.at(L, "e", 3))
        else:
            pe.wait_ge(A.sem, A.at(L, "oT0"))
        for n, (a0, a1) in enumerate(PAIR_BANKS):
            for a in range(a0, a1):
                ins = nc.tensor.matmul(S.bank(n)[:, (a - a0) * 130:(a - a0 + 1) * 130], S.ef[:, a * SEQ + t * P:][:, 0:P],
                                       S.vpair[:], start=True, stop=True)
            ins.then_inc(T.sem, T.hit(L, "pv%d" % (3 * t + n)))
        yield
        yield
        pe.wait_ge(V.sem, V.at(L, "on", 3 * t + 2))
        for a in range(8):
            ins = nc.tensor.transpose(S.ps[:, a * P:(a + 1) * P], S.scratch[:, t * 1024 + a * P:][:, 0:P], K.ident)
        ins.then_inc(T.sem, T.hit(L, "oT%d" % t))
        yield
        yield
    for c in range(4):
        if c == 0:
            pe.wait_ge(A.sem, A.at(L, "oT1"))
        if c == 3:
            pe.wait_ge(V.sem, V.at(L, "h", 0))
        for i in range(2):
            ins = nc.tensor.matmul(S.bank(c % 3)[:, i * SEQ:(i + 1) * SEQ], W(L, "w1")[:, i * 512 + c * P:][:, 0:P],
                                   S.xn2T[:], start=True, stop=True)
        ins.then_inc(T.sem, T.hit(L, "ff", c))
        if c % 2:
            yield
    yield
    pe.wait_ge(V.sem, V.at(L, "h", 3))
    for t in range(TILES):
        out = S.misc[:, t * P:(t + 1) * P]
        for a in range(8):
            nc.tensor.matmul(out, S.oT2(t, a), W(L, "wo")[:, a * P:(a + 1) * P], start=a == 0, stop=False)
        for c in range(4):
            ins = nc.tensor.matmul(out, S.scratch[:, 1024 + c * SEQ + t * P:][:, 0:P], W(L, "w2")[:, c * P:(c + 1) * P],
                                   start=False, stop=c == 3)
    ins.then_inc(T.sem, T.hit(L, "y"))
    yield
    yield


def l2x_scalar(nc, act, K, S, L, before):
    T, V, A, W = S.T, S.V, S.A, K.w
    for _ in range(3):
        yield
    act.wait_ge(T.sem, T.at(L, "nT"))
    nc.scalar.activation(S.cnT[:], S.bank(0)[:, SEQ:SEQ + KEYS], ACT.Identity, bias=W(L, "cb"), scale=W(L, "cg"))
    nc.scalar.activation(S.xn2T[:], S.bank(0)[:, 0:SEQ], ACT.Identity, bias=W(L, "lb"), scale=W(L, "lg"))\
        .then_inc(A.sem, A.hit(L, "xn2T"))
    yield
    yield
    act.wait_ge(T.sem, T.at(L, "kv"))
    for r in (slice(0, 64), slice(64, 128)):
        ins = nc.scalar.activation(S.kpair[r, r], S.misc[r, 0:KEYS], ACT.Copy)
    ins.then_inc(A.sem, A.hit(L, "kc"))
    for n in range(2):
        act.wait_ge(T.sem, T.at(L, "q", n))
        nc.scalar.activation(S.scratch[:, n * 1024:(n + 1) * 1024], S.ps[:, BANK:BANK + 1024], ACT.Copy)\
            .then_inc(A.sem, A.hit(L, "qc", n))
        yield
        yield
    for _ in range(3):
        yield
    act.wait_ge(T.sem, T.at(L, "mT"))
    nc.scalar.activation(S.nmT[:], S.misc_bf[:, 0:SEQ], ACT.Copy).then_inc(A.sem, A.hit(L, "nmT"))
    yield
    for u in range(4):
        act.wait_ge(T.sem, T.at(L, "s2", u))
        nc.scalar.activation(S.e[:, u], S.bank(u % 3), ACT.Exp, scale=64.0 ** -0.5).then_inc(A.sem, A.hit(L, "e", u))
        if u % 2:
            yield
    for t in range(TILES):
        for _ in range(3):
            yield
        act.wait_ge(T.sem, T.at(L, "oT%d" % t))
        nc.scalar.activation(S.oT2_all(t), S.ps[:, 0:1024], ACT.Copy).then_inc(A.sem, A.hit(L, "oT%d" % t))
        yield
    for c in range(4):
        act.wait_ge(T.sem, T.at(L, "ff", c))
        nc.scalar.activation(S.scratch[:, c * SEQ:(c + 1) * SEQ], S.bank(c % 3)[:, SEQ:2 * SEQ], ACT.Silu)\
            .then_inc(A.sem, A.hit(L, "g", c))
        if c % 2:
            yield
    for _ in range(3):
        yield


def l2x_vector(nc, dve, link, K, S, L, before):
    T, V, A = S.T, S.V, S.A
    dve.wait_ge(V.sem, V.at(before, "xn"))
    for t in range(TILES):
        nc.vector.bn_stats(S.stats[:, t], S.xn[:, t])
    link(nc.vector.bn_stats(S.stats[0:KEYS, 2], S.ctx[0:KEYS]))
    for t in range(TILES):
        nc.vector.bn_aggr(S.mv[:, t], S.stats[:, t])
    link(nc.vector.bn_aggr(S.mv[0:KEYS, 2], S.stats[0:KEYS, 2]))
    nc.vector.tensor_scalar(S.var3[:], S.mv[:, :, 1], EPS, None, ALU.add).then_inc(V.sem, V.hit(L, "var2"))
    yield
    dve.wait_ge(S.G.sem, S.G.at(L, "rstd2"))
    for t in range(TILES):
        nc.vector.tensor_scalar(S.xn2[:, t], S.xn[:, t], S.mv[:, t, 0:1], S.rstd3[:, t:t + 1],
                                ALU.subtract, ALU.mult)
    nc.vector.tensor_scalar(S.cn[0:KEYS], S.ctx[0:KEYS], S.mv[0:KEYS, 2, 0:1], S.rstd3[0:KEYS, 2:3],
                            ALU.subtract, ALU.mult).then_inc(V.sem, V.hit(L, "xn2"))
    for _ in range(5):
        yield
    dve.wait_ge(T.sem, T.at(L, "kv"))
    dve.wait_ge(A.sem, A.at(L, "kc"))
    nc.vector.tensor_copy(S.vpair[0:64, 0:64], S.bank(0)[0:64, 0:64])
    nc.vector.tensor_copy(S.vpair[64:128, 65:129], S.bank(0)[64:128, 0:64]).then_inc(V.sem, V.hit(L, "vaug"))
    yield
    yield
    for u in range(4):
        dve.wait_ge(T.sem, T.at(L, "s1", u))
        first = 4 * (u % 2)
        nc.vector.tensor_reduce(S.negm2[:, u // 2, :, first:first + 4].rearrange("p h a -> p a h"),
                                S.bank(u % 3).rearrange("p (a h k) -> p a h k", a=4, h=2), X,
                                ALU.max, negate=True).then_inc(V.sem, V.hit(L, "max", u))
        if u % 2:
            yield
    dve.wait_ge(V.sem, V.at(L, "max", 3))
    link(nc.vector.tensor_copy(S.nm2[:, :, :, 0:8], S.negm2[:]))
    nc.vector.tensor_tensor(S.nm2[:, :, :, 8:16], S.negm2[:], S.nm2[:, :, :, 0:8], ALU.subtract)\
        .then_inc(V.sem, V.hit(L, "negm"))
    for _ in range(5):
        yield
    for t in range(TILES):
        yield
        for n, (a0, a1) in enumerate(PAIR_BANKS):
            m = 2 * (a1 - a0)
            dve.wait_ge(T.sem, T.at(L, "pv%d" % (3 * t + n)))
            o = S.bank(n)[:, 0:65 * m].rearrange("p (h d) -> p h d", d=65)
            link(nc.vector.reciprocal(S.small[:, 0:m], o[:, :, 64]))
            nc.vector.tensor_tensor(
                S.scratch[:, t * 1024 + a0 * P:t * 1024 + a1 * P].rearrange("p (h d) -> p h d", d=64), o[:, :, 0:64],
                S.small[:, 0:m].unsqueeze(2).to_broadcast([P, m, 64]), ALU.mult).then_inc(V.sem, V.hit(L, "on", 3 * t + n))
            dve.wait_ge(V.sem, V.at(L, "on", 3 * t + n))
        for _ in range(3):
            yield
    yield
    for c in range(4):
        dve.wait_ge(A.sem, A.at(L, "g", c))
        nc.vector.tensor_tensor(S.scratch[:, 1024 + c * SEQ:1024 + (c + 1) * SEQ], S.bank(c % 3)[:, 0:SEQ],
                                S.scratch[:, c * SEQ:(c + 1) * SEQ], ALU.mult).then_inc(V.sem, V.hit(L, "h", c))
        if c % 2:
            yield
    yield
    add_output(nc, dve, S, L, S.misc)
    yield


L2F_PLAN = dict(
    gpsimd=[],
    tensor=["lg"] + [k for e in range(MOE) for k in
                     [("up", e, 0), ("up", e, 1)] + ([("dn", e - 1)] if e else [])] + [("dn", MOE - 1)],
    scalar=["ex"] + [("h", e, i) for e in range(MOE) for i in range(2)],
    vector=["d", "w"] + [("acc", e) for e in range(MOE)])


def l2f_tensor(nc, pe, K, S, L, before):
    T, V, A, W = S.T, S.V, S.A, K.w
    K.loaded(pe, L)
    rows = K.rows[L]
    pe.wait_ge(A.sem, A.at(before, "xnT"))
    for t in range(TILES):
        out = S.misc[:, t * MOE:(t + 1) * MOE]
        nc.tensor.matmul(out, S.xnT[:, t * P:(t + 1) * P], W(L, "wr"), start=True, stop=False)
        ins = nc.tensor.matmul(out, K.ones_bf[96:99, 0:P], rows[96:99, 0:MOE], start=False, stop=True)
    ins.then_inc(T.sem, T.hit(L, "lg"))
    yield

    def down(e):
        if e == 0:
            pe.wait_ge(V.sem, V.at(L, "d"))
        else:
            pe.wait_ge(V.sem, V.at(L, "acc", e - 1))
        pe.wait_ge(A.sem, A.at(L, "h", e, 1))
        part = 32 * (e // 4)
        for t in range(TILES):
            out = S.misc[:, t * P:(t + 1) * P]
            for c in range(MOE_C):
                nc.tensor.matmul(out, S.scratch[:, (e % 2) * 1024 + c * SEQ + t * P:][:, 0:P],
                                 W(L, "w2")[:, (e * MOE_C + c) * P:][:, 0:P], start=c == 0, stop=False)
            ins = nc.tensor.matmul(out, K.ones_bf[part:part + 3, 0:P], rows[part:part + 3, e % 4 * P:(e % 4 + 1) * P],
                                   start=False, stop=True)
        ins.then_inc(T.sem, T.hit(L, "dn", e))

    for e in range(MOE):
        for i in range(2):
            n = 2 * e + i
            if n >= 3:
                pe.wait_ge(A.sem, A.at(L, "h", (n - 3) // 2, (n - 3) % 2))
            for c in range(2):
                ins = nc.tensor.matmul(S.bank(n % 3)[:, c * SEQ:(c + 1) * SEQ],
                                       W(L, "w1")[:, e * MOE_H + (2 * i + c) * P:][:, 0:P], S.xnT[:],
                                       start=True, stop=True)
            ins.then_inc(T.sem, T.hit(L, "up", e, i))
        if e:
            down(e - 1)
        yield
    yield
    down(MOE - 1)
    yield
    yield


def l2f_scalar(nc, act, K, S, L, before):
    T, V, A, W = S.T, S.V, S.A, K.w
    act.wait_ge(V.sem, V.at(L, "d"))
    nc.scalar.activation(S.gate[:], S.gate_d[:], ACT.Exp).then_inc(A.sem, A.hit(L, "ex"))
    yield
    for e in range(MOE):
        for i in range(2):
            n = 2 * e + i
            act.wait_ge(T.sem, T.at(L, "up", e, i))
            if e >= 2 and i == 0:
                act.wait_ge(T.sem, T.at(L, "dn", e - 2))
            for c in range(2):
                ins = nc.scalar.activation(S.scratch[:, (e % 2) * 1024 + (2 * i + c) * SEQ:][:, 0:SEQ],
                                           S.bank(n % 3)[:, c * SEQ:(c + 1) * SEQ], ACT.Gelu,
                                           bias=W(L, "b1")[:, e * MOE_C + 2 * i + c:][:, 0:1])
            ins.then_inc(A.sem, A.hit(L, "h", e, i))
        yield
    yield
    yield
    yield


def l2f_vector(nc, dve, link, K, S, L, before):
    T, V, A = S.T, S.V, S.A
    dve.wait_ge(T.sem, T.at(L, "lg"))
    link(nc.vector.tensor_copy(S.logit[:], S.misc[:, 0:2 * MOE].rearrange("p (t e) -> p t e", t=TILES)))
    for t in range(TILES):
        ins = nc.vector.max(S.best8[:, t], S.logit[:, t])
    link(ins)
    nc.vector.tensor_tensor(S.gate_d[:], S.logit[:], S.best8[:, :, 0:1].to_broadcast([P, 2, MOE]), ALU.subtract)\
        .then_inc(V.sem, V.hit(L, "d"))
    link(nc.vector.tensor_tensor(S.kept[:], S.logit[:], S.best8[:, :, 1:2].to_broadcast([P, 2, MOE]), ALU.is_ge))
    dve.wait_ge(A.sem, A.at(L, "ex"))
    link(nc.vector.tensor_tensor(S.gate[:], S.gate[:], S.kept[:], ALU.mult))
    link(nc.vector.tensor_reduce(S.small[:, 0:2], S.gate[:], X, ALU.add))
    link(nc.vector.reciprocal(S.small[:, 2:4], S.small[:, 0:2]))
    nc.vector.tensor_tensor(S.gate[:], S.gate[:], S.small[:, 2:4].unsqueeze(2).to_broadcast([P, 2, MOE]), ALU.mult)\
        .then_inc(V.sem, V.hit(L, "w"))
    dve.wait_ge(V.sem, V.at(L, "w"))
    yield
    for e in range(MOE + 1):
        if e == MOE:
            yield
            yield
        if e:
            dve.wait_ge(T.sem, T.at(L, "dn", e - 1))
            for t in range(TILES):
                ins = nc.vector.scalar_tensor_tensor(S.x[:, t], S.misc[:, t * P:(t + 1) * P], S.gate[:, t, e - 1:e],
                                                     S.x[:, t], ALU.mult, ALU.add)
            ins.then_inc(V.sem, V.hit(L, "acc", e - 1))
            dve.wait_ge(V.sem, V.at(L, "acc", e - 1))
        yield


def l2f_gpsimd(nc, pool, K, S, L, before):
    for _ in range(MOE + 4):
        yield


RANKS = [1, 2, 4, 8]
L3F_PLAN = dict(gpsimd=["nrm"], tensor=["pj", "lg", "zT", "y"], scalar=["pjc", "ex", "zTc"],
                vector=["sq", "ss", "d", "zs", "x"])


def l3f_gpsimd(nc, pool, K, S, L, before):
    for _ in range(4):
        yield
    pool.wait_ge(S.V.sem, S.V.at(L, "ss"))
    nc.gpsimd.tensor_tensor(S.small[:, 2:4], S.small[:, 0:2], K.half[:], ALU.pow).then_inc(S.G.sem, S.G.hit(L, "nrm"))
    for _ in range(8):
        yield


def l3f_tensor(nc, pe, K, S, L, before):
    T, V, A, W = S.T, S.V, S.A, K.w
    K.loaded(pe, L)
    pe.wait_ge(A.sem, A.at(before, "xnT"))
    nc.tensor.matmul(S.bank(0)[0:32, 0:SEQ], W(L, "wp"), S.xnT[:], start=True, stop=True)\
        .then_inc(T.sem, T.hit(L, "pj"))
    for _ in range(3):
        yield
    pe.wait_ge(A.sem, A.at(L, "pjc"))
    pe.wait_ge(V.sem, V.at(L, "sq"))
    for t in range(TILES):
        tok = slice(t * P, (t + 1) * P)
        nc.tensor.matmul(S.bank(2)[:, 5 * t:5 * t + 4], S.scratch[0:32, tok], W(L, "sim")[0:32], start=True, stop=True)
        nc.tensor.matmul(S.bank(2)[:, 5 * t + 4:5 * t + 5], S.scratch[0:32, SEQ + t * P:][:, 0:P], K.ones[0:32, 0:1],
                         start=True, stop=True)
        ins = nc.tensor.matmul(S.misc[:, 15 * t:15 * t + 15], S.xnT[:, tok], W(L, "down"), start=True, stop=True)
    ins.then_inc(T.sem, T.hit(L, "lg"))
    for _ in range(5):
        yield
    pe.wait_ge(V.sem, V.at(L, "zs"))
    for t in range(TILES):
        ins = nc.tensor.transpose(S.bank(0)[0:15, t * P:(t + 1) * P], S.scratch[:, 1024 + 15 * t:1024 + 15 * t + 15],
                                  K.ident)
    ins.then_inc(T.sem, T.hit(L, "zT"))
    yield
    yield
    pe.wait_ge(A.sem, A.at(L, "zTc"))
    for t in range(TILES):
        tok = slice(t * P, (t + 1) * P)
        nc.tensor.matmul(S.bank(1)[:, tok], S.xnT[:, tok], W(L, "w"), start=True, stop=False)
        ins = nc.tensor.matmul(S.bank(1)[:, tok], S.scratch[0:15, 512 + t * P:][:, 0:P], W(L, "up")[0:15],
                               start=False, stop=True)
    ins.then_inc(T.sem, T.hit(L, "y"))
    yield
    yield


def l3f_scalar(nc, act, K, S, L, before):
    T, V, A, W = S.T, S.V, S.A, K.w
    yield
    act.wait_ge(T.sem, T.at(L, "pj"))
    nc.scalar.activation(S.scratch[0:32, 0:SEQ], S.bank(0)[0:32, 0:SEQ], ACT.Identity, bias=W(L, "bp")[0:32])\
        .then_inc(A.sem, A.hit(L, "pjc"))
    for _ in range(5):
        yield
    act.wait_ge(V.sem, V.at(L, "d"))
    nc.scalar.activation(S.top4[:, 1], S.top4[:, 0], ACT.Exp).then_inc(A.sem, A.hit(L, "ex"))
    for _ in range(3):
        yield
    act.wait_ge(T.sem, T.at(L, "zT"))
    nc.scalar.activation(S.scratch[0:15, 512:768], S.bank(0)[0:15, 0:SEQ], ACT.Copy).then_inc(A.sem, A.hit(L, "zTc"))
    for _ in range(3):
        yield


def l3f_vector(nc, dve, link, K, S, L, before):
    T, V, A = S.T, S.V, S.A
    yield
    yield
    dve.wait_ge(A.sem, A.at(L, "pjc"))
    nc.vector.tensor_tensor(S.scratch[0:32, SEQ:2 * SEQ], S.scratch[0:32, 0:SEQ], S.scratch[0:32, 0:SEQ], ALU.mult)\
        .then_inc(V.sem, V.hit(L, "sq"))
    yield
    yield
    dve.wait_ge(T.sem, T.at(L, "lg"))
    raw = S.bank(2)[:, 0:10].rearrange("p (t e) -> p t e", t=TILES)
    nc.vector.tensor_copy(S.small[:, 0:2], raw[:, :, 4]).then_inc(V.sem, V.hit(L, "ss"))
    yield
    lg, ex, eq = S.top4[:, 0], S.top4[:, 1], S.top4[:, 2]
    dve.wait_ge(S.G.sem, S.G.at(L, "nrm"))
    link(nc.vector.tensor_scalar(S.small[:, 4:6], S.small[:, 2:4], 1e-12, None, ALU.max))
    link(nc.vector.reciprocal(S.small[:, 6:8], S.small[:, 4:6]))
    link(nc.vector.tensor_tensor(lg, raw[:, :, 0:4], S.small[:, 6:8].unsqueeze(2).to_broadcast([P, 2, 4]), ALU.mult))
    link(nc.vector.tensor_tensor(lg, lg, K.route[:].unsqueeze(1).to_broadcast([P, 2, 4]), ALU.mult))
    link(nc.vector.tensor_reduce(S.small[:, 8:10], lg, X, ALU.max, negate=True))
    nc.vector.tensor_tensor(lg, lg, S.small[:, 8:10].unsqueeze(2).to_broadcast([P, 2, 4]), ALU.add)\
        .then_inc(V.sem, V.hit(L, "d"))
    dve.wait_ge(V.sem, V.at(L, "d"))
    link(nc.vector.tensor_scalar(eq, lg, 0.0, None, ALU.is_equal))
    first, seen = S.top4[:, 3], S.small[:, 10:12].unsqueeze(2)
    link(nc.vector.tensor_copy(first[:, :, 0:1], eq[:, :, 0:1]))
    link(nc.vector.tensor_copy(seen, eq[:, :, 0:1]))
    for e in range(1, 4):
        link(nc.vector.tensor_tensor(first[:, :, e:e + 1], eq[:, :, e:e + 1], seen, ALU.is_gt))
        link(nc.vector.tensor_tensor(seen, seen, eq[:, :, e:e + 1], ALU.max))
    yield
    yield
    dve.wait_ge(A.sem, A.at(L, "ex"))
    link(nc.vector.tensor_reduce(S.small[:, 12:14], ex, X, ALU.add))
    link(nc.vector.reciprocal(S.small[:, 14:16], S.small[:, 12:14]))
    link(nc.vector.tensor_tensor(first, first, ex, ALU.mult))
    link(nc.vector.tensor_tensor(first, first, S.small[:, 14:16].unsqueeze(2).to_broadcast([P, 2, 4]), ALU.mult))
    z = S.misc[:, 0:30].rearrange("p (t r) -> p t r", t=TILES)
    zs = S.scratch[:, 1024:1054].rearrange("p (t r) -> p t r", t=TILES)
    at = 0
    for e, r in enumerate(RANKS):
        ins = nc.vector.tensor_tensor(zs[:, :, at:at + r], z[:, :, at:at + r],
                                      first[:, :, e:e + 1].to_broadcast([P, 2, r]), ALU.mult)
        at += r
    ins.then_inc(V.sem, V.hit(L, "zs"))
    for _ in range(4):
        yield
    add_output(nc, dve, S, L, S.bank(1))
    yield


LAYER = {
    **{L: dict(tensor=mha_tensor, scalar=mha_scalar, vector=mha_vector, gpsimd=mha_gpsimd) for L in MHA},
    "L2a": dict(tensor=l2a_tensor, scalar=l2a_scalar, vector=l2a_vector, gpsimd=l2a_gpsimd),
    "L1a": dict(tensor=l1a_tensor, scalar=l1a_scalar, vector=l1a_vector, gpsimd=l1a_gpsimd),
    "L0f": dict(tensor=l0f_tensor, scalar=l0f_scalar, vector=l0f_vector, gpsimd=l0f_gpsimd),
    "L1f": dict(tensor=l1f_tensor, scalar=l1f_scalar, vector=l1f_vector, gpsimd=l1f_gpsimd),
    "L2x": dict(tensor=l2x_tensor, scalar=l2x_scalar, vector=l2x_vector, gpsimd=l2x_gpsimd),
    "L2f": dict(tensor=l2f_tensor, scalar=l2f_scalar, vector=l2f_vector, gpsimd=l2f_gpsimd),
    "L3f": dict(tensor=l3f_tensor, scalar=l3f_scalar, vector=l3f_vector, gpsimd=l3f_gpsimd),
}
PLAN = {**{L: mha_plan(L) for L in MHA}, "L2a": l2a_plan(), "L1a": L1A_PLAN, "L0f": L0F_PLAN, "L1f": L1F_PLAN, "L2x": L2X_PLAN,
        "L2f": L2F_PLAN, "L3f": L3F_PLAN}


class Shared:
    pass


def decoder(nc, x, ctx, ctx_t, mask_row, mask_col, weights, raw, sel2, upto, causal, out):
    where, spans, columns = weight_columns()
    with ExitStack() as stack:
        def sb(name, shape, dt=F32):
            return stack.enter_context(nc.sbuf_tensor(name, shape, dt))

        def sem(name):
            return stack.enter_context(nc.semaphore(name))

        K = Shared()
        weights_sb = sb("weights_sb", [P, columns])
        K.ones = sb("ones", [P, P])
        K.ones_bf = sb("ones_bf", [P, SEQ], BF16)
        K.causal = sb("causal", [P, TILES * SEQ], BF16)
        K.rows = {L: sb("rows_" + L, [P, 512], BF16) for L in (*MHA, "L2f")}
        K.ident_bf = sb("ident_bf", [P, P], BF16)[:, :]
        K.spread_bf = sb("spread_bf", [P, 512], BF16)
        K.ident_h = sb("ident_h", [P, P], F16)
        K.sel2 = sb("sel2", [P, 8, P], BF16)
        K.upto = sb("upto", [P, TILES, SEQ], BF16)
        K.neg_half = sb("neg_half", [P, 2])
        K.neg_half3 = sb("neg_half3", [P, 3])
        K.half = sb("half", [P, 2])
        K.wv_1a = sb("wv_1a", [P, P])
        K.w1q = sb("w1q", [P, 512], BF16)
        K.w2q = sb("w2q", [P, 512], BF16)
        K.b1q = sb("b1q", [P, 4])
        K.b2q = sb("b2q", [P, P], BF16)
        K.route = sb("route", [P, 4])
        K.tmp, K.half4 = sb("tmp", [P, 8]), sb("half4", [P, 4])
        K.temp_cut, K.sim2, K.route_scale = sb("temp_cut", [P, 1]), sb("sim2", [P, 4]), sb("route_scale", [P, 1])
        x_sb = sb("x_sb", [P, STREAMS, TILES, P])
        weights_loaded = {g: sem("loaded_" + g) for g in LOAD_ORDER}

        def w(group, name):
            at, n = where[group, name]
            return weights_sb[:, at:at + n]

        def loaded(eng, group):
            eng.wait_ge(weights_loaded[group], 16)

        K.w, K.loaded = w, loaded
        K.ident = w("base", "ident")

        inputs_loaded = [sem("inputs_loaded_%d" % n) for n in range(STREAMS)]
        outputs_stored, setup_chain, setup_done = (
            sem("outputs_stored"), sem("setup_chain"), sem("setup_done"))
        consts_loaded, pool_ready, setup_tensor, setup_scalar, chain = (
            sem("consts_loaded"), sem("pool_ready"), sem("setup_tensor"), sem("setup_scalar"), sem("vector_chain"))

        streams = []
        for n in range(STREAMS):
            S = Stream()

            def tile(name, shape, dt=F32):
                return sb("%s_%d" % (name, n), shape, dt)

            S.x = x_sb[:, n]
            S.xn, S.xnT = tile("xn", [P, TILES, P]), tile("xnT", [P, SEQ])
            ops = tile("operands", [P, 2048], F16)
            S.qop, S.kop = ops[:, 0:1024], ops[:, 1024:2048]
            S.kop_bf = ops[:, 1024:2048].bitcast(BF16)
            ops32 = ops[:, :].bitcast(F32)
            S.wide = tile("wide", [P, 1024])
            S.e = tile("e", [P, 4, 512])
            S.ef = S.e[:, :, :].rearrange("p a b -> p (a b)")
            S.scratch = tile("scratch", [P, 2048])
            S.hi, S.hi_bf = S.scratch[:, 1536:2048].bitcast(F16), S.scratch[:, 1536:2048].bitcast(BF16)
            S.hi_k = S.scratch[:, 1024:1536].bitcast(F16)
            S.masked = S.scratch[:, 0:1024].rearrange("p (a b) -> p a b", a=2)
            S.e_pair = S.ef.bitcast(F16).rearrange("p (u h n) -> p u h n", u=4, h=2)
            S.on, S.oT = tile("on", [P, TILES, P]), tile("oT", [P, SEQ])
            S.xn2, S.xn2T = S.on, S.oT
            S.oT2_all = lambda t, a=ops32, b=S.ef: (a, b)[t][:, 0:1024]
            S.oT2 = lambda t, i, f=S.oT2_all: f(t)[:, i * P:(i + 1) * P]
            S.vaug, S.vstack = tile("vaug", [P, TILES, HEADS, 2 * (HD + 1)], F16), tile("vstack", [P, HEADS // 2, 4 * (HD + 1)], F16)
            S.negm, S.negm2 = tile("negm", [P, TILES, QUADS, SLOTS]), tile("negm2", [P, TILES, 2, 8])
            S.nm, S.nm2 = tile("nm", [P, TILES, QUADS, P], F16), tile("nm2", [P, TILES, 2, 64], BF16)
            S.nmT = tile("nmT", [P, SEQ], BF16)
            S.rden, S.den = tile("rden", [P, TILES, HEADS]), tile("den", [P, TILES, HEADS])
            S.ctx, S.ctxT = tile("ctx", [KEYS, P]), tile("ctxT", [P, KEYS])
            S.cn, S.cnT, S.kpair = tile("cn", [KEYS, P]), tile("cnT", [P, KEYS]), tile("kpair", [P, 2 * KEYS])
            S.vpair = tile("vpair", [P, 130])
            S.mask_row_u8, S.mask_col_u8 = tile("mask_row_u8", [P, KEYS], U8), tile("mask_col_u8", [P, 1], U8)
            S.mask_row, S.mask_col = tile("mask_row", [P, KEYS], BF16), tile("mask_col", [P, 1])
            S.stats, S.mv = tile("stats", [P, 3, 6]), tile("mv", [P, 3, 2])
            S.var, S.rstd, S.var3, S.rstd3 = (tile("var", [P, 2]), tile("rstd", [P, 2]), tile("var3", [P, 3]),
                                              tile("rstd3", [P, 3]))
            S.small = tile("small", [P, 16])
            S.score, S.dist = tile("score", [P, TILES, EXPERTS]), tile("dist", [P, TILES, EXPERTS])
            S.sT, S.selT = S.scratch[:, 0:256], S.scratch[:, 256:512]
            S.work = S.scratch[:, 512:1024].rearrange("p (a b) -> p a b", a=2)
            S.rmT = S.nmT
            S.best, S.best8 = tile("best", [P, 8]), tile("best8", [P, TILES, 8])
            S.sel_bf, S.rank = tile("sel_bf", [P, TILES, EXPERTS], BF16), tile("rank", [P, TILES, EXPERTS])
            S.logit, S.gate_d, S.gate, S.kept = (tile(k, [P, TILES, MOE]) for k in ("logit", "gate_d", "gate", "kept"))
            S.top4 = tile("top4", [P, 4, TILES, 4])
            S.ps = stack.enter_context(nc.psum_tensor("ps_%d" % n, [P, 4 * BANK], F32))
            S.bank = lambda i, ps=S.ps: ps[:, i * BANK:(i + 1) * BANK]
            S.misc = S.bank(3)
            S.misc_bf, S.misc_h = S.misc.bitcast(BF16), S.misc.bitcast(F16)
            S.T, S.V, S.A, S.G = (Track(sem("%s_done_%d" % (k, n))) for k in ("tensor", "vector", "scalar", "gpsimd"))
            for kind, track in (("tensor", S.T), ("vector", S.V), ("scalar", S.A), ("gpsimd", S.G)):
                track.plan("start", NORM[kind])
                for L in LAYERS:
                    track.plan(L, PLAN[L][kind])
                    if L != LAYERS[-1]:
                        track.plan(L, NORM[kind])
            streams.append(S)

        def load_context(sp, batch, n):
            S = streams[n]
            for dst, src in ((S.ctx, ctx), (S.ctxT, ctx_t), (S.mask_row_u8, mask_row), (S.mask_col_u8, mask_col)):
                sp.dma_start(dst[:], src[batch]).then_inc(inputs_loaded[n], 16)

        def load_x(sp, r, n):
            sp.dma_start(streams[n].x, x[r, n]).then_inc(inputs_loaded[n], 16)

        def first_inputs(sp):
            for n in range(STREAMS):
                load_x(sp, 0, n)
                load_context(sp, n, n)

        setup(nc, K, streams, w, weights_sb, spans, weights_loaded, weights, raw, (sel2, upto, causal), consts_loaded,
              setup_chain, setup_tensor, setup_scalar, setup_done, pool_ready, first_inputs)

        steps = {}

        def run(kind, eng, link=None):
            def program(S):
                if kind == "vector":
                    eng.wait_ge(inputs_loaded[streams.index(S)], 16 * 5)
                    link(nc.vector.tensor_scalar(S.mask_row[:], S.mask_row_u8[:], BIG, None, ALU.mult))
                    link(nc.vector.tensor_scalar(S.mask_col[:], S.mask_col_u8[:], BIG, None, ALU.mult))
                yield from norm(S, "start", kind, eng, link)
                if kind == "gpsimd":
                    nc.gpsimd.sem_clear(inputs_loaded[streams.index(S)])
                before = "start"
                for L in LAYERS:
                    count = 0
                    args = (nc, eng, link, K, S, L, before) if kind == "vector" else (nc, eng, K, S, L, before)
                    for _ in LAYER[L][kind](*args):
                        count += 1
                        yield
                    assert steps.setdefault(L, count) == count, (L, kind, count, steps[L])
                    before = L
                    if L != LAYERS[-1]:
                        yield from norm(S, L, kind, eng, link)

            programs = [program(S) for S in streams]
            live, k = [True] * STREAMS, 0
            while any(live):
                for n in range(STREAMS):
                    if live[n] and k >= n * OFFSET:
                        live[n] = next(programs[n], "end") != "end"
                k += 1
            for S in streams:
                track = dict(tensor=S.T, vector=S.V, scalar=S.A, gpsimd=S.G)[kind]
                assert track.reached == len(track.value), (kind, track.reached)

        def norm(S, L, kind, eng, link):
            if kind == "vector":
                if L != "start":
                    last = ("acc", MOE - 1) if L == "L2f" else ("x",)
                    eng.wait_ge(S.V.sem, S.V.at(L, *last))
                yield from norm_vector(nc, eng, link, S, L)
            elif kind == "gpsimd":
                yield from norm_gpsimd(nc, eng, K, S, L)
            elif kind == "tensor":
                yield from norm_tensor(nc, eng, K, S, L)
            else:
                yield from norm_scalar(nc, eng, S, L)

        with nc.Fori(0, ROUNDS) as r:
            with nc.Block() as block:
                @block.sync
                def _(sp):
                    for n, S in enumerate(streams):
                        sp.wait_ge(S.G.sem, S.G.at(MHA_ORDER[0], "wide"))
                        sp.wait_ge(S.V.sem, S.V.at("L2x", "xn2"))
                        sp.wait_ge(S.T.sem, S.T.at("L3x", "v"))
                        load_context(sp, (r + 1) * STREAMS + n, n)
                    for n, S in enumerate(streams):
                        sp.wait_ge(S.V.sem, S.V.at(LAYERS[-1], "x"))
                        sp.dma_start(out[r, n], S.x).then_inc(outputs_stored, 16)
                        sp.wait_ge(outputs_stored, 16 * (n + 1))
                        load_x(sp, r + 1, n)

                @block.tensor
                def _(pe):
                    run("tensor", pe)

                @block.scalar
                def _(act):
                    run("scalar", act)

                @block.gpsimd
                def _(pool):
                    run("gpsimd", pool)

                @block.vector
                def _(dve):
                    links = [0]

                    def link(ins):
                        links[0] += 1
                        ins.then_inc(chain, 1)
                        dve.wait_ge(chain, links[0])

                    run("vector", dve, link)

            for s in [outputs_stored, chain] + [t.sem for S in streams for t in (S.T, S.V, S.A, S.G)]:
                nc.gpsimd.sem_clear(s)
            nc.all_engine_barrier()

        with nc.Block() as block:
            @block.sync
            def _(sp):
                for s in inputs_loaded:
                    sp.wait_ge(s, 16 * 5)


def setup(nc, K, streams, w, weights_sb, spans, weights_loaded, weights, raw, consts, consts_loaded,
          setup_chain, setup_tensor, setup_scalar, setup_done, pool_ready, first_inputs):
    early = ["base", "L3x", "L3f", "L2a"]
    raw_at = raw_columns()

    def raw_sb(*key):
        at, n = raw_at[key]
        return streams[at // RAW_HALF].scratch[:, at % RAW_HALF:at % RAW_HALF + n]

    with nc.Block() as block:
        @block.sync
        def _(sp):
            for g in LOAD_ORDER:
                a, b = spans[g]
                sp.dma_start(weights_sb[:, a:b], weights[:, a:b]).then_inc(weights_loaded[g], 16)
                if g == "base":
                    for dst, src in zip((K.sel2, K.upto, K.causal), consts):
                        sp.dma_start(dst[:], src).then_inc(consts_loaded, 16)
                    for n, S in enumerate(streams):
                        sp.dma_start(S.scratch[:], raw[:, n * RAW_HALF:(n + 1) * RAW_HALF]).then_inc(consts_loaded, 16)
            first_inputs(sp)
            sp.wait_ge(consts_loaded, 16 * (3 + STREAMS))

        @block.gpsimd
        def _(pool):
            nc.gpsimd.memset(K.neg_half[:], -0.5)
            nc.gpsimd.memset(K.neg_half3[:], -0.5)
            nc.gpsimd.memset(K.half[:], 0.5)
            nc.gpsimd.memset(K.half4[:], 0.5).then_inc(pool_ready, 1)
            for S in streams:
                nc.gpsimd.memset(S.nm[:], 0.0)
                nc.gpsimd.memset(S.nm2[:], 0.0)
                nc.gpsimd.memset(S.wide[:], 0.0).then_inc(pool_ready, 1)
                nc.gpsimd.memset(S.vaug[:, :, :, HD], 1.0)
                nc.gpsimd.memset(S.vaug[:, :, :, 2 * HD + 1], 0.0)
                nc.gpsimd.memset(S.mv[:], 1.0)
            pool.wait_ge(pool_ready, 1 + STREAMS)
            K.loaded(pool, MHA_ORDER[0])
            for S in streams:
                widen(nc, pool, K, S, MHA_ORDER[0])
            pool.wait_ge(setup_done, 1)
            nc.gpsimd.tensor_tensor(K.tmp[:, 4:8], K.tmp[:, 0:4], K.half4[:], ALU.pow).then_inc(setup_done, 1)

        @block.tensor
        def _(pe):
            pe.wait_ge(consts_loaded, 16 * (3 + STREAMS))
            nc.tensor.matmul(streams[0].bank(0)[:, 0:P], raw_sb("L1a", "vdown")[0:32], raw_sb("L1a", "vup")[0:32],
                             start=True, stop=True).then_inc(setup_tensor, 1)
            pe.wait_ge(setup_chain, 3 + 7 * STREAMS)
            nc.tensor.matmul(streams[0].bank(1)[:, 0:4], K.ones[0:32, 0:P], K.sim2[0:32], start=True, stop=True)\
                .then_inc(setup_tensor, 1)

        @block.scalar
        def _(act):
            K.loaded(act, "L3f")
            act.wait_ge(setup_chain, 2 + 7 * STREAMS)
            nc.scalar.activation(K.route_scale[:], K.temp_cut[:], ACT.Exp).then_inc(setup_scalar, 1)

        @block.vector
        def _(dve):
            links = [0]

            def link(ins):
                links[0] += 1
                ins.then_inc(setup_chain, 1)
                dve.wait_ge(setup_chain, links[0])

            for g in early:
                K.loaded(dve, g)
            link(nc.vector.memset(K.ones[:], 1.0))
            for S in streams:
                link(nc.vector.memset(S.vstack[:], 0.0))
                for half in range(2):
                    link(nc.vector.memset(S.vstack[64 * half:64 * half + 64, :, 18 * half + HD:18 * half + HD + 1], 1.0))
                link(nc.vector.memset(S.kpair[:], 0.0))
                link(nc.vector.memset(S.vpair[:], 0.0))
                link(nc.vector.memset(S.vpair[0:64, 64:65], 1.0))
                link(nc.vector.memset(S.vpair[64:128, 129:130], 1.0))
            link(nc.vector.tensor_scalar(K.temp_cut[:], w("L3f", "temp"), HOTTEST, None, ALU.min))
            link(nc.vector.tensor_tensor(K.sim2[0:32], w("L3f", "sim")[0:32], w("L3f", "sim")[0:32], ALU.mult))
            dve.wait_ge(setup_tensor, 2)
            nc.vector.tensor_copy(K.tmp[:, 0:4], streams[0].bank(1)[:, 0:4]).then_inc(setup_done, 1)
            dve.wait_ge(setup_done, 2)
            link(nc.vector.tensor_scalar(K.tmp[:, 0:4], K.tmp[:, 4:8], 1e-12, None, ALU.max))
            link(nc.vector.reciprocal(K.tmp[:, 4:8], K.tmp[:, 0:4]))
            dve.wait_ge(setup_scalar, 1)
            link(nc.vector.tensor_scalar(K.route[:], K.tmp[:, 4:8], K.route_scale[:, 0:1], None, ALU.mult))
            link(nc.vector.tensor_copy(K.wv_1a[:], streams[0].bank(0)[:, 0:P]))
            link(nc.vector.tensor_scalar(w("L3x", "wq"), w("L3x", "wq"), w("L3x", "scale"), None, ALU.mult))
            dve.wait_ge(consts_loaded, 16 * (3 + STREAMS))
            for a in (w("L2a", "wq"), raw_sb("L2a", "rows")[0:3, 0:P]):
                link(nc.vector.tensor_scalar(a, a, HD ** -0.5, None, ALU.mult))
            link(nc.vector.tensor_scalar(raw_sb("L3x", "rows")[0:3, 0:P], raw_sb("L3x", "rows")[0:3, 0:P],
                                         w("L3x", "scale")[0:3], None, ALU.mult))
            for at in (0, 1024):
                rest, part = streams[0].scratch[:, at:at + 1024], streams[0].ef[:, 0:1024]
                total, bf = streams[1].ef[:, at:at + 1024], streams[0].kop_bf[:, 0:1024]
                for i in range(3):
                    link(nc.vector.tensor_copy(bf, rest))
                    link(nc.vector.tensor_copy(part, bf))
                    if i < 2:
                        link(nc.vector.tensor_tensor(rest, rest, part, ALU.subtract))
                    if i == 0:
                        link(nc.vector.tensor_scalar(total, part, w("base", "part")[:, 0:1], None, ALU.mult))
                    else:
                        link(nc.vector.scalar_tensor_tensor(total, part, w("base", "part")[:, i:i + 1], total,
                                                            ALU.mult, ALU.add))
            for L in (*MHA, "L2f"):
                at, n = raw_at[L, "rows"]
                assert at + n <= RAW_HALF
                total = streams[1].ef[:, at:at + n]
                if L == "L2f":
                    link(nc.vector.tensor_copy(K.rows[L][:], total))
                    continue
                for p in (0, 32):
                    copies = K.rows[L][p:p + 3].rearrange("p (h r d) -> p h r d", r=4, d=HD)
                    link(nc.vector.memset(copies[:, :, 3], 0.0))
                    link(nc.vector.tensor_copy(
                        copies[:, :, 0:3], total[p:p + 3, 0:P].rearrange("p (h d) -> p h d", d=HD).unsqueeze(2)
                        .to_broadcast([3, HEADS, 3, HD])))
                link(nc.vector.memset(copies[0:1, :, 3, 0:2], GUARD))
                link(nc.vector.tensor_copy(K.rows[L][64:67, 0:256], total[64:67]))
            for src, dst, n, part, factor in (("w1", K.w1q, 512, P, 1.0), ("w2", K.w2q, 512, P, 1.0),
                                              ("b1", K.b1q, 4, P, 0.25), ("b2", K.b2q, P, 1, 16.0)):
                a, b = streams[0].ef[0:part, 0:n], streams[0].ef[0:part, 1024:1024 + n]
                link(nc.vector.tensor_scalar(a, raw_sb("L1f", src)[0:part], 64.0, 127.0, ALU.mult, ALU.min))
                link(nc.vector.tensor_scalar(b, a, -128.0, ROUND, ALU.max, ALU.add))
                link(nc.vector.tensor_scalar(dst[0:part], b, -ROUND, factor, ALU.add, ALU.mult))
            link(nc.vector.memset(K.ones_bf[:], 1.0))
            link(nc.vector.tensor_copy(K.ident_bf[:], K.ident))
            link(nc.vector.tensor_copy(K.ident_h[:], K.ident))
            link(nc.vector.tensor_copy(K.spread_bf[:], w("base", "spread")))


def packed_weights(v, np):
    where, _, columns = weight_columns()
    raw_at = raw_columns()
    out, raw = np.zeros((P, columns), np.float32), np.zeros((P, 2 * RAW_HALF), np.float32)

    def put(group, name, a, row=0, col=0):
        a = np.asarray(a)
        to, at = (out, where[group, name]) if (group, name) in where else (raw, raw_at[group, name])
        to[row:row + a.shape[0], at[0] + col:at[0] + col + a.shape[1]] = a

    put("base", "ident", np.eye(P))
    rep = (np.arange(P) // HD) % 4
    put("base", "lo_q", -(rep == 1).astype(np.float32)[:, None])
    put("base", "lo_k", -(rep == 2).astype(np.float32)[:, None])
    put("base", "slot", (np.arange(P) % CAP + 1)[:, None])
    i64 = np.arange(64)
    put("base", "mask_qk", np.where(i64[None, :] > i64[:, None], BIG, 0.0))
    put("base", "mask_kq", np.where((np.arange(P) % 64)[:, None] > i64[None, :], BIG, 0.0))
    for n in range(3):
        put("base", "part", (np.arange(P) % 32 == n)[:, None], col=n)
    put("base", "count", np.tile(np.arange(1, CAP + 1), (P, 1)))
    cols = np.arange(512)
    put("base", "spread", np.arange(EXPERTS)[:, None] == (cols // CAP)[None, :])

    def mha(L, wq, wk, wv, wo, bq=None, bk=None, bv=None, bo=None):
        for name, a in (("wq", wq), ("wk", wk), ("wv", wv), ("wo", wo)):
            put(L, name, a)
        for a, row, col in ((bq, 0, 0), (bk, 32, 0), (bv, 64, 0), (bo, 64, P)):
            if a is not None:
                put(L, "rows", np.broadcast_to(a.reshape(1, P), (3, P)), row, col)

    w, b = v["L0_attn_w_in"], v["L0_attn_b_in"]
    mha("L0a", w[0:P].T, w[P:2 * P].T, w[2 * P:].T, v["L0_attn_w_out"].T, b[0:P], b[P:2 * P], b[2 * P:], v["L0_attn_b_out"])
    q = {k: v["L0_xattn_W" + k].transpose(1, 0, 2).reshape(P, P) for k in "qkv"}
    mha("L0x", q["q"], q["k"], q["v"], v["L0_xattn_Wo"].T, v["L0_xattn_bq"], v["L0_xattn_bk"], v["L0_xattn_bv"],
        v["L0_xattn_bo"])
    w, b = v["L1_xattn_Wkv"], v["L1_xattn_bkv"]
    mha("L1x", v["L1_xattn_Wq"], w[:, 0:P], w[:, P:], v["L1_xattn_Wout"], v["L1_xattn_bq"], b[0:P], b[P:],
        v["L1_xattn_bout"])
    w = v["L2_attn_w_in"].reshape(HEADS, 3, HD, P).transpose(1, 3, 0, 2).reshape(3, P, P)
    b = v["L2_attn_b_in"].reshape(HEADS, 3, HD).transpose(1, 0, 2).reshape(3, P)
    mha("L2a", w[0], w[1], w[2], v["L2_attn_w_out"].T, b[0], b[1], b[2], v["L2_attn_b_out"])
    mha("L3a", v["L3_attn_Wq"].T, v["L3_attn_Wk"].T, v["L3_attn_Wv"].T, v["L3_attn_Wo"].T, bo=v["L3_attn_bo"])
    mha("L3x", v["L3_xattn_Wq"].T, v["L3_xattn_Wk"].T, v["L3_xattn_Wv"].T, v["L3_xattn_Wp"].T, v["L3_xattn_bq"],
        v["L3_xattn_bk"], v["L3_xattn_bv"], v["L3_xattn_bp"])
    put("L3x", "scale", np.broadcast_to(v["L3_xattn_scale"], (P, 1)))

    def halves(a):
        return a.reshape(-1, P, a.shape[1]).transpose(1, 0, 2).reshape(P, -1)

    put("L0f", "gate", v["L0_ffn_gate_w"].T)
    put("L0f", "wg", v["L0_ffn_Wg"].transpose(2, 0, 1).reshape(P, -1))
    put("L0f", "wu", v["L0_ffn_Wu"].transpose(2, 0, 1).reshape(P, -1))
    put("L0f", "wd", halves(v["L0_ffn_Wd"].transpose(0, 2, 1).reshape(-1, P)))
    put("L0f", "sg", v["L0_ffn_Ws_g"].T)
    put("L0f", "su", v["L0_ffn_Ws_u"].T)
    put("L0f", "sd", halves(v["L0_ffn_Ws_d"].T))
    put("L1a", "wq", v["L1_attn_Wq"])
    put("L1a", "wk", v["L1_attn_Wk"])
    put("L1a", "vdown", v["L1_attn_Wvdown"].T)
    put("L1a", "vup", v["L1_attn_Wvup"])
    put("L1f", "w1", v["L1_ffn_w1"].T)
    put("L1f", "w2", halves(v["L1_ffn_w2"].T))
    put("L1f", "b1", v["L1_ffn_b1"].reshape(4, P).T)
    put("L1f", "b2", v["L1_ffn_b2"].reshape(1, P))
    put("L2x", "wq", v["L2_xattn_Wq"])
    kv = v["L2_xattn_Wkv"]
    put("L2x", "wk", kv[:, 0:64])
    put("L2x", "wk", kv[:, 0:64], col=64)
    put("L2x", "wv", kv[:, 64:128])
    put("L2x", "wo", halves(v["L2_xattn_Wo"]))
    put("L2x", "w1", v["L2_xattn_Wff1"])
    put("L2x", "w2", halves(v["L2_xattn_Wff2"]))
    for name, key in (("lg", "ln_g"), ("lb", "ln_b"), ("cg", "cln_g"), ("cb", "cln_b")):
        put("L2x", name, v["L2_xattn_" + key].reshape(P, 1))
    put("L2f", "w1", v["L2_ffn_W1"].transpose(1, 0, 2).reshape(P, -1))
    put("L2f", "w2", halves(v["L2_ffn_W2"].reshape(-1, P)))
    put("L2f", "b1", v["L2_ffn_b1"].reshape(MOE, MOE_C, P).transpose(2, 0, 1).reshape(P, -1))
    put("L2f", "wr", v["L2_ffn_Wr"])
    for e in range(MOE):
        put("L2f", "rows", np.broadcast_to(v["L2_ffn_b2"][e:e + 1], (3, P)), row=32 * (e // 4), col=e % 4 * P)
    put("L2f", "rows", np.broadcast_to(v["L2_ffn_br"].reshape(1, MOE), (3, MOE)), row=96)
    put("L3f", "w", v["L3_ffn_W"].T)
    put("L3f", "wp", v["L3_ffn_Wp"].T)
    put("L3f", "bp", v["L3_ffn_bp"].reshape(32, 1))
    put("L3f", "sim", v["L3_ffn_sim"])
    put("L3f", "temp", np.broadcast_to(v["L3_ffn_temp"], (P, 1)))
    at = 0
    for e, r in enumerate(RANKS):
        put("L3f", "down", v["L3_ffn_Wd%d" % e].T, col=at)
        put("L3f", "up", v["L3_ffn_Wu%d" % e].T, row=at)
        at += r
    return out, raw


def kernel(**inputs):
    import ml_dtypes as _ml
    import numpy as _np
    import concourse.bacc as _bacc
    from concourse import mybir as _mybir
    from concourse.bass_utils import run_bass_kernel_spmd as _run

    v = {k: _np.asarray(a) for k, a in inputs.items()}
    x = v["x"].reshape(ROUNDS, STREAMS, 64, TILES, 2, D).transpose(0, 1, 4, 2, 3, 5).reshape(ROUNDS, STREAMS, P, TILES, D)
    ctx = v["ctx_1024"]
    mask = v["mask_BxS2_bf0"]
    part = _np.arange(P)
    sel2 = _np.zeros((P, 8, P), _ml.bfloat16)
    for a in range(8):
        for half in range(2):
            sel2[[64 * half + a, 64 * half + 8 + a], a, 64 * half:64 * half + 64] = 1
    upto = (_np.arange(SEQ).reshape(TILES, P).T[:, :, None] <= _np.arange(SEQ)).astype(_ml.bfloat16)
    order = _np.array([4 * i + r for r in range(4) for i in range(64)])
    causal = (order.reshape(TILES, P).T[:, :, None] >= order).astype(_ml.bfloat16).reshape(P, TILES * SEQ)
    weights, raw = packed_weights(v, _np)
    arrays = {
        "x": x, "ctx": ctx, "ctx_t": ctx.transpose(0, 2, 1), "mask_row": _np.broadcast_to(mask[:, None], (BATCH, P, KEYS)),
        "mask_col": _np.concatenate([mask, mask], 1)[:, :, None], "weights": weights, "raw": raw, "sel2": sel2, "upto": upto,
        "causal": causal,
    }
    for k in ("x", "ctx", "ctx_t", "mask_row", "mask_col"):
        arrays[k] = _np.concatenate([arrays[k], arrays[k][:1 if k == "x" else STREAMS]])
    nc = _bacc.Bacc("TRN2", target_bir_lowering=False, num_devices=1)
    arrays = {"in_" + k: _np.ascontiguousarray(a) for k, a in arrays.items()}
    args = [nc.dram_tensor(k, a.shape, _mybir.dt.from_np(a.dtype), kind="ExternalInput").ap() for k, a in arrays.items()]
    out = nc.dram_tensor("out_x", x.shape, _mybir.dt.float32, kind="ExternalOutput").ap()
    decoder(nc, *args, out)
    y = _run(nc, [arrays], core_ids=[0]).results[0]["out_x"]
    y = y.reshape(ROUNDS, STREAMS, 2, 64, TILES, D).transpose(0, 1, 3, 4, 2, 5)
    return _np.ascontiguousarray(y.reshape(BATCH, SEQ, D))
```
